# Optimizing a Trainium2 kernel written in Bass

```python
import numpy as np
import jax
import jax.numpy as jnp

def _softmax(x, axis=-1):
    return jax.nn.softmax(x, axis=axis)

def _gelu(x):
    return jax.nn.gelu(x, approximate=True)

def _silu(x):
    return jax.nn.silu(x)

def _sigmoid(x):
    return jax.nn.sigmoid(x)

def _layernorm(x, axis=-1, eps=1e-05):
    m = jnp.mean(x, axis=axis, keepdims=True)
    v = jnp.var(x, axis=axis, keepdims=True)
    return (x - m) / jnp.sqrt(v + eps)

def _scatter_add(tgt, idx, src, axis=0):
    return tgt.at[idx].add(src)

def _segment_sum(src, seg, n):
    return jax.ops.segment_sum(src, seg, n)
kernel_name = 'mk_gnn_ffn_d2_gnn_r32_2c0970'

def setup_inputs(seed: int=0):
    np.random.seed(seed)
    _w = jnp.asarray

    def _rec_inputs():
        import jax
        import jax.numpy as jnp
        _gk = jax.random.key(seed)
        x = -6.415e-05 + 1 * jax.random.normal(jax.random.fold_in(_gk, 1), (625, 512), jnp.float32)
        _s = jax.random.randint(jax.random.fold_in(_gk, 2), (10000,), 0, 625, jnp.int32)
        _d = jax.random.randint(jax.random.fold_in(_gk, 3), (10000,), 0, 625, jnp.int32)
        _loop = jnp.arange(625, dtype=jnp.int32)
        src = jnp.concatenate([_s, _d, _loop])
        dst = jnp.concatenate([_d, _s, _loop])
        _o = jnp.argsort(dst, stable=True)
        src = src[_o]
        dst = dst[_o]
        node_vec1 = jax.random.uniform(jax.random.fold_in(_gk, 12), (625, 1), jnp.float32, 0.0, 0.999957)
        return (x, src, dst, node_vec1)
    x, src, dst, node_vec1 = _rec_inputs()

    def _L0_gnn_setup():
        import jax, jax.numpy as jnp
        import numpy as np
        N_NODES = 625
        key = jax.random.key(seed)
        ks = jax.random.split(key, 6)
        d = 512
        E = 20000
        x = jax.random.normal(ks[0], (N_NODES, d), dtype=jnp.float32)
        edge_index = jax.random.randint(ks[1], (2, E), 0, N_NODES, dtype=jnp.int64)
        s = 1.0 / np.sqrt(d)
        W1 = jax.random.uniform(ks[2], (d, d), jnp.float32, -s, s)
        b1 = jax.random.uniform(ks[3], (d,), jnp.float32, -s, s)
        W2 = jax.random.uniform(ks[4], (d, d), jnp.float32, -s, s)
        b2 = jax.random.uniform(ks[5], (d,), jnp.float32, -s, s)
        return {'x': x, 'edge_index': edge_index, 'W1': W1, 'b1': b1, 'W2': W2, 'b2': b2}
    _L0_gnn_all = _L0_gnn_setup()
    _L0_gnn_in = {k: v for k, v in _L0_gnn_all.items() if k in ('W1', 'b1', 'W2', 'b2')}
    del _L0_gnn_all

    def _L0_ffn_setup():
        import jax, jax.numpy as jnp
        import numpy as np
        import math
        E, K, CAPF = (8, 2, 1.25)
        D, DFF = (512, 64)

        def _moe(x, Wr, br, W1, b1, W2, b2):
            orig = x.shape
            d = orig[-1]
            xf = x.reshape(-1, d)
            N = xf.shape[0]
            logits = xf @ Wr + br
            probs = jax.nn.softmax(logits, axis=-1)
            topk_p, topk_i = jax.lax.top_k(probs, K)
            topk_w = topk_p / (jnp.sum(topk_p, axis=-1, keepdims=True) + 1e-09)
            cap = max(1, int(math.ceil(CAPF * float(N * K) / float(E))))
            flat_e = topk_i.reshape(-1)
            flat_w = topk_w.reshape(-1)
            tok = jnp.repeat(jnp.arange(N), K)
            one_hot = jax.nn.one_hot(flat_e, E, dtype=xf.dtype)
            pos = (jnp.cumsum(one_hot, axis=0) - one_hot)[jnp.arange(N * K), flat_e]
            pos = pos.astype(jnp.int32)
            keep = pos < cap
            w_k = jnp.where(keep, flat_w, 0.0)
            sum_w = jnp.zeros((N,), xf.dtype).at[tok].add(w_k)
            w_norm = w_k / (sum_w[tok] + 1e-09)
            slot = flat_e * cap + pos
            slot_safe = jnp.where(keep, slot, E * cap)
            expert_in = jnp.zeros((E * cap, d), xf.dtype).at[slot_safe].set(xf[tok], mode='drop').reshape(E, cap, d)
            h = jax.nn.gelu(jnp.einsum('ecd,edf->ecf', expert_in, W1) + b1[:, None, :], approximate=False)
            expert_out = (jnp.einsum('ecf,efd->ecd', h, W2) + b2[:, None, :]).reshape(E * cap, d)
            contrib = expert_out[jnp.where(keep, slot, 0)]
            y = jnp.zeros((N, d), xf.dtype).at[tok].add(contrib * w_norm[:, None])
            return y.reshape(orig)
        key = jax.random.key(seed)
        ks = jax.random.split(key, 5)
        s = lambda k, sh, sc: jax.random.normal(k, sh, jnp.float32) * sc
        return {'x': jax.random.normal(ks[0], (8, 128, D), jnp.float32), 'Wr': s(ks[1], (D, E), 1.0 / math.sqrt(D)), 'br': jnp.zeros((E,), jnp.float32), 'W1': s(ks[2], (E, D, DFF), 1.0 / math.sqrt(D)), 'b1': jnp.zeros((E, DFF), jnp.float32), 'W2': s(ks[3], (E, DFF, D), 1.0 / math.sqrt(DFF)), 'b2': jnp.zeros((E, D), jnp.float32)}
    _L0_ffn_all = _L0_ffn_setup()
    _L0_ffn_in = {k: v for k, v in _L0_ffn_all.items() if k in ('Wr', 'br', 'W1', 'b1', 'W2', 'b2')}
    del _L0_ffn_all

    def _L1_gnn_setup():
        import jax, jax.numpy as jnp
        import numpy as np
        N_NODES = 40962
        LATENT_DIM = 512
        N_EDGES = 20481
        NUM_BLOCKS = 4
        NUM_HEADS = 4
        NUM_FREQ = 32
        BASE_PERIOD = 16
        NOISE_EMB_DIM = 16
        EPS = 1e-05

        def _cond_layer_norm(x, cond, sw, sb, bw, bb):
            mu = jnp.mean(x, axis=-1, keepdims=True)
            var = jnp.var(x, axis=-1, keepdims=True)
            xn = (x - mu) * jax.lax.rsqrt(var + EPS)
            scale = cond @ sw + sb
            bias = cond @ bw + bb
            return xn * (1.0 + scale) + bias

        def _sparse_attention(x, src, dst, wq, bq, wk, bk, wv, bv, wo, bo):
            N, D = x.shape
            H, Dh = (NUM_HEADS, D // NUM_HEADS)
            q = (x @ wq + bq).reshape(N, H, Dh) * Dh ** (-0.5)
            k = (x @ wk + bk).reshape(N, H, Dh)
            v = (x @ wv + bv).reshape(N, H, Dh)
            scores = jnp.einsum('ehd,ehd->eh', q[src], k[dst])
            smax = jax.ops.segment_max(scores, src, num_segments=N)
            ex = jnp.exp(scores - smax[src])
            denom = jax.ops.segment_sum(ex, src, num_segments=N)
            attn = ex / denom[src]
            out = jax.ops.segment_sum(attn[:, :, None] * v[dst], src, num_segments=N)
            return out.reshape(N, D) @ wo + bo

        def _forward(x, edge_index, noise_levels, f_w1, f_b1, f_w2, f_b2, s1_w, s1_b, b1_w, b1_b, wq, bq, wk, bk, wv, bv, wo, bo, s2_w, s2_b, b2_w, b2_b, m_w1, m_b1, m_w2, m_b2):
            src, dst = (edge_index[0], edge_index[1])
            freqs = jnp.arange(1, NUM_FREQ + 1, dtype=x.dtype) * (2.0 * np.pi / BASE_PERIOD)
            ph = noise_levels * freqs
            emb = jnp.concatenate([jnp.sin(ph), jnp.cos(ph)], axis=-1)
            cond = jax.nn.silu(emb @ f_w1 + f_b1) @ f_w2 + f_b2
            for i in range(NUM_BLOCKS):
                y = _cond_layer_norm(x, cond, s1_w[i], s1_b[i], b1_w[i], b1_b[i])
                y = _sparse_attention(y, src, dst, wq[i], bq[i], wk[i], bk[i], wv[i], bv[i], wo[i], bo[i])
                x = x + y
                y = _cond_layer_norm(x, cond, s2_w[i], s2_b[i], b2_w[i], b2_b[i])
                y = jax.nn.relu(y @ m_w1[i] + m_b1[i]) @ m_w2[i] + m_b2[i]
                x = x + y
            return x
        key = jax.random.key(seed)
        ks = jax.random.split(key, 20)

        def w(k, shape, s=0.02):
            return jax.random.normal(k, shape, dtype=jnp.float32) * s
        D, B, C = (LATENT_DIM, NUM_BLOCKS, NOISE_EMB_DIM)
        z = lambda *s: jnp.zeros(s, jnp.float32)
        return {'latent_mesh_nodes': jax.random.normal(ks[0], (N_NODES, D), dtype=jnp.float32), 'edge_index': jax.random.randint(ks[1], (2, N_EDGES), 0, N_NODES, dtype=jnp.int32), 'noise_levels': jax.random.uniform(ks[2], (N_NODES, 1), dtype=jnp.float32), 'f_w1': w(ks[3], (2 * NUM_FREQ, C)), 'f_b1': z(C), 'f_w2': w(ks[4], (C, C)), 'f_b2': z(C), 's1_w': w(ks[5], (B, C, D)), 's1_b': z(B, D), 'b1_w': w(ks[6], (B, C, D)), 'b1_b': z(B, D), 'wq': w(ks[7], (B, D, D)), 'bq': z(B, D), 'wk': w(ks[8], (B, D, D)), 'bk': z(B, D), 'wv': w(ks[9], (B, D, D)), 'bv': z(B, D), 'wo': w(ks[10], (B, D, D)), 'bo': z(B, D), 's2_w': w(ks[11], (B, C, D)), 's2_b': z(B, D), 'b2_w': w(ks[12], (B, C, D)), 'b2_b': z(B, D), 'm_w1': w(ks[13], (B, D, D)), 'm_b1': z(B, D), 'm_w2': w(ks[14], (B, D, D)), 'm_b2': z(B, D)}
    _L1_gnn_all = _L1_gnn_setup()
    _L1_gnn_in = {k: v for k, v in _L1_gnn_all.items() if k in ('f_w1', 'f_b1', 'f_w2', 'f_b2', 's1_w', 's1_b', 'b1_w', 'b1_b', 'wq', 'bq', 'wk', 'bk', 'wv', 'bv', 'wo', 'bo', 's2_w', 's2_b', 'b2_w', 'b2_b', 'm_w1', 'm_b1', 'm_w2', 'm_b2')}
    del _L1_gnn_all

    def _L1_ffn_setup():
        import jax, jax.numpy as jnp
        import numpy as np
        B, S, D, F, E = (4, 64, 512, 64, 8)
        key = jax.random.key(seed)
        k = jax.random.split(key, 5)
        x = jax.random.normal(k[0], (B, S, D), dtype=jnp.float32)
        Ws = jax.random.normal(k[1], (D, E), dtype=jnp.float32) * 0.02
        bs = jnp.zeros((E,), dtype=jnp.float32)
        W1 = jax.random.normal(k[2], (E, D, F), dtype=jnp.float32) * 0.02
        b1 = jnp.zeros((E, F), dtype=jnp.float32)
        W2 = jax.random.normal(k[3], (E, F, D), dtype=jnp.float32) * 0.02
        b2 = jnp.zeros((E, D), dtype=jnp.float32)
        return {'x': x, 'Ws': Ws, 'bs': bs, 'W1': W1, 'b1': b1, 'W2': W2, 'b2': b2}
    _L1_ffn_all = _L1_ffn_setup()
    _L1_ffn_in = {k: v for k, v in _L1_ffn_all.items() if k in ('Ws', 'bs', 'W1', 'b1', 'W2', 'b2')}
    del _L1_ffn_all
    return {'x': x, 'src': src, 'dst': dst, 'node_vec1': node_vec1, 'L0_gnn_W1': _L0_gnn_in['W1'], 'L0_gnn_b1': _L0_gnn_in['b1'], 'L0_gnn_W2': _L0_gnn_in['W2'], 'L0_gnn_b2': _L0_gnn_in['b2'], 'L0_ffn_Wr': _L0_ffn_in['Wr'], 'L0_ffn_br': _L0_ffn_in['br'], 'L0_ffn_W1': _L0_ffn_in['W1'], 'L0_ffn_b1': _L0_ffn_in['b1'], 'L0_ffn_W2': _L0_ffn_in['W2'], 'L0_ffn_b2': _L0_ffn_in['b2'], 'L1_gnn_f_w1': _L1_gnn_in['f_w1'], 'L1_gnn_f_b1': _L1_gnn_in['f_b1'], 'L1_gnn_f_w2': _L1_gnn_in['f_w2'], 'L1_gnn_f_b2': _L1_gnn_in['f_b2'], 'L1_gnn_s1_w': _L1_gnn_in['s1_w'], 'L1_gnn_s1_b': _L1_gnn_in['s1_b'], 'L1_gnn_b1_w': _L1_gnn_in['b1_w'], 'L1_gnn_b1_b': _L1_gnn_in['b1_b'], 'L1_gnn_wq': _L1_gnn_in['wq'], 'L1_gnn_bq': _L1_gnn_in['bq'], 'L1_gnn_wk': _L1_gnn_in['wk'], 'L1_gnn_bk': _L1_gnn_in['bk'], 'L1_gnn_wv': _L1_gnn_in['wv'], 'L1_gnn_bv': _L1_gnn_in['bv'], 'L1_gnn_wo': _L1_gnn_in['wo'], 'L1_gnn_bo': _L1_gnn_in['bo'], 'L1_gnn_s2_w': _L1_gnn_in['s2_w'], 'L1_gnn_s2_b': _L1_gnn_in['s2_b'], 'L1_gnn_b2_w': _L1_gnn_in['b2_w'], 'L1_gnn_b2_b': _L1_gnn_in['b2_b'], 'L1_gnn_m_w1': _L1_gnn_in['m_w1'], 'L1_gnn_m_b1': _L1_gnn_in['m_b1'], 'L1_gnn_m_w2': _L1_gnn_in['m_w2'], 'L1_gnn_m_b2': _L1_gnn_in['m_b2'], 'L1_ffn_Ws': _L1_ffn_in['Ws'], 'L1_ffn_bs': _L1_ffn_in['bs'], 'L1_ffn_W1': _L1_ffn_in['W1'], 'L1_ffn_b1': _L1_ffn_in['b1'], 'L1_ffn_W2': _L1_ffn_in['W2'], 'L1_ffn_b2': _L1_ffn_in['b2']}

def reference(x, src, dst, node_vec1, L0_gnn_W1, L0_gnn_b1, L0_gnn_W2, L0_gnn_b2, L0_ffn_Wr, L0_ffn_br, L0_ffn_W1, L0_ffn_b1, L0_ffn_W2, L0_ffn_b2, L1_gnn_f_w1, L1_gnn_f_b1, L1_gnn_f_w2, L1_gnn_f_b2, L1_gnn_s1_w, L1_gnn_s1_b, L1_gnn_b1_w, L1_gnn_b1_b, L1_gnn_wq, L1_gnn_bq, L1_gnn_wk, L1_gnn_bk, L1_gnn_wv, L1_gnn_bv, L1_gnn_wo, L1_gnn_bo, L1_gnn_s2_w, L1_gnn_s2_b, L1_gnn_b2_w, L1_gnn_b2_b, L1_gnn_m_w1, L1_gnn_m_b1, L1_gnn_m_w2, L1_gnn_m_b2, L1_ffn_Ws, L1_ffn_bs, L1_ffn_W1, L1_ffn_b1, L1_ffn_W2, L1_ffn_b2):
    import jax
    import jax.numpy as jnp

    def _L0_gnn_ref(x, edge_index, W1, b1, W2, b2):
        import jax, jax.numpy as jnp
        import numpy as np
        N_NODES = 625
        eps = 0.0
        src, dst = (edge_index[0], edge_index[1])
        agg = jax.ops.segment_sum(x[src], dst, num_segments=N_NODES)
        h = (1.0 + eps) * x + agg
        h = jax.nn.relu(h @ W1 + b1)
        out = h @ W2 + b2
        return out

    def _L0_ffn_ref(x, Wr, br, W1, b1, W2, b2):
        import jax, jax.numpy as jnp
        import numpy as np
        import math
        E, K, CAPF = (8, 2, 1.25)
        D, DFF = (512, 64)

        def _moe(x, Wr, br, W1, b1, W2, b2):
            orig = x.shape
            d = orig[-1]
            xf = x.reshape(-1, d)
            N = xf.shape[0]
            logits = xf @ Wr + br
            probs = jax.nn.softmax(logits, axis=-1)
            topk_p, topk_i = jax.lax.top_k(probs, K)
            topk_w = topk_p / (jnp.sum(topk_p, axis=-1, keepdims=True) + 1e-09)
            cap = max(1, int(math.ceil(CAPF * float(N * K) / float(E))))
            flat_e = topk_i.reshape(-1)
            flat_w = topk_w.reshape(-1)
            tok = jnp.repeat(jnp.arange(N), K)
            one_hot = jax.nn.one_hot(flat_e, E, dtype=xf.dtype)
            pos = (jnp.cumsum(one_hot, axis=0) - one_hot)[jnp.arange(N * K), flat_e]
            pos = pos.astype(jnp.int32)
            keep = pos < cap
            w_k = jnp.where(keep, flat_w, 0.0)
            sum_w = jnp.zeros((N,), xf.dtype).at[tok].add(w_k)
            w_norm = w_k / (sum_w[tok] + 1e-09)
            slot = flat_e * cap + pos
            slot_safe = jnp.where(keep, slot, E * cap)
            expert_in = jnp.zeros((E * cap, d), xf.dtype).at[slot_safe].set(xf[tok], mode='drop').reshape(E, cap, d)
            h = jax.nn.gelu(jnp.einsum('ecd,edf->ecf', expert_in, W1) + b1[:, None, :], approximate=False)
            expert_out = (jnp.einsum('ecf,efd->ecd', h, W2) + b2[:, None, :]).reshape(E * cap, d)
            contrib = expert_out[jnp.where(keep, slot, 0)]
            y = jnp.zeros((N, d), xf.dtype).at[tok].add(contrib * w_norm[:, None])
            return y.reshape(orig)
        return _moe(x, Wr, br, W1, b1, W2, b2)

    def _L1_gnn_ref(latent_mesh_nodes, edge_index, noise_levels, f_w1, f_b1, f_w2, f_b2, s1_w, s1_b, b1_w, b1_b, wq, bq, wk, bk, wv, bv, wo, bo, s2_w, s2_b, b2_w, b2_b, m_w1, m_b1, m_w2, m_b2):
        import jax, jax.numpy as jnp
        import numpy as np
        N_NODES = 40962
        LATENT_DIM = 512
        N_EDGES = 20481
        NUM_BLOCKS = 4
        NUM_HEADS = 4
        NUM_FREQ = 32
        BASE_PERIOD = 16
        NOISE_EMB_DIM = 16
        EPS = 1e-05

        def _cond_layer_norm(x, cond, sw, sb, bw, bb):
            mu = jnp.mean(x, axis=-1, keepdims=True)
            var = jnp.var(x, axis=-1, keepdims=True)
            xn = (x - mu) * jax.lax.rsqrt(var + EPS)
            scale = cond @ sw + sb
            bias = cond @ bw + bb
            return xn * (1.0 + scale) + bias

        def _sparse_attention(x, src, dst, wq, bq, wk, bk, wv, bv, wo, bo):
            N, D = x.shape
            H, Dh = (NUM_HEADS, D // NUM_HEADS)
            q = (x @ wq + bq).reshape(N, H, Dh) * Dh ** (-0.5)
            k = (x @ wk + bk).reshape(N, H, Dh)
            v = (x @ wv + bv).reshape(N, H, Dh)
            scores = jnp.einsum('ehd,ehd->eh', q[src], k[dst])
            smax = jax.ops.segment_max(scores, src, num_segments=N)
            ex = jnp.exp(scores - smax[src])
            denom = jax.ops.segment_sum(ex, src, num_segments=N)
            attn = ex / denom[src]
            out = jax.ops.segment_sum(attn[:, :, None] * v[dst], src, num_segments=N)
            return out.reshape(N, D) @ wo + bo

        def _forward(x, edge_index, noise_levels, f_w1, f_b1, f_w2, f_b2, s1_w, s1_b, b1_w, b1_b, wq, bq, wk, bk, wv, bv, wo, bo, s2_w, s2_b, b2_w, b2_b, m_w1, m_b1, m_w2, m_b2):
            src, dst = (edge_index[0], edge_index[1])
            freqs = jnp.arange(1, NUM_FREQ + 1, dtype=x.dtype) * (2.0 * np.pi / BASE_PERIOD)
            ph = noise_levels * freqs
            emb = jnp.concatenate([jnp.sin(ph), jnp.cos(ph)], axis=-1)
            cond = jax.nn.silu(emb @ f_w1 + f_b1) @ f_w2 + f_b2
            for i in range(NUM_BLOCKS):
                y = _cond_layer_norm(x, cond, s1_w[i], s1_b[i], b1_w[i], b1_b[i])
                y = _sparse_attention(y, src, dst, wq[i], bq[i], wk[i], bk[i], wv[i], bv[i], wo[i], bo[i])
                x = x + y
                y = _cond_layer_norm(x, cond, s2_w[i], s2_b[i], b2_w[i], b2_b[i])
                y = jax.nn.relu(y @ m_w1[i] + m_b1[i]) @ m_w2[i] + m_b2[i]
                x = x + y
            return x
        return _forward(latent_mesh_nodes, edge_index, noise_levels, f_w1, f_b1, f_w2, f_b2, s1_w, s1_b, b1_w, b1_b, wq, bq, wk, bk, wv, bv, wo, bo, s2_w, s2_b, b2_w, b2_b, m_w1, m_b1, m_w2, m_b2)

    def _L1_ffn_ref(x, Ws, bs, W1, b1, W2, b2):
        import jax, jax.numpy as jnp
        import numpy as np
        B, S, D, F, E = (4, 64, 512, 64, 8)
        Bb, Ss, Dd = x.shape
        xt = x.reshape(-1, Dd)
        logits = xt @ Ws + bs
        probs = jax.nn.softmax(logits, axis=-1)
        prob_max = jnp.max(probs, axis=-1)
        routes = jnp.argmax(probs, axis=-1)
        onehot = jax.nn.one_hot(routes, W1.shape[0], dtype=xt.dtype)

        def expert_ffn(w1, bb1, w2, bb2):
            h = jax.nn.gelu(xt @ w1 + bb1, approximate=False)
            return h @ w2 + bb2
        y = jax.vmap(expert_ffn)(W1, b1, W2, b2)
        out = jnp.einsum('te,etd->td', onehot, y)
        out = out * prob_max[:, None]
        return out.reshape(Bb, Ss, Dd)
    edge_index = jnp.stack([src, dst])
    x = x + _L0_gnn_ref(_layernorm(x, axis=-1), edge_index, L0_gnn_W1, L0_gnn_b1, L0_gnn_W2, L0_gnn_b2)
    x = x + _L0_ffn_ref(_layernorm(x, axis=-1)[None], L0_ffn_Wr, L0_ffn_br, L0_ffn_W1, L0_ffn_b1, L0_ffn_W2, L0_ffn_b2)[0]
    x = x + _L1_gnn_ref(_layernorm(x, axis=-1), edge_index, node_vec1, L1_gnn_f_w1, L1_gnn_f_b1, L1_gnn_f_w2, L1_gnn_f_b2, L1_gnn_s1_w, L1_gnn_s1_b, L1_gnn_b1_w, L1_gnn_b1_b, L1_gnn_wq, L1_gnn_bq, L1_gnn_wk, L1_gnn_bk, L1_gnn_wv, L1_gnn_bv, L1_gnn_wo, L1_gnn_bo, L1_gnn_s2_w, L1_gnn_s2_b, L1_gnn_b2_w, L1_gnn_b2_b, L1_gnn_m_w1, L1_gnn_m_b1, L1_gnn_m_w2, L1_gnn_m_b2)
    x = x + _L1_ffn_ref(_layernorm(x, axis=-1)[None], L1_ffn_Ws, L1_ffn_bs, L1_ffn_W1, L1_ffn_b1, L1_ffn_W2, L1_ffn_b2)[0]
    return x

_drawn_inputs = setup_inputs


def setup_inputs(seed=0):
    import zlib

    import numpy as np

    out = dict(_drawn_inputs(seed))
    spreads = {'L0_ffn_br': (0.0, 0.1),
     'L0_ffn_b1': (0.0, 0.275),
     'L0_ffn_b2': (0.0, 0.1),
     'L1_gnn_f_b1': (0.0, 0.8),
     'L1_gnn_f_b2': (0.0, 0.8),
     'L1_gnn_s1_b': (0.0, 0.8),
     'L1_gnn_b1_b': (0.0, 0.537),
     'L1_gnn_bq': (0.0, 0.8),
     'L1_gnn_bk': (0.0, 0.8),
     'L1_gnn_bv': (0.0, 0.1),
     'L1_gnn_bo': (0.0, 0.1),
     'L1_gnn_s2_b': (0.0, 0.758),
     'L1_gnn_b2_b': (0.0, 0.784),
     'L1_gnn_m_b1': (0.0, 0.356),
     'L1_gnn_m_b2': (0.0, 0.1),
     'L1_ffn_bs': (0.0, 0.8),
     'L1_ffn_b1': (0.0, 0.8),
     'L1_ffn_b2': (0.0, 0.8)}
    factors = {'node_vec1': 8.0,
     'L1_gnn_f_w1': 8.0,
     'L1_gnn_f_w2': 8.0,
     'L1_gnn_s1_w': 8.0,
     'L1_gnn_b1_w': 8.0,
     'L1_gnn_wq': 8.0,
     'L1_gnn_wk': 8.0,
     'L1_gnn_s2_w': 8.0,
     'L1_gnn_b2_w': 8.0,
     'L1_ffn_Ws': 6.61,
     'L1_ffn_W1': 8.0,
     'L1_ffn_W2': 8.0}
    for name, (base, spread) in spreads.items():
        noise = np.random.default_rng([zlib.crc32(name.encode()), seed]).standard_normal(out[name].shape)
        drawn = base * np.exp(spread * noise) if base else spread * noise
        out[name] = jnp.asarray(drawn.astype(out[name].dtype))
    for name, factor in factors.items():
        out[name] = (out[name] * factor).astype(out[name].dtype)
    return out
```

```python
from contextlib import ExitStack, contextmanager

import concourse.bass as bass
from concourse import mybir

F32 = mybir.dt.float32
F16 = mybir.dt.float16
I32 = mybir.dt.int32
U32 = mybir.dt.uint32
ALU = mybir.AluOpType
ACT = mybir.ActivationFunctionType
AX_X = mybir.AxisListType.X

WSCALE = 64.0
PSCALE = 1024.0
PASSES = ((0, 0), (1, 0), (0, 1))
DIGIT = 4096
MASKED = -1.0e30
FLOOR = -1.0e20
RSQRT_MAGIC = 0x5F3759DF
EPS = 1e-5
TWO_PI_PARTS = (6.28125, 0.0019350051879882812, 3.019916050561733e-07)
INV_TWO_PI = 0.15915494309189535
ROUND_MAGIC = 12582912.0
PI_SAFE = 3.1415925


class Chain:

    def __init__(self, engine, sem):
        self.engine, self.sem, self.n = engine, sem, 0

    def __call__(self, ins):
        self.n += 1
        ins.then_inc(self.sem, 1)
        self.engine.wait_ge(self.sem, self.n)


def build(nc, A, out):
    x_in = A["x"]
    T, D = x_in.shape
    P = 125
    NT = T // P
    K = D // 128
    E = A["L0_ffn_Wr"].shape[2]
    DFF = D // E
    NL = A["mod"].shape[0]
    C = A["f_w2"].shape[0]
    H = 4
    DH = D // H
    SCORE = float(DH) ** -0.5
    NE = A["src"].shape[0]
    NCH = NE // P
    assert T == NT * P and D == K * 128 and NE == NCH * P and E * DFF == D and DH == 128
    CAP = -(-5 * T * 2 // (4 * E))
    NF = A["L1_gnn_f_w1"].shape[0] // 2
    HALF = (T + 1) // 2
    GROUPS = [(0, 3), (3, 2)]
    UNROLL = 5
    CHUNKS = [30] * 5 + [15]
    assert sum(CHUNKS) == NCH and max(CHUNKS) * P < DIGIT and (max(CHUNKS) * P) * DIGIT < 2 ** 24

    SEMS = ("x_loaded idx_loaded const_made chain_dve chain_act chain_pool onehot_ready onehot_used "
            "count_mm count_copied count_split count_added count_done xn_parts "
            "w_loaded0 w_loaded1 w_loaded2 w_loaded3 w_loaded4 w_loaded5 "
            "w_hi0 w_hi1 w_hi2 w_hi3 w_hi4 w_hi5 w_lo0 w_lo1 w_lo2 w_lo3 w_lo4 w_lo5 "
            "small_loaded small_hi small_lo bias_loaded "
            "norm1 norm2 mod_mm1 mod_mm2 mod1 mod2 yt_mm1 yt_mm2 yt_hi1 yt_hi2 yt_lo1 yt_lo2 "
            "a_mm a_f a_hi a_lo b_mm b_f b_hi b_lo c_mm c_f c_hi c_lo "
            "v_mm v_f v_hi v_lo o_mm o_f o_hi o_lo res1_mm res2_mm res1 res2 resb1 resb2 "
            "s_mm s_max s_exp s_inv s_prob pt_mm pt_hi pt_lo "
            "r_mm r_lg r_exp r_w wt_mm wt_parts pos_mm pos_done gm gelu_done hm_done "
            "s_x e_a e_b e_c e_d e_e stored ln_c").split()
    ctx = ExitStack()
    with ctx:
        S = {n: ctx.enter_context(nc.semaphore(n)) for n in SEMS}
        nums = [s.num for s in S.values()]
        assert nums == list(range(nums[0], nums[0] + len(nums)))

        def clear_all():
            nc.all_engine_barrier(sems_to_clear=range(nums[0], nums[0] + len(nums)))

        def sb(name, shape, dt=F32):
            return ctx.enter_context(nc.sbuf_tensor(name, shape, dt))

        ps = ctx.enter_context(nc.psum_tensor("ps", [128, 8, 512], F32))

        def bank(b, p=128, n=512):
            return ps[0:p, b, 0:n]

        def pair(b, p, n):
            return ps[0:p, b:b + 2, :].rearrange("p b n -> p (b n)")[:, 0:n]

        def blocks(b, p):
            return pair(b, p, NT * 128).rearrange("p (t n) -> p t n", n=128)[:, :, 0:P]

        x = sb("x", [P, NT, D])
        xg = sb("xg", [P, NT, D])
        y = sb("y", [P, NT, D])
        stats = sb("stats", [P, NT, 16])
        ident = sb("ident", [128, 128])
        lnc = sb("lnc", [P, NT, T])
        stage = [sb(f"stage{i}", [128, K, D])[:, :, :] for i in range(3)]
        parts = sb("parts", [128, 6, 2, K, D], F16)
        w = [parts[:, i] for i in range(6)]
        bias_col = sb("bias_col", [128, 3, K])
        bias_row = sb("bias_row", [P, 3, D])
        a_T = sb("a_T", [128, 2, K, T], F16)
        b_T = sb("b_T", [128, 2, K, T], F16)
        fbuf = sb("fbuf", [128, 4, 375])
        cond = sb("cond", [81, T], F16)

        def row_stats(dve, chain, src, t):
            chain(nc.vector.bn_stats(stats[:, t, 2:8], src[:, t, :]))
            return nc.vector.bn_aggr(stats[:, t, 0:2], stats[:, t, 2:8])

        def inv_std(dve, chain, t0, t1, unit=1.0):
            V = nc.vector
            ve, r, q, h = (stats[:, t0:t1, i] for i in range(8, 12))
            chain(V.tensor_scalar(ve, stats[:, t0:t1, 1], EPS, None, ALU.add))
            chain(V.tensor_scalar(q.bitcast(I32), ve.bitcast(I32), 1, None, ALU.logical_shift_right))
            chain(V.tensor_scalar(r.bitcast(I32), q.bitcast(I32), -1.0, float(RSQRT_MAGIC), ALU.mult, ALU.add))
            for i in range(3):
                chain(V.tensor_tensor(q, r, r, ALU.mult))
                chain(V.tensor_tensor(q, q, ve, ALU.mult))
                u = unit if i == 2 else 1.0
                chain(V.tensor_scalar(h, q, -0.5 * u, 1.5 * u, ALU.mult, ALU.add))
                chain(V.tensor_tensor(r, r, h, ALU.mult))

        def norm(src, t, dst=None):
            return nc.vector.tensor_scalar((y if dst is None else dst)[:, t, :], src[:, t, :], stats[:, t, 0:1],
                                           stats[:, t, 9:10], ALU.subtract, ALU.mult)

        def cols(g):
            return slice(GROUPS[g][0] * P, (GROUPS[g][0] + GROUPS[g][1]) * P)

        def span(t):
            return slice(t * P, (t + 1) * P)

        def mat_to_T(dst, weights, act, m, g):
            n = len(PASSES) * K
            for i in range(n):
                (wp, ap), k = PASSES[i // K], i % K
                ins = nc.tensor.matmul(dst, weights[:, wp, k, m * 128:(m + 1) * 128], act[:, ap, k, cols(g)],
                                       start=i == 0, stop=i == n - 1)
            return ins

        def mat_to_rows(dst, weights, act, t, last=True):
            n = len(PASSES) * K
            for i in range(n):
                (ap, wp), k = PASSES[i // K], i % K
                ins = nc.tensor.matmul(dst, act[:, ap, k, span(t)], weights[:, wp, k, :],
                                       start=i == 0, stop=last and i == n - 1)
            return ins

        def load_w(eng, i, src, stg):
            eng.dma_start(stage[stg], src).then_inc(S[f"w_loaded{i}"], 16)

        def split_hi(i, stg):
            nc.scalar.wait_ge(S[f"w_loaded{i}"], 16)
            split_hi_now(i, stg)

        def split_hi_now(i, stg):
            nc.scalar.activation(w[i][:, 0], stage[stg], ACT.Copy, scale=WSCALE).then_inc(S[f"w_hi{i}"], 1)

        def split_lo(i, stg):
            nc.vector.wait_ge(S[f"w_hi{i}"], 1)
            nc.vector.scalar_tensor_tensor(w[i][:, 1], stage[stg], WSCALE, w[i][:, 0],
                                           ALU.mult, ALU.subtract).then_inc(S[f"w_lo{i}"], 1)

        graph = ExitStack()

        def gsb(name, shape, dt=F32):
            return graph.enter_context(nc.sbuf_tensor(name, shape, dt))

        idx_i = gsb("idx_i", [P, 2, NCH], I32)
        src_f = gsb("src_f", [P, NCH])
        dst_f = gsb("dst_f", [P, NCH])
        dst_hi = gsb("dst_hi", [P, NCH])
        dst_w = gsb("dst_w", [P, NCH])
        iota_i = gsb("iota_i", [P, T], I32)
        iota = gsb("iota", [P, T], F16)
        hot_s = gsb("hot_s", [P, UNROLL, T], F16)
        hot_d = gsb("hot_d", [P, UNROLL, HALF], F16)
        zeros = gsb("zeros", [P, 128], F16)
        free_w = parts[:, 2:6].rearrange("p s h k n -> p (s h k n)").bitcast(I32)
        copied = free_w[0:P, 0:2 * NT * HALF].rearrange("p (g t n) -> p g t n", g=2, t=NT)
        count = free_w[0:P, 2 * K * D:2 * K * D + NT * 2 * HALF].rearrange("p (t n) -> p t n", t=NT)
        cf = gsb("cf", [P, NT, T])
        digits = gsb("digits", [P, 2, 2, HALF], I32)
        adj = gsb("adj", [P, 2, NT, T], F16)
        xn = gsb("xn", [P, 2, NT, D], F16)

        with nc.Block() as block:
            @block.sync
            def _(sp):
                sp.dma_start(idx_i[:, 0, :], A["src"].rearrange("(p c) -> p c", p=P)).then_inc(S["idx_loaded"], 16)
                sp.dma_start(idx_i[:, 1, :], A["dst"].rearrange("(p c) -> p c", p=P)).then_inc(S["idx_loaded"], 16)
                sp.dma_start(x[:, :, :], x_in.rearrange("(t p) d -> p t d", p=P)).then_inc(S["x_loaded"], 16)
                for i, n in enumerate(("L0_gnn_W1", "L0_gnn_W2")):
                    load_w(sp, i, A[n], i)

            @block.gpsimd
            def _(pool):
                chain = Chain(pool, S["chain_pool"])
                nc.gpsimd.iota(iota_i[:, :], [[1, T]], base=0, channel_multiplier=0).then_inc(S["const_made"], 1)
                nc.gpsimd.memset(zeros[:, :], 0.0).then_inc(S["const_made"], 1)
                chain(nc.gpsimd.memset(ident[:, :], 0.0))
                nc.gpsimd.affine_select(out=ident[:, :], in_=ident[:, :], compare_op=ALU.not_equal, fill=1.0,
                                        base=0, pattern=[[-1, 128]], channel_multiplier=1).then_inc(S["const_made"], 1)
                chain(nc.gpsimd.memset(count[:, :, :], 0))
                n = 0
                for g in range(len(CHUNKS)):
                    for t in range(NT):
                        pool.wait_ge(S["count_split"], n + 1)
                        for j in range(2):
                            part = count[:, t, j * HALF:(j + 1) * HALF]
                            ins = nc.gpsimd.tensor_tensor(part, part, digits[:, n % 2, j, :], ALU.add)
                            if j == 0:
                                chain(ins)
                            else:
                                ins.then_inc(S["count_added"], 1)
                        n += 1

            @block.scalar
            def _(act):
                for i in range(2):
                    split_hi(i, i)
                for g in range(len(CHUNKS)):
                    for t in range(NT):
                        act.wait_ge(S["count_mm"], g * NT + t + 1)
                        if g >= 2:
                            act.wait_ge(S["count_split"], (g - 2) * NT + t + 1)
                        nc.scalar.activation(copied[:, g % 2, t, :], bank(t, P, HALF), ACT.Copy).then_inc(
                            S["count_copied"], 1)
                act.wait_ge(S["ln_c"], 1)
                nc.scalar.activation(lnc[:, :, :], lnc[:, :, :], ACT.Ln).then_inc(S["ln_c"], 1)

            @block.vector
            def _(dve):
                V = nc.vector
                chain = Chain(dve, S["chain_dve"])
                dve.wait_ge(S["idx_loaded"], 32)
                V.tensor_copy(src_f[:, :], idx_i[:, 0, :])
                chain(V.tensor_copy(dst_f[:, :], idx_i[:, 1, :]))
                chain(V.tensor_scalar(dst_hi[:, :], dst_f[:, :], float(HALF), None, ALU.is_ge))
                chain(V.tensor_scalar(dst_w[:, :], dst_hi[:, :], float(DIGIT - 1), 1.0, ALU.mult, ALU.add))
                chain(V.scalar_tensor_tensor(dst_f[:, :], dst_hi[:, :], -float(HALF), dst_f[:, :],
                                             ALU.mult, ALU.add))
                dve.wait_ge(S["const_made"], 1)
                chain(V.tensor_copy(iota[:, :], iota_i[:, :]))

                def unpack(g):
                    for t in range(NT):
                        n = g * NT + t
                        dve.wait_ge(S["count_copied"], n + 1)
                        if n >= 2:
                            dve.wait_ge(S["count_added"], n - 1)
                        V.tensor_scalar(digits[:, n % 2, 0, :], copied[:, g % 2, t, :], DIGIT - 1, None,
                                        ALU.bitwise_and)
                        V.tensor_scalar(digits[:, n % 2, 1, :], copied[:, g % 2, t, :], DIGIT.bit_length() - 1,
                                        None, ALU.logical_shift_right).then_inc(S["count_split"], 1)

                first = 0
                for g, n in enumerate(CHUNKS):
                    with dve.Fori(0, n // UNROLL) as body:
                        c0 = body * UNROLL + first
                        for j in range(UNROLL):
                            dve.wait_ge(S["onehot_used"], c0 + (j + 1))
                            c = dve.snap(c0 + j)
                            V.tensor_scalar(hot_s[:, j, :], iota[:, :], src_f[:, bass.ds(c, 1)], None, ALU.is_equal)
                            V.tensor_scalar(hot_d[:, j, :], iota[:, 0:HALF], dst_f[:, bass.ds(c, 1)],
                                            dst_w[:, bass.ds(c, 1)], ALU.is_equal, ALU.mult).then_inc(
                                S["onehot_ready"], 1)
                    first += n
                    if g == 0:
                        dve.wait_ge(S["x_loaded"], 16)
                    if g < NT:
                        chain(row_stats(dve, chain, x, g))
                        inv_std(dve, chain, g, g + 1)
                        chain(norm(x, g))
                        chain(V.tensor_copy(xn[:, 0, g, :], y[:, g, :]))
                        chain(V.tensor_tensor(xn[:, 1, g, :], y[:, g, :], xn[:, 0, g, :], ALU.subtract))
                    if 1 <= g <= 2:
                        split_lo(g - 1, g - 1)
                    if g >= 1:
                        unpack(g - 1)
                unpack(len(CHUNKS) - 1)
                dve.wait_ge(S["count_added"], len(CHUNKS) * NT)
                for t in range(NT):
                    chain(V.tensor_copy(cf[:, t, :], count[:, t, 0:T]))
                    chain(V.tensor_scalar(lnc[:, t, :], cf[:, t, :], 1.0, None, ALU.max))
                dve.wait_ge(S["const_made"], 3)
                V.nop().then_inc(S["ln_c"], 1)
                dve.wait_ge(S["ln_c"], 2)
                for t in range(NT):
                    chain(V.tensor_scalar(y[:, 0:2, :].rearrange("p a b -> p (a b)")[:, 0:T], cf[:, t, :], 0.0,
                                          MASKED, ALU.is_equal, ALU.mult))
                    chain(V.tensor_tensor(lnc[:, t, :], lnc[:, t, :],
                                          y[:, 0:2, :].rearrange("p a b -> p (a b)")[:, 0:T], ALU.add))
                    chain(V.tensor_tensor(cf[:, t, span(t)], cf[:, t, span(t)], ident[0:P, 0:P], ALU.add))
                    chain(V.tensor_copy(adj[:, 0, t, :], cf[:, t, :]))
                    chain(V.tensor_tensor(adj[:, 1, t, :], cf[:, t, :], adj[:, 0, t, :], ALU.subtract))

            @block.tensor
            def _(pe):
                pe.wait_ge(S["const_made"], 2)
                pe.sem_inc(S["onehot_used"], UNROLL)

                def edge(t, start):
                    return nc.tensor.matmul(bank(t, P, 2), zeros[:, 0:P], zeros[:, 0:2], start=start,
                                            stop=not start, skip_group_check=True)

                first = 0
                for g, n in enumerate(CHUNKS):
                    for t in range(NT):
                        if g:
                            pe.wait_ge(S["count_copied"], (g - 1) * NT + t + 1)
                        edge(t, True)
                    with pe.Fori(0, n // UNROLL) as body:
                        c0 = body * UNROLL + first
                        for j in range(UNROLL):
                            pe.wait_ge(S["onehot_ready"], c0 + (j + 1))
                            for t in range(NT):
                                ins = nc.tensor.matmul(bank(t, P, HALF), hot_s[:, j, span(t)], hot_d[:, j, :],
                                                       start=False, stop=False, skip_group_check=True)
                            ins.then_inc(S["onehot_used"], 1)
                    first += n
                    for t in range(NT):
                        edge(t, False).then_inc(S["count_mm"], 1)
        clear_all()


        def evac_T(act, s, u, dst, src, m, where, func, scale=1.0, bias=None, slot_free=None):
            n = where.stop - where.start
            act.wait_ge(S[s + "_mm"], u + 1)
            if slot_free is not None:
                act.wait_ge(*slot_free)
            f = fbuf[:, u % 4, 0:n]
            if bias is None:
                nc.scalar.activation(f, src, func, scale=scale).then_inc(S[s + "_f"], 1)
            else:
                nc.scalar.activation(f, src, func, scale=scale, bias=bias).then_inc(S[s + "_f"], 1)
            act.wait_ge(S[s + "_f"], u + 1)
            nc.scalar.activation(dst[:, 0, m, where], f, ACT.Copy).then_inc(S[s + "_hi"], 1)

        def low_T(dve, s, u, dst, m, where):
            n = where.stop - where.start
            dve.wait_ge(S[s + "_hi"], u + 1)
            nc.vector.tensor_tensor(dst[:, 1, m, where], fbuf[:, u % 4, 0:n], dst[:, 0, m, where],
                                    ALU.subtract).then_inc(S[s + "_lo"], 1)

        def tr_bank(b):
            return ps[:, b, 0:K * P].rearrange("p (k n) -> p k n", k=K)

        def transpose_rows(pe, b, src, sem):
            for k in range(K):
                ins = nc.tensor.transpose(ps[:, b, k * P:(k + 1) * P], src[:, k * 128:(k + 1) * 128],
                                          ident[0:P, 0:P])
            ins.then_inc(sem, 1)

        units8 = [(g, m) for g in range(2) for m in range(K)]
        with nc.Block() as block:
            @block.sync
            def _(sp):
                sp.dma_start(bias_col[:, 0, :], A["L0_gnn_b1"]).then_inc(
                    S["bias_loaded"], 16)
                sp.dma_start(bias_row[:, 0, :], A["L0_gnn_b2"].partition_broadcast(P)).then_inc(
                    S["bias_loaded"], 16)
                load_w(sp, 2, A["L0_ffn_W1"], 2)
                load_w(sp, 3, A["L0_ffn_W2"], 0)

            @block.gpsimd
            def _(pool):
                pool.wait_ge(S["bias_loaded"], 32)
                for t in range(NT):
                    nc.gpsimd.tensor_tensor(x[:, t, :], x[:, t, :], bias_row[:, 0, :], ALU.add).then_inc(
                        S["resb1"], 1)

            @block.tensor
            def _(pe):
                for u, (g, m) in enumerate(units8):
                    if u >= 4:
                        pe.wait_ge(S["a_f"], u - 3)
                    n = len(PASSES) * NT
                    dst = bank(u % 4, 128, GROUPS[g][1] * P)
                    for i in range(n):
                        (ap, wp), t = PASSES[i // NT], i % NT
                        ins = nc.tensor.matmul(dst, xn[:, ap, t, m * 128:(m + 1) * 128], adj[:, wp, t, cols(g)],
                                               start=i == 0, stop=i == n - 1)
                    ins.then_inc(S["a_mm"], 1)
                for u, (g, m) in enumerate(units8):
                    pe.wait_ge(S["a_lo"], 4 * (g + 1))
                    if u >= 4:
                        pe.wait_ge(S["b_f"], u - 3)
                    mat_to_T(bank(4 + u % 4, 128, GROUPS[g][1] * P), w[0], a_T, m, g).then_inc(S["b_mm"], 1)
                for t in range(NT):
                    pe.wait_ge(S["b_lo"], 4 if t < 3 else 8)
                    if t >= 4:
                        pe.wait_ge(S["res1"], t - 3)
                    mat_to_rows(bank(t % 4, P), w[1], b_T, t).then_inc(S["res1_mm"], 1)

            @block.scalar
            def _(act):
                for u, (g, m) in enumerate(units8):
                    evac_T(act, "a", u, a_T, bank(u % 4, 128, GROUPS[g][1] * P), m, cols(g), ACT.Copy,
                           slot_free=(S["a_lo"], u - 3) if u >= 4 else None)
                act.wait_ge(S["bias_loaded"], 32)
                for u, (g, m) in enumerate(units8):
                    evac_T(act, "b", u, b_T, bank(4 + u % 4, 128, GROUPS[g][1] * P), m, cols(g), ACT.Relu,
                           scale=1 / WSCALE, bias=bias_col[:, 0, m:m + 1],
                           slot_free=(S["b_lo"], u - 3) if u >= 4 else (S["a_lo"], u + 5))
                split_hi(2, 2)
                split_hi(3, 0)

            @block.vector
            def _(dve):
                for u, (g, m) in enumerate(units8):
                    low_T(dve, "a", u, a_T, m, cols(g))
                for u, (g, m) in enumerate(units8):
                    low_T(dve, "b", u, b_T, m, cols(g))
                split_lo(2, 2)
                split_lo(3, 0)
                for t in range(NT):
                    dve.wait_ge(S["res1_mm"], t + 1)
                    dve.wait_ge(S["resb1"], t + 1)
                    nc.vector.scalar_tensor_tensor(x[:, t, :], bank(t % 4, P), 1 / WSCALE, x[:, t, :],
                                                   ALU.mult, ALU.add).then_inc(S["res1"], 1)
        clear_all()

        graph.close()

        def experts(Wr, br, W1, b1, W2, b2, top, cap, i1, i2, last):
            moe = ExitStack()

            def msb(name, shape, dt=F32):
                return moe.enter_context(nc.sbuf_tensor(name + ("a" if cap else "b"), shape, dt))

            wr_f = msb("wr_f", [128, K, E])
            wr = msb("wr", [128, 2, K, E], F16)
            br_row = msb("br_row", [P, E])
            b2_f = msb("b2_f", [E, D])
            b2_p = msb("b2_p", [E, 2, D], F16)
            prob = msb("prob", [P, NT, E])
            hot = msb("hot", [P, 3, NT, E])
            top_v = msb("top_v", [P, NT, 8])
            top_i = msb("top_i", [P, NT, 8], U32)
            top_f = msb("top_f", [P, NT, 8])
            one = msb("one", [P, 8, NT])
            sent = msb("sent", [P, NT, E], F16)
            before = msb("before", [P, 2, P], F16)
            iota_e = msb("iota_e", [P, E], I32)
            iota_f = msb("iota_f", [P, E])
            wt = msb("wt", [E, 2, T], F16)
            hid = msb("hid", [P, 2, D])

            def each(v):
                return v.unsqueeze(2).to_broadcast([P, NT, E])

            with nc.Block() as block:
                @block.sync
                def _(sp):
                    sp.dma_start(wr_f[:, :, :], Wr).then_inc(S["small_loaded"], 16)
                    sp.dma_start(br_row[:, :], br.partition_broadcast(P)).then_inc(S["small_loaded"], 16)
                    sp.dma_start(b2_f[:, :], b2).then_inc(S["small_loaded"], 16)
                    sp.dma_start(bias_row[:, 1, :], b1.partition_broadcast(P)).then_inc(
                        S["small_loaded"], 16)
                    if last:
                        load_w(sp, i1, W1, 0)
                        load_w(sp, i2, W2, 1)
                    else:
                        for i, n in enumerate(("wq", "wk", "wv", "wo")):
                            if i == 3:
                                sp.wait_ge(S["w_lo0"], 1)
                            load_w(sp, i, A["L1_gnn_" + n][0], i % 3)
                    if last:
                        for t in range(NT):
                            sp.wait_ge(S["res1"], t + 1)
                            sp.dma_start(out[span(t), :], x[:, t, :]).then_inc(S["stored"], 16)
                        sp.wait_ge(S["stored"], 16 * NT)

                @block.gpsimd
                def _(pool):
                    chain = Chain(pool, S["chain_pool"])
                    nc.gpsimd.iota(iota_e[:, :], [[1, E]], base=0, channel_multiplier=0).then_inc(S["const_made"], 1)
                    chain(nc.gpsimd.memset(before[:, :, :], 1.0))
                    nc.gpsimd.affine_select(out=before[:, 0, :], in_=before[:, 0, :], compare_op=ALU.is_gt,
                                            fill=0.0, base=0, pattern=[[1, P]], channel_multiplier=-1).then_inc(
                        S["const_made"], 1)

                @block.vector
                def _(dve):
                    V = nc.vector
                    chain = Chain(dve, S["chain_dve"])
                    for t in range(NT):
                        chain(row_stats(dve, chain, x, t))
                    inv_std(dve, chain, 0, NT)
                    for t in range(NT):
                        norm(x, t).then_inc(S["norm1"], 1)
                    dve.wait_ge(S["small_loaded"], 64)
                    chain(V.tensor_scalar(wr_f[:, :, :], wr_f[:, :, :], WSCALE, None, ALU.mult))
                    chain(V.tensor_copy(wr[:, 0], wr_f[:, :, :]))
                    V.tensor_tensor(wr[:, 1], wr_f[:, :, :], wr[:, 0], ALU.subtract).then_inc(S["small_lo"], 1)
                    chain(V.tensor_scalar(b2_f[:, :], b2_f[:, :], WSCALE, None, ALU.mult))
                    chain(V.tensor_copy(b2_p[:, 0, :], b2_f[:, :]))
                    V.tensor_tensor(b2_p[:, 1, :], b2_f[:, :], b2_p[:, 0, :], ALU.subtract).then_inc(S["small_lo"], 1)
                    if last:
                        split_lo(i1, 0)
                        split_lo(i2, 1)
                    for t in range(NT):
                        dve.wait_ge(S["yt_hi1"], t + 1)
                        V.tensor_tensor(a_T[:, 1, :, span(t)], tr_bank(t % 2), a_T[:, 0, :, span(t)],
                                        ALU.subtract).then_inc(S["yt_lo1"], 1)
                    dve.wait_ge(S["r_mm"], NT)
                    lg = ps[0:P, 4, 0:NT * E].rearrange("p (t e) -> p t e", e=E)
                    chain(V.scalar_tensor_tensor(prob[:, :, :], lg, 1 / WSCALE,
                                                 br_row[:, :].unsqueeze(1).to_broadcast([P, NT, E]),
                                                 ALU.mult, ALU.add))
                    chain(V.reduce_max(one[:, 0, :], prob[:, :, :], AX_X))
                    V.tensor_tensor(prob[:, :, :], prob[:, :, :], each(one[:, 0, :]), ALU.subtract).then_inc(
                        S["r_lg"], 1)
                    dve.wait_ge(S["r_exp"], 1)
                    chain(V.reduce_sum(one[:, 1, :], prob[:, :, :], AX_X))
                    chain(V.reciprocal(one[:, 2, :], one[:, 1, :]))
                    chain(V.tensor_tensor(prob[:, :, :], prob[:, :, :], each(one[:, 2, :]), ALU.mult))
                    for t in range(NT):
                        chain(V.max(top_v[:, t, :], prob[:, t, :]))
                        chain(V.max_index(top_i[:, t, :], top_v[:, t, :], prob[:, t, :]))
                    chain(V.tensor_copy(top_f[:, :, :], top_i[:, :, :]))
                    dve.wait_ge(S["const_made"], 2)
                    chain(V.tensor_copy(iota_f[:, :], iota_e[:, :]))
                    for j in range(top):
                        chain(V.tensor_tensor(hot[:, j], iota_f[:, :].unsqueeze(1).to_broadcast([P, NT, E]),
                                              each(top_f[:, :, j]), ALU.is_equal))
                    gate = hot[:, 0]
                    if top == 1:
                        chain(V.tensor_tensor(gate, gate, each(top_v[:, :, 0]), ALU.mult))
                    else:
                        chain(V.tensor_tensor(hot[:, 2], hot[:, 0], hot[:, 1], ALU.add))
                        V.tensor_copy(sent[:, :, :], hot[:, 2]).then_inc(S["r_w"], 1)
                        chain(V.tensor_tensor(one[:, 3, :], top_v[:, :, 0], top_v[:, :, 1], ALU.add))
                        chain(V.tensor_scalar(one[:, 3, :], one[:, 3, :], 1e-9, None, ALU.add))
                        chain(V.reciprocal(one[:, 4, :], one[:, 3, :]))
                        for j in range(top):
                            chain(V.tensor_tensor(one[:, 5 + j, :], top_v[:, :, j], one[:, 4, :], ALU.mult))
                            chain(V.tensor_tensor(hot[:, j], hot[:, j], each(one[:, 5 + j, :]), ALU.mult))
                        chain(V.tensor_tensor(gate, hot[:, 0], hot[:, 1], ALU.add))
                        dve.wait_ge(S["pos_mm"], NT)
                        pos = ps[0:P, 5, 0:NT * E].rearrange("p (t e) -> p t e", e=E)
                        chain(V.tensor_scalar(hot[:, 2], pos, float(cap), None, ALU.is_lt))
                        chain(V.tensor_tensor(gate, gate, hot[:, 2], ALU.mult))
                        chain(V.reduce_sum(one[:, 1, :], gate, AX_X))
                        chain(V.tensor_scalar(one[:, 1, :], one[:, 1, :], 1e-9, None, ALU.add))
                        chain(V.reciprocal(one[:, 2, :], one[:, 1, :]))
                        chain(V.tensor_tensor(gate, gate, each(one[:, 2, :]), ALU.mult))
                    V.nop().then_inc(S["pos_done"], 1)
                    for t in range(NT):
                        dve.wait_ge(S["gm"], t + 1)
                        if t >= 2:
                            dve.wait_ge(S["hm_done"], t - 1)
                        V.scalar_tensor_tensor(hid[:, t % 2, :], bank(6 + t % 2, P), 1 / WSCALE, bias_row[:, 1, :],
                                               ALU.mult, ALU.add).then_inc(S["mod1"], 1)
                        dve.wait_ge(S["gelu_done"], t + 1)
                        V.tensor_tensor(y[:, t, :].rearrange("p (e f) -> p e f", e=E),
                                        hid[:, t % 2, :].rearrange("p (e f) -> p e f", e=E),
                                        gate[:, t, :].unsqueeze(2).to_broadcast([P, E, DFF]),
                                        ALU.mult).then_inc(S["hm_done"], 1)
                    dve.wait_ge(S["wt_mm"], 1)
                    wtp = blocks(4, E)
                    wt3 = wt[:, :, :].rearrange("e a (t n) -> e a t n", n=P)
                    chain(V.tensor_copy(wt3[:, 0], wtp))
                    V.tensor_tensor(wt3[:, 1], wtp, wt3[:, 0], ALU.subtract).then_inc(S["wt_parts"], 1)
                    for t in range(NT):
                        dve.wait_ge(S["yt_hi2"], t + 1)
                        V.tensor_tensor(b_T[:, 1, :, span(t)], tr_bank(t % 2), b_T[:, 0, :, span(t)],
                                        ALU.subtract).then_inc(S["yt_lo2"], 1)
                    for t in range(NT):
                        dve.wait_ge(S["res1_mm"], t + 1)
                        V.scalar_tensor_tensor(x[:, t, :], bank(2 + t % 2, P), 1 / WSCALE, x[:, t, :],
                                               ALU.mult, ALU.add).then_inc(S["res1"], 1)
                    if not last:
                        for i in range(4):
                            split_lo(i, i % 3)

                @block.scalar
                def _(act):
                    if last:
                        split_hi(i1, 0)
                        split_hi(i2, 1)
                    for t in range(NT):
                        act.wait_ge(S["yt_mm1"], t + 1)
                        nc.scalar.activation(a_T[:, 0, :, span(t)], tr_bank(t % 2), ACT.Copy).then_inc(S["yt_hi1"], 1)
                    act.wait_ge(S["r_lg"], 1)
                    nc.scalar.activation(prob[:, :, :], prob[:, :, :], ACT.Exp).then_inc(S["r_exp"], 1)
                    for t in range(NT):
                        act.wait_ge(S["mod1"], t + 1)
                        nc.scalar.activation(hid[:, t % 2, :], hid[:, t % 2, :], ACT.Gelu).then_inc(S["gelu_done"], 1)
                    for t in range(NT):
                        act.wait_ge(S["yt_mm2"], t + 1)
                        nc.scalar.activation(b_T[:, 0, :, span(t)], tr_bank(t % 2), ACT.Copy).then_inc(S["yt_hi2"], 1)
                    if not last:
                        for i in range(4):
                            if i >= 2:
                                act.wait_ge(S["res1_mm"], NT)
                            split_hi(i, i % 3)

                @block.tensor
                def _(pe):
                    for t in range(NT):
                        pe.wait_ge(S["norm1"], t + 1)
                        if t >= 2:
                            pe.wait_ge(S["yt_lo1"], t - 1)
                        transpose_rows(pe, t % 2, y[:, t, :], S["yt_mm1"])
                    pe.wait_ge(S["small_lo"], 2)
                    n = len(PASSES) * K
                    for t in range(NT):
                        pe.wait_ge(S["yt_lo1"], t + 1)
                        for i in range(n):
                            (ap, wp), k = PASSES[i // K], i % K
                            ins = nc.tensor.matmul(ps[0:P, 4, t * E:(t + 1) * E], a_T[:, ap, k, span(t)],
                                                   wr[:, wp, k, :], start=i == 0, stop=i == n - 1)
                        ins.then_inc(S["r_mm"], 1)
                    if last:
                        pe.wait_ge(S[f"w_lo{i1}"], 1)
                    for t in range(2):
                        mat_to_rows(bank(6 + t % 2, P), w[i1], a_T, t).then_inc(S["gm"], 1)
                    if cap:
                        pe.wait_ge(S["const_made"], 2)
                        pe.wait_ge(S["r_w"], 1)
                        for t in range(NT):
                            for s in range(t + 1):
                                ins = nc.tensor.matmul(ps[0:P, 5, t * E:(t + 1) * E],
                                                       before[:, 0 if s == t else 1, :], sent[:, s, :],
                                                       start=s == 0, stop=s == t)
                            ins.then_inc(S["pos_mm"], 1)
                    for t in range(2, NT):
                        pe.wait_ge(S["mod1"], t - 1)
                        mat_to_rows(bank(6 + t % 2, P), w[i1], a_T, t).then_inc(S["gm"], 1)
                    pe.wait_ge(S["pos_done"], 1)
                    for t in range(NT):
                        ins = nc.tensor.transpose(blocks(4, E)[:, t, :], hot[:, 0, t, :], ident[0:P, 0:P])
                    ins.then_inc(S["wt_mm"], 1)
                    for t in range(NT):
                        pe.wait_ge(S["hm_done"], t + 1)
                        if t >= 2:
                            pe.wait_ge(S["yt_lo2"], t - 1)
                        transpose_rows(pe, t % 2, y[:, t, :], S["yt_mm2"])
                    pe.wait_ge(S["wt_parts"], 1)
                    if last:
                        pe.wait_ge(S[f"w_lo{i2}"], 1)
                    for t in range(NT):
                        pe.wait_ge(S["yt_lo2"], t + 1)
                        if t >= 2:
                            pe.wait_ge(S["res1"], t - 1)
                        mat_to_rows(bank(2 + t % 2, P), w[i2], b_T, t, last=False)
                        for i, (ap, wp) in enumerate(PASSES):
                            ins = nc.tensor.matmul(bank(2 + t % 2, P), wt[:, ap, span(t)], b2_p[:, wp, :],
                                                   start=False, stop=i == len(PASSES) - 1)
                        ins.then_inc(S["res1_mm"], 1)
            moe.close()
            clear_all()

        experts(A["L0_ffn_Wr"], A["L0_ffn_br"], A["L0_ffn_W1"], A["L0_ffn_b1"], A["L0_ffn_W2"], A["L0_ffn_b2"],
                top=2, cap=CAP, i1=2, i2=3, last=False)

        net = ExitStack()

        def nsb(name, shape, dt=F32):
            return net.enter_context(nc.sbuf_tensor(name, shape, dt))

        mod_f = nsb("mod_f", [81, 4, D])
        mod_p = nsb("mod_p", [81, 4, D], F16)
        q_T = nsb("q_T", [128, 2, K, T], F16)
        k_T = b_T
        v_p = nsb("v_p", [P, 2, NT, D], F16)
        GMAX = max(n for _, n in GROUPS) * P + 1
        p_T = nsb("p_T", [P, 2, 2, NT, GMAX], F16)
        rows_s = nsb("rows_s", [P, 3, T])
        soft = nsb("soft", [P, 3, 4])

        def mod_hi(act):
            nc.scalar.activation(mod_p[:, :, :], mod_f[:, :, :], ACT.Copy, scale=WSCALE).then_inc(S["small_hi"], 1)

        def mod_lo(dve):
            dve.wait_ge(S["small_hi"], 1)
            nc.vector.scalar_tensor_tensor(mod_p[64:81], mod_f[64:81], WSCALE, mod_p[64:81],
                                           ALU.mult, ALU.subtract).then_inc(S["small_lo"], 1)

        flat = p_T[:, :, :, :, :].rearrange("p a b t n -> p (a b t n)").bitcast(F32)
        phase = flat[0:2 * NF, 0:T]
        turns = flat[0:2 * NF, T:2 * T]
        noise = flat[0:2 * NF, 2 * T:3 * T]
        cond_f = rows_s[:, :, :].rearrange("p a t -> p (a t)")[0:81, 0:T]
        e1_f = rows_s[:, :, :].rearrange("p a t -> p (a t)")[0:C, T:2 * T]
        emb = q_T[0:2 * NF, 0, 0:2, :]
        e1 = q_T[0:C, 0, 2:4, :]
        f_w1f = fbuf[0:2 * NF, 0, 0:C]
        f_w2f = fbuf[0:C, 1, 0:81]
        f_b = fbuf[0:81, 2, 0:2]
        freq = fbuf[0:2 * NF, 3, 0:4]
        f_w1 = b_T[0:2 * NF, 0, 0:2, 0:C]
        f_w2 = b_T[0:C, 0, 2:4, 0:81]
        freq_i = stats[0:2 * NF, NT - 1, 12:13].bitcast(I32)
        halves = ((0, 512), (512, T))

        with nc.Block() as block:
            @block.sync
            def _(sp):
                for dst, src in ((noise, A["noise"].partition_broadcast(2 * NF)), (f_w1f[:, :], A["L1_gnn_f_w1"]),
                                 (f_w2f[:, :], A["f_w2"]), (f_b[:, :], A["f_b"]), (mod_f[:, :, :], A["mod"][0])):
                    sp.dma_start(dst, src).then_inc(S["small_loaded"], 16)
                load_w(sp, 4, A["L1_gnn_m_w1"][0], 0)
                load_w(sp, 5, A["L1_gnn_m_w2"][0], 1)
                sp.wait_ge(S["w_loaded4"], 16)
                sp.wait_ge(S["w_loaded5"], 16)

            @block.gpsimd
            def _(pool):
                nc.gpsimd.iota(freq_i, [[1, 1]], base=1, channel_multiplier=1).then_inc(S["const_made"], 1)

            @block.vector
            def _(dve):
                V = nc.vector
                chain = Chain(dve, S["chain_dve"])
                dve.wait_ge(S["const_made"], 1)
                k, is_cos, shift, f = (freq[:, i:i + 1] for i in range(4))
                chain(V.tensor_copy(k, freq_i))
                chain(V.tensor_scalar(is_cos, k, float(NF), None, ALU.is_gt))
                chain(V.scalar_tensor_tensor(k, is_cos, -float(NF), k, ALU.mult, ALU.add))
                chain(V.tensor_scalar(shift, is_cos, 1.5707963267948966, None, ALU.mult))
                chain(V.tensor_scalar(f, k, 0.39269908169872414, None, ALU.mult))
                dve.wait_ge(S["small_loaded"], 80)
                chain(V.tensor_scalar(phase, noise, f, None, ALU.mult))
                chain(V.tensor_scalar(turns, phase, INV_TWO_PI, ROUND_MAGIC, ALU.mult, ALU.add))
                chain(V.tensor_scalar(turns, turns, ROUND_MAGIC, None, ALU.subtract))
                for part in TWO_PI_PARTS:
                    chain(V.scalar_tensor_tensor(phase, turns, -part, phase, ALU.mult, ALU.add))
                chain(V.tensor_scalar(phase, phase, shift, None, ALU.add))
                chain(V.tensor_scalar(turns, phase, 3.141592653589793, -6.283185307179586, ALU.is_gt, ALU.mult))
                chain(V.tensor_tensor(phase, phase, turns, ALU.add))
                V.tensor_scalar(phase, phase, PI_SAFE, -PI_SAFE, ALU.min, ALU.max).then_inc(S["e_a"], 1)
                for f_, p_ in ((f_w1f, f_w1), (f_w2f, f_w2)):
                    chain(V.tensor_scalar(f_[:, :], f_[:, :], WSCALE, None, ALU.mult))
                    chain(V.tensor_copy(p_[:, 0, :], f_[:, :]))
                    chain(V.tensor_tensor(p_[:, 1, :], f_[:, :], p_[:, 0, :], ALU.subtract))
                dve.wait_ge(S["e_b"], 1)
                chain(V.tensor_copy(emb[:, 0, :], phase))
                V.tensor_tensor(emb[:, 1, :], phase, emb[:, 0, :], ALU.subtract).then_inc(S["e_c"], 1)
                for t in range(NT):
                    chain(row_stats(dve, chain, x, t))
                inv_std(dve, chain, 0, NT)
                dve.wait_ge(S["e_d"], 1)
                chain(V.tensor_copy(e1[:, 0, :], e1_f))
                V.tensor_tensor(e1[:, 1, :], e1_f, e1[:, 0, :], ALU.subtract).then_inc(S["e_c"], 1)
                for t in range(NT):
                    chain(norm(x, t, dst=xg))
                dve.wait_ge(S["e_d"], 2)
                chain(V.tensor_copy(cond[:, :], cond_f))
                chain(V.tensor_tensor(cond[32:32 + C, :], cond_f[32:32 + C, :], cond[32:32 + C, :], ALU.subtract))
                mod_lo(dve)

            @block.scalar
            def _(act):
                act.wait_ge(S["e_a"], 1)
                nc.scalar.activation(phase, phase, ACT.Sin).then_inc(S["e_b"], 1)
                act.wait_ge(S["e_e"], 1)
                nc.scalar.activation(e1_f, pair(0, C, T), ACT.Silu, scale=1 / WSCALE, bias=f_b[0:C, 1:2]).then_inc(
                    S["e_d"], 1)
                act.wait_ge(S["e_e"], 2)
                nc.scalar.activation(cond_f, pair(2, 81, T), ACT.Identity, scale=1 / WSCALE,
                                     bias=f_b[:, 0:1]).then_inc(S["e_d"], 1)
                mod_hi(act)

            @block.tensor
            def _(pe):
                pe.wait_ge(S["e_c"], 1)
                for a, b in halves:
                    for i, (wp, ep) in enumerate(PASSES):
                        ins = nc.tensor.matmul(pair(0, C, T)[:, a:b], f_w1[:, wp, :], emb[:, ep, a:b],
                                               start=i == 0, stop=i == len(PASSES) - 1)
                ins.then_inc(S["e_e"], 1)
                pe.wait_ge(S["e_c"], 2)
                for a, b in halves:
                    for i, (wp, ep) in enumerate(PASSES):
                        ins = nc.tensor.matmul(pair(2, 81, T)[:, a:b], f_w2[:, wp, :], e1[:, ep, a:b],
                                               start=i == 0, stop=i == len(PASSES) - 1)
                ins.then_inc(S["e_e"], 1)
        clear_all()

        qk_units = [(g, which, m) for g in range(2) for which in range(2) for m in range(K)]
        QK_BANK = (6, 7, 0, 1)
        C_BANK = (0, 1, 4, 5)
        NEXT = ((0, 2), (1, 0), (2, 1), (3, 2))
        heads = [(g, h) for g in range(2) for h in range(H)]
        s_units = [(g, h, i) for g, h in heads for i in range(GROUPS[g][1])]
        NS = len(s_units)
        last_of = {}
        for n, (g, h, i) in enumerate(s_units):
            last_of[g * H + h] = n
        av_after = {last_of[gh] + 1: gh for gh in range(2 * H)}
        o_after = {last_of[gh] + 3: gh for gh in range(2 * H)}

        def modulate(dve, chain, t, j, base, sem):
            dve.wait_ge(S[f"mod_mm{j}"], t + 1)
            nc.vector.scalar_tensor_tensor(y[:, t, :], bank(base(t), P), WSCALE, y[:, t, :],
                                           ALU.add, ALU.mult).then_inc(sem, 1)

        def mod_rows(t, j, base):
            nc.tensor.matmul(bank(base(t), P), cond[:, span(t)], mod_p[:, 2 * (j - 1), :],
                             start=True, stop=True).then_inc(S[f"mod_mm{j}"], 1)

        def base1(t):
            return t % 4

        def base2(t):
            return 2 + t % 4

        with nc.Fori(0, NL) as layer:
            with nc.Block() as block:
                @block.sync
                def _(sp):
                    nxt = sp.snap((layer + 1) % NL)

                    def of(name, which):
                        return A[name][bass.ds(which, 1)]

                    sp.dma_start(bias_col[:, :, :], of("L1_gnn_cols", layer)[0]).then_inc(S["bias_loaded"], 16)
                    for i, n in enumerate(("bv", "bo", "m_b2")):
                        sp.dma_start(bias_row[:, i, :], of("L1_gnn_" + n, layer)[0].partition_broadcast(P)).then_inc(
                            S["bias_loaded"], 16)
                    sp.dma_start(mod_f[:, :, :], of("mod", nxt)[0]).then_inc(S["small_loaded"], 16)
                    load_w(sp, 0, of("L1_gnn_wq", nxt)[0], 2)
                    sp.wait_ge(S["w_lo4"], 1)
                    load_w(sp, 1, of("L1_gnn_wk", nxt)[0], 0)
                    sp.wait_ge(S["w_lo5"], 1)
                    load_w(sp, 2, of("L1_gnn_wv", nxt)[0], 1)
                    sp.wait_ge(S["w_lo0"], 1)
                    load_w(sp, 3, of("L1_gnn_wo", nxt)[0], 2)
                    sp.wait_ge(S["w_lo1"], 1)
                    load_w(sp, 4, of("L1_gnn_m_w1", nxt)[0], 0)
                    sp.wait_ge(S["w_lo2"], 1)
                    load_w(sp, 5, of("L1_gnn_m_w2", nxt)[0], 1)
                    for i in (4, 5):
                        sp.wait_ge(S[f"w_loaded{i}"], 16)

                @block.gpsimd
                def _(pool):
                    pool.wait_ge(S["bias_loaded"], 64)
                    pool.wait_ge(S["norm1"], NT)
                    for t in range(NT):
                        nc.gpsimd.tensor_tensor(xg[:, t, :], xg[:, t, :], bias_row[:, 1, :], ALU.add).then_inc(
                            S["resb1"], 1)
                    for t in range(NT):
                        pool.wait_ge(S["v_f"], t + 1)
                        pool.wait_ge(S["v_hi"], t + 1)
                        nc.gpsimd.tensor_tensor(v_p[:, 1, t, :], y[:, t, :], v_p[:, 0, t, :],
                                                ALU.subtract).then_inc(S["v_lo"], 1)
                    for t in range(NT):
                        pool.wait_ge(S["norm2"], t + 1)
                        nc.gpsimd.tensor_tensor(xg[:, t, :], xg[:, t, :], bias_row[:, 2, :], ALU.add).then_inc(
                            S["resb2"], 1)

                @block.tensor
                def _(pe):
                    def score(n):
                        g, h, i = s_units[n]
                        t = GROUPS[g][0] + i
                        if n >= 2:
                            pe.wait_ge(S["s_max"], n - 1)
                        for a, b in halves:
                            for j, (qp, kp) in enumerate(PASSES):
                                ins = nc.tensor.matmul(pair(2 * (n % 2), P, T)[:, a:b], q_T[:, qp, h, span(t)],
                                                       k_T[:, kp, h, a:b], start=j == 0, stop=j == len(PASSES) - 1)
                        ins.then_inc(S["s_mm"], 1)

                    def prob_T(n):
                        pe.wait_ge(S["s_prob"], n + 1)
                        if n:
                            pe.wait_ge(S["pt_lo"], n)
                        for j in range(NT):
                            ins = nc.tensor.transpose(blocks(4, P)[:, j, :], rows_s[:, n % 3, span(j)],
                                                      ident[0:P, 0:P])
                        ins.then_inc(S["pt_mm"], 1)

                    def times_v(gh):
                        g, h = heads[gh]
                        cells = GROUPS[g][1] * P
                        pe.wait_ge(S["pt_lo"], last_of[gh] + 1)
                        if gh >= 2:
                            pe.wait_ge(S["o_f"], gh - 1)
                        c = len(PASSES) * NT
                        for i in range(c):
                            (vp, pp), j = PASSES[i // NT], i % NT
                            ins = nc.tensor.matmul(bank(6 + gh % 2, 128, cells),
                                                   v_p[:, vp, j, h * DH:(h + 1) * DH],
                                                   p_T[:, gh % 2, pp, j, 0:cells], start=i == 0, stop=i == c - 1)
                        ins.then_inc(S["o_mm"], 1)

                    def transposed(t, j, b):
                        pe.wait_ge(S[f"mod{j}"], t + 1)
                        if t >= 2:
                            pe.wait_ge(S[f"yt_lo{j}"], t - 1)
                        for k in range(K):
                            nc.tensor.matmul(ps[:, b + t % 2, k * P:(k + 1) * P], y[:, t, k * 128:(k + 1) * 128],
                                             ident[0:P, 0:P], is_transpose=True, start=k == 0, stop=False,
                                             skip_group_check=True)
                        for k in range(K):
                            ins = nc.tensor.matmul(ps[:, b + t % 2, k * P:(k + 1) * P],
                                                   mod_p[:, 2 * j - 1, k * 128:(k + 1) * 128], cond[:, span(t)],
                                                   start=False, stop=k == K - 1, skip_group_check=True)
                        ins.then_inc(S[f"yt_mm{j}"], 1)

                    for t in range(NT + 1):
                        if t < NT:
                            if t >= 4:
                                pe.wait_ge(S["mod1"], t - 3)
                            mod_rows(t, 1, base1)
                        if t:
                            transposed(t - 1, 1, 4)
                    for u, (g, which, m) in enumerate(qk_units):
                        pe.wait_ge(S["yt_lo1"], 3 if g == 0 else NT)
                        if u < 4:
                            pe.wait_ge(S["mod1"], NT)
                        else:
                            pe.wait_ge(S["a_f"], u - 3)
                        mat_to_T(bank(QK_BANK[u % 4], 128, GROUPS[g][1] * P), w[which], a_T, m, g).then_inc(
                            S["a_mm"], 1)
                    for t in range(NT):
                        if t >= 2:
                            pe.wait_ge(S["v_f"], t - 1)
                        mat_to_rows(bank(2 + t % 2, P), w[2], a_T, t).then_inc(S["v_mm"], 1)
                    pe.wait_ge(S["a_lo"], len(qk_units))
                    pe.wait_ge(S["v_f"], NT)
                    score(0)
                    score(1)
                    for n in range(NS):
                        if n + 2 < NS:
                            score(n + 2)
                        prob_T(n)
                        if n == 0:
                            pe.wait_ge(S["v_lo"], NT)
                        if n in av_after:
                            times_v(av_after[n])
                    times_v(2 * H - 1)
                    pe.wait_ge(S["s_max"], NS)
                    lag = GROUPS[0][1]
                    for t in range(NT + lag):
                        if t < NT:
                            pe.wait_ge(S["o_lo"], H if t < 3 else 2 * H)
                            if t >= 2:
                                pe.wait_ge(S["res1"], t - 1)
                            mat_to_rows(bank(t % 2, P), w[3], a_T, t).then_inc(S["res1_mm"], 1)
                            if t == 0:
                                pe.wait_ge(S["pt_lo"], NS)
                            if t >= 4:
                                pe.wait_ge(S["mod2"], t - 3)
                            mod_rows(t, 2, base2)
                        if t >= lag:
                            if t == lag:
                                pe.wait_ge(S["o_f"], 2 * H)
                            transposed(t - lag, 2, 6)
                    for u, (g, m) in enumerate(units8):
                        pe.wait_ge(S["yt_lo2"], 3 if g == 0 else NT)
                        if u < 4:
                            pe.wait_ge(S["res1"], NT)
                            pe.wait_ge(S["mod2"], NT)
                        else:
                            pe.wait_ge(S["c_f"], u - 3)
                        if u == 0:
                            pe.wait_ge(S["w_lo4"], 1)
                        mat_to_T(bank(C_BANK[u % 4], 128, GROUPS[g][1] * P), w[4], b_T, m, g).then_inc(S["c_mm"], 1)
                    pe.wait_ge(S["w_lo5"], 1)
                    pe.wait_ge(S["mod2"], NT)
                    for t in range(NT):
                        pe.wait_ge(S["c_lo"], 4 if t < 3 else 8)
                        if t >= 2:
                            pe.wait_ge(S["res2"], t - 1)
                        mat_to_rows(bank(2 + t % 2, P), w[5], q_T, t).then_inc(S["res2_mm"], 1)

                @block.scalar
                def _(act):
                    A_ = nc.scalar.activation
                    for t in range(NT):
                        act.wait_ge(S["yt_mm1"], t + 1)
                        A_(a_T[:, 0, :, span(t)], tr_bank(4 + t % 2), ACT.Copy, scale=1 / WSCALE).then_inc(S["yt_hi1"], 1)
                    split_hi_now(4, 0)
                    split_hi_now(5, 1)
                    act.wait_ge(S["small_lo"], 1)
                    for u, (g, which, m) in enumerate(qk_units):
                        evac_T(act, "a", u, (q_T, k_T)[which], bank(QK_BANK[u % 4], 128, GROUPS[g][1] * P), m, cols(g),
                               ACT.Identity, scale=(SCORE if which == 0 else 1.0) / WSCALE,
                               bias=bias_col[:, which, m:m + 1],
                               slot_free=(S["a_lo"], u - 3) if u >= 4 else None)
                    for t in range(NT):
                        act.wait_ge(S["v_f"], t + 1)
                        A_(v_p[:, 0, t, :], y[:, t, :], ACT.Copy).then_inc(S["v_hi"], 1)
                    def prob_hi(n):
                        g, h, i = s_units[n]
                        act.wait_ge(S["pt_mm"], n + 1)
                        gh = g * H + h
                        if gh >= 2 and i == 0:
                            act.wait_ge(S["o_mm"], gh - 1)
                        A_(p_T[:, gh % 2, 0, :, span(i)], blocks(4, P), ACT.Copy).then_inc(S["pt_hi"], 1)

                    def out_f(gh):
                        g, h = heads[gh]
                        evac_T(act, "o", gh, a_T, bank(6 + gh % 2, 128, GROUPS[g][1] * P), h, cols(g), ACT.Copy,
                               scale=1 / PSCALE, slot_free=(S["o_lo"], gh - 3) if gh >= 4 else
                               (S["a_lo"], len(qk_units)))

                    for n in range(NS):
                        act.wait_ge(S["s_max"], n + 1)
                        A_(rows_s[:, n % 3, :], rows_s[:, n % 3, :], ACT.Exp, scale=-1.0, bias=soft[:, n % 3, 1:2],
                           accum_out=soft[:, n % 3, 2:3]).then_inc(S["s_exp"], 1)
                        if n:
                            prob_hi(n - 1)
                        if n in o_after:
                            out_f(o_after[n])
                    prob_hi(NS - 1)
                    for gh in range(2 * H):
                        if last_of[gh] + 3 >= NS:
                            out_f(gh)
                    for t in range(NT):
                        act.wait_ge(S["yt_mm2"], t + 1)
                        A_(b_T[:, 0, :, span(t)], tr_bank(6 + t % 2), ACT.Copy, scale=1 / WSCALE).then_inc(S["yt_hi2"], 1)
                    for u, (g, m) in enumerate(units8):
                        evac_T(act, "c", u, q_T, bank(C_BANK[u % 4], 128, GROUPS[g][1] * P), m, cols(g), ACT.Relu,
                               scale=1 / WSCALE, bias=bias_col[:, 2, m:m + 1],
                               slot_free=(S["c_lo"], u - 3) if u >= 4 else (S["o_lo"], 2 * H))
                        if u == 3:
                            act.wait_ge(S["res1_mm"], NT)
                        if u in (3, 5, 7):
                            split_hi(*NEXT[(u - 3) // 2])
                    split_hi(*NEXT[3])
                    act.wait_ge(S["small_loaded"], 16)
                    act.wait_ge(S["mod_mm2"], NT)
                    mod_hi(act)

                @block.vector
                def _(dve):
                    V = nc.vector
                    chain = Chain(dve, S["chain_dve"])

                    def low_rows(t, j, b, dst):
                        dve.wait_ge(S[f"yt_hi{j}"], t + 1)
                        V.scalar_tensor_tensor(dst[:, 1, :, span(t)], tr_bank(b + t % 2), 1 / WSCALE,
                                               dst[:, 0, :, span(t)], ALU.mult, ALU.subtract).then_inc(
                            S[f"yt_lo{j}"], 1)

                    for t in range(NT):
                        chain(row_stats(dve, chain, xg, t))
                    inv_std(dve, chain, 0, NT)
                    for t in range(NT):
                        norm(xg, t).then_inc(S["norm1"], 1)
                        dve.wait_ge(S["norm1"], t + 1)
                        modulate(dve, chain, t, 1, base1, S["mod1"])
                        if t:
                            low_rows(t - 1, 1, 4, a_T)
                    low_rows(NT - 1, 1, 4, a_T)
                    dve.wait_ge(S["bias_loaded"], 64)
                    V.tensor_scalar(bias_col[:, 0, :], bias_col[:, 0, :], SCORE, None, ALU.mult).then_inc(
                        S["small_lo"], 1)
                    split_lo(4, 0)
                    split_lo(5, 1)
                    for u, (g, which, m) in enumerate(qk_units):
                        low_T(dve, "a", u, (q_T, k_T)[which], m, cols(g))
                    for t in range(NT):
                        dve.wait_ge(S["v_mm"], t + 1)
                        V.scalar_tensor_tensor(y[:, t, :], bank(2 + t % 2, P), 1 / WSCALE, bias_row[:, 0, :],
                                               ALU.mult, ALU.add).then_inc(S["v_f"], 1)

                    def row_max(n):
                        g, h, i = s_units[n]
                        t = GROUPS[g][0] + i
                        dve.wait_ge(S["s_mm"], n + 1)
                        if n >= 3:
                            dve.wait_ge(S["pt_mm"], n - 2)
                        V.tensor_tensor_reduce(out=rows_s[:, n % 3, :], in0=pair(2 * (n % 2), P, T),
                                               in1=lnc[:, t, :], scale=-1.0, scalar=-FLOOR, op0=ALU.add,
                                               op1=ALU.min, accum_out=soft[:, n % 3, 1:2]).then_inc(S["s_max"], 1)

                    def normalise(n):
                        dve.wait_ge(S["s_exp"], n + 1)
                        chain(V.tensor_scalar(soft[:, n % 3, 2:3], soft[:, n % 3, 2:3], 1e-30, None, ALU.max))
                        chain(V.reciprocal(soft[:, n % 3, 3:4], soft[:, n % 3, 2:3]))
                        V.tensor_scalar(rows_s[:, n % 3, :], rows_s[:, n % 3, :], soft[:, n % 3, 3:4], PSCALE,
                                        ALU.mult, ALU.mult).then_inc(S["s_prob"], 1)

                    def prob_lo(n):
                        g, h, i = s_units[n]
                        gh = g * H + h
                        dve.wait_ge(S["pt_hi"], n + 1)
                        V.tensor_tensor(p_T[:, gh % 2, 1, :, span(i)], blocks(4, P), p_T[:, gh % 2, 0, :, span(i)],
                                        ALU.subtract).then_inc(S["pt_lo"], 1)

                    row_max(0)
                    row_max(1)
                    for n in range(NS):
                        normalise(n)
                        if n:
                            prob_lo(n - 1)
                        if n + 2 < NS:
                            row_max(n + 2)
                        if n in o_after:
                            gh = o_after[n]
                            low_T(dve, "o", gh, a_T, heads[gh][1], cols(heads[gh][0]))
                    prob_lo(NS - 1)
                    for gh in range(2 * H):
                        if last_of[gh] + 3 >= NS:
                            low_T(dve, "o", gh, a_T, heads[gh][1], cols(heads[gh][0]))
                    for first, count_ in GROUPS:
                        tiles_ = range(first, first + count_)
                        for t in tiles_:
                            dve.wait_ge(S["res1_mm"], t + 1)
                            dve.wait_ge(S["resb1"], t + 1)
                            V.scalar_tensor_tensor(xg[:, t, :], bank(t % 2, P), 1 / WSCALE, xg[:, t, :],
                                                   ALU.mult, ALU.add).then_inc(S["res1"], 1)
                            dve.wait_ge(S["res1"], t + 1)
                            chain(row_stats(dve, chain, xg, t))
                        inv_std(dve, chain, first, first + count_)
                        for t in tiles_:
                            norm(xg, t).then_inc(S["norm2"], 1)
                            dve.wait_ge(S["norm2"], t + 1)
                            modulate(dve, chain, t, 2, base2, S["mod2"])
                            if t > first:
                                low_rows(t - 1, 2, 6, b_T)
                        low_rows(first + count_ - 1, 2, 6, b_T)
                    for u, (g, m) in enumerate(units8):
                        low_T(dve, "c", u, q_T, m, cols(g))
                        if u in (3, 5, 7):
                            split_lo(*NEXT[(u - 3) // 2])
                    for t in range(NT):
                        if t == 2:
                            split_lo(*NEXT[3])
                            mod_lo(dve)
                        dve.wait_ge(S["res2_mm"], t + 1)
                        dve.wait_ge(S["resb2"], t + 1)
                        V.scalar_tensor_tensor(xg[:, t, :], bank(2 + t % 2, P), 1 / WSCALE, xg[:, t, :],
                                               ALU.mult, ALU.add).then_inc(S["res2"], 1)
            clear_all()
        net.close()

        with nc.Block() as block:
            @block.vector
            def _(dve):
                for t in range(NT):
                    nc.vector.tensor_tensor(x[:, t, :], x[:, t, :], xg[:, t, :], ALU.add).then_inc(S["res1"], 1)
        clear_all()
        experts(A["L1_ffn_Ws"], A["L1_ffn_bs"], A["L1_ffn_W1"], A["L1_ffn_b1"], A["L1_ffn_W2"], A["L1_ffn_b2"],
                top=1, cap=0, i1=0, i2=1, last=True)


def layout(inputs):
    import numpy as np

    a = {k: np.asarray(v) for k, v in inputs.items()}

    def tiles(m):
        *lead, rows, n = m.shape
        return np.ascontiguousarray(np.moveaxis(m.reshape(*lead, rows // 128, 128, n), -2, -3))

    def columns(v):
        return np.ascontiguousarray(np.swapaxes(v.reshape(*v.shape[:-1], -1, 128), -1, -2))

    out = {k: a[k] for k in ("x", "src", "dst", "L0_gnn_b2", "L0_ffn_br", "L0_ffn_b2", "L1_ffn_bs", "L1_ffn_b2",
                             "L1_gnn_bv", "L1_gnn_bo", "L1_gnn_m_b2", "L1_gnn_f_w1")}
    out["noise"] = a["node_vec1"].reshape(-1)
    for k in ("L0_gnn_W1", "L0_gnn_W2", "L0_ffn_Wr", "L1_ffn_Ws", "L1_gnn_wq", "L1_gnn_wk", "L1_gnn_wv",
              "L1_gnn_wo", "L1_gnn_m_w1", "L1_gnn_m_w2"):
        out[k] = tiles(a[k])
    out["L0_gnn_b1"] = columns(a["L0_gnn_b1"])
    out["L1_gnn_cols"] = np.ascontiguousarray(
        np.stack([columns(a["L1_gnn_" + k]) for k in ("bq", "bk", "m_b1")], axis=2))
    for k in ("L0_ffn_", "L1_ffn_"):
        w1, w2 = a[k + "W1"], a[k + "W2"]
        out[k + "W1"] = tiles(np.moveaxis(w1, 0, 1).reshape(w1.shape[1], -1))
        out[k + "b1"] = a[k + "b1"].reshape(-1)
        out[k + "W2"] = tiles(w2.reshape(-1, w2.shape[-1]))
    nl, c, d = a["L1_gnn_s1_w"].shape
    mod = np.zeros((nl, 81, 4, d), np.float32)
    for j, k in enumerate(("s1", "b1", "s2", "b2")):
        for at in (0, 32, 64):
            mod[:, at:at + c, j] = a[f"L1_gnn_{k}_w"]
            if at != 32:
                mod[:, at + c, j] = a[f"L1_gnn_{k}_b"]
    out["mod"] = mod
    f_w2 = np.zeros((c, 81), np.float32)
    f_b = np.zeros((81, 2), np.float32)
    for at in (0, 32, 64):
        f_w2[:, at:at + c] = a["L1_gnn_f_w2"]
        f_b[at:at + c, 0] = a["L1_gnn_f_b2"]
        if at != 32:
            f_b[at + c, 0] = 1.0
    f_b[0:c, 1] = a["L1_gnn_f_b1"]
    out["f_w2"], out["f_b"] = f_w2, f_b
    return out


def kernel(**inputs):
    import numpy as np
    import concourse.bacc as bacc
    from concourse.bass_utils import run_bass_kernel_spmd

    nc = bacc.Bacc("TRN2", target_bir_lowering=False, num_devices=1)
    arrays, args = {}, {}
    for name, a in layout(inputs).items():
        a = np.ascontiguousarray(a)
        arrays[f"in_{name}_dram"] = a
        args[name] = nc.dram_tensor(f"in_{name}_dram", a.shape, mybir.dt.from_np(a.dtype),
                                    kind="ExternalInput").ap()
    shape = inputs["x"].shape
    out = nc.dram_tensor("out_0_dram", tuple(shape), F32, kind="ExternalOutput").ap()
    build(nc, args, out)
    r = run_bass_kernel_spmd(nc, [arrays], core_ids=[0])
    return r.results[0]["out_0_dram"]
```

```python
from contextlib import ExitStack, contextmanager

import concourse.bass as bass
from concourse import mybir

F32 = mybir.dt.float32
F16 = mybir.dt.float16
I32 = mybir.dt.int32
U32 = mybir.dt.uint32
ALU = mybir.AluOpType
ACT = mybir.ActivationFunctionType
AX_X = mybir.AxisListType.X

WSCALE = 64.0
PSCALE = 1024.0
PASSES = ((0, 0), (1, 0), (0, 1))
DIGIT = 4096
MASK_UNIT = 1.0e28
NO_EDGE = 1.0e-10
FLOOR = -1.0e20
RSQRT_MAGIC = 0x5F3759DF
EPS = 1e-5
TWO_PI_PARTS = (6.28125, 0.0019350051879882812, 3.019916050561733e-07)
INV_TWO_PI = 0.15915494309189535
ROUND_MAGIC = 12582912.0
PI_SAFE = 3.1415925


class Chain:

    def __init__(self, engine, sem):
        self.engine, self.sem, self.n = engine, sem, 0

    def __call__(self, ins):
        self.n += 1
        ins.then_inc(self.sem, 1)
        self.engine.wait_ge(self.sem, self.n)


def build(nc, A, out):
    x_in = A["x"]
    T, D = x_in.shape
    P = 125
    NT = T // P
    K = D // 128
    E = A["L0_ffn_Wr"].shape[2]
    DFF = D // E
    NL = A["mod"].shape[0]
    C = A["f_w2"].shape[0]
    H = 4
    DH = D // H
    SCORE = float(DH) ** -0.5
    NE = A["src"].shape[0]
    NCH = NE // P
    assert T == NT * P and D == K * 128 and NE == NCH * P and E * DFF == D and DH == 128
    CAP = -(-5 * T * 2 // (4 * E))
    NF = A["L1_gnn_f_w1"].shape[0] // 2
    HALF = -(-T // 4) * 2
    GROUPS = [(0, 3), (3, 2)]
    SLOTS = 15
    GROUP = 2 * SLOTS
    LOOPS = NCH // GROUP
    REST = NCH - LOOPS * GROUP
    assert 0 < REST <= GROUP and REST % SLOTS == 0 and GROUP * P < DIGIT and GROUP * P * DIGIT < 2 ** 24

    SEMS = ("x_loaded idx_loaded const_made chain_dve chain_act chain_pool onehot_ready onehot_used "
            "count_mm count_copied count_split count_added count_done adj_hi adj_lo xn_hi xn_lo "
            "x_summed mod_scaled w_scaled0 w_scaled1 w_scaled2 w_scaled3 ln_f "
            "w_loaded0 w_loaded1 w_loaded2 w_loaded3 w_loaded4 w_loaded5 "
            "w_hi0 w_hi1 w_hi2 w_hi3 w_hi4 w_hi5 w_lo0 w_lo1 w_lo2 w_lo3 w_lo4 w_lo5 "
            "small_loaded small_hi small_lo mod_hi0 mod_hi1 mod_lo0 mod_lo1 bias_loaded "
            "norm1 norm2 mod_mm1 mod_mm2 mod1 mod2 yt_mm1 yt_mm2 yt_hi1 yt_hi2 yt_lo1 yt_lo2 "
            "a_mm a_f a_hi a_lo b_mm b_f b_hi b_lo c_mm c_f c_hi c_lo "
            "v_mm v_f v_hi v_lo o_mm o_f o_hi o_lo res1_mm res2_mm res1 res2 resb1 resb2 "
            "s_mm s_max s_exp s_inv s_prob0 s_prob1 pt_mm pt_hi pt_lo "
            "r_mm r_lg r_exp r_w wt_mm wt_parts pos_mm pos_done gm gelu_done hm_done "
            "s_x e_a e_b e_c e_d e_e stored").split()
    ctx = ExitStack()
    with ctx:
        S = {n: ctx.enter_context(nc.semaphore(n)) for n in SEMS}
        nums = [s.num for s in S.values()]
        assert nums == list(range(nums[0], nums[0] + len(nums)))

        def clear_all():
            nc.all_engine_barrier(sems_to_clear=range(nums[0], nums[0] + len(nums)))

        def sb(name, shape, dt=F32):
            return ctx.enter_context(nc.sbuf_tensor(name, shape, dt))

        ps = ctx.enter_context(nc.psum_tensor("ps", [128, 8, 512], F32))

        def bank(b, p=128, n=512):
            return ps[0:p, b, 0:n]

        def pair(b, p, n):
            return ps[0:p, b:b + 2, :].rearrange("p b n -> p (b n)")[:, 0:n]

        def blocks(b, p):
            return pair(b, p, NT * 128).rearrange("p (t n) -> p t n", n=128)[:, :, 0:P]

        x = sb("x", [P, NT, D])
        xg = sb("xg", [P, NT, D])
        y = sb("y", [P, NT, D])
        stats = sb("stats", [P, NT, 16])
        ident = sb("ident", [128, 128])
        lnc = sb("lnc", [P, NT, T])
        stage = [sb(f"stage{i}", [128, K, D])[:, :, :] for i in range(3)]
        parts = sb("parts", [128, 6, 2, K, D], F16)
        w = [parts[:, i] for i in range(6)]
        bias_col = sb("bias_col", [128, 3, K])
        bias_row = sb("bias_row", [P, 3, D])
        a_T = sb("a_T", [128, 2, K, T], F16)
        b_T = sb("b_T", [128, 2, K, T], F16)
        fbuf = sb("fbuf", [128, 4, 375])
        cond = sb("cond", [81, T], F16)

        def row_stats(dve, chain, src, t):
            chain(nc.vector.bn_stats(stats[:, t, 2:8], src[:, t, :]))
            return nc.vector.bn_aggr(stats[:, t, 0:2], stats[:, t, 2:8])

        def inv_std(dve, chain, t0, t1):
            V = nc.vector
            ve, r, q, h = (stats[:, t0:t1, i] for i in range(8, 12))
            chain(V.tensor_scalar(ve, stats[:, t0:t1, 1], EPS, None, ALU.add))
            chain(V.tensor_scalar(q.bitcast(I32), ve.bitcast(I32), 1, None, ALU.logical_shift_right))
            chain(V.tensor_scalar(r.bitcast(I32), q.bitcast(I32), -1.0, float(RSQRT_MAGIC), ALU.mult, ALU.add))
            chain(V.tensor_tensor(q, r, r, ALU.mult))
            chain(V.tensor_tensor(q, q, ve, ALU.mult))
            chain(V.scalar_tensor_tensor(r, q, 3.0, r, ALU.subtract, ALU.mult))
            chain(V.tensor_tensor(q, r, r, ALU.mult))
            chain(V.tensor_tensor(q, q, ve, ALU.mult))
            chain(V.scalar_tensor_tensor(h, q, 4 * 10 / 3, q, ALU.subtract, ALU.mult))
            chain(V.tensor_scalar(h, h, -0.5 * 3 / 8 / 16, -0.5 * 15 / 8, ALU.mult, ALU.add))
            chain(V.tensor_tensor(r, r, h, ALU.mult))

        def norm(src, t, dst=None):
            return nc.vector.tensor_scalar((y if dst is None else dst)[:, t, :], src[:, t, :], stats[:, t, 0:1],
                                           stats[:, t, 9:10], ALU.subtract, ALU.mult)

        def cols(g):
            return slice(GROUPS[g][0] * P, (GROUPS[g][0] + GROUPS[g][1]) * P)

        def span(t):
            return slice(t * P, (t + 1) * P)

        def mat_to_T(dst, weights, act, m, g):
            n = len(PASSES) * K
            for i in range(n):
                (wp, ap), k = PASSES[i // K], i % K
                ins = nc.tensor.matmul(dst, weights[:, wp, k, m * 128:(m + 1) * 128], act[:, ap, k, cols(g)],
                                       start=i == 0, stop=i == n - 1)
            return ins

        def mat_to_rows(dst, weights, act, t, last=True):
            n = len(PASSES) * K
            for i in range(n):
                (ap, wp), k = PASSES[i // K], i % K
                ins = nc.tensor.matmul(dst, act[:, ap, k, span(t)], weights[:, wp, k, :],
                                       start=i == 0, stop=last and i == n - 1)
            return ins

        def load_w(eng, i, src, stg):
            eng.dma_start(stage[stg], src).then_inc(S[f"w_loaded{i}"], 16)

        def split_hi(i, stg):
            nc.scalar.wait_ge(S[f"w_loaded{i}"], 16)
            split_hi_now(i, stg)

        def split_hi_now(i, stg):
            nc.scalar.activation(w[i][:, 0], stage[stg], ACT.Copy, scale=WSCALE).then_inc(S[f"w_hi{i}"], 1)

        def split_hi_scaled(act, i, stg):
            act.wait_ge(S[f"w_loaded{i}"], 16)
            nc.scalar.activation(stage[stg], stage[stg], ACT.Copy, scale=WSCALE).then_inc(S[f"w_scaled{i}"], 1)
            act.wait_ge(S[f"w_scaled{i}"], 1)
            nc.scalar.activation(w[i][:, 0], stage[stg], ACT.Copy).then_inc(S[f"w_hi{i}"], 1)

        def split_lo_scaled(pool, i, stg):
            pool.wait_ge(S[f"w_hi{i}"], 1)
            nc.gpsimd.tensor_tensor(w[i][:, 1], stage[stg], w[i][:, 0], ALU.subtract).then_inc(S[f"w_lo{i}"], 1)

        def split_lo(i, stg):
            nc.vector.wait_ge(S[f"w_hi{i}"], 1)
            nc.vector.scalar_tensor_tensor(w[i][:, 1], stage[stg], WSCALE, w[i][:, 0],
                                           ALU.mult, ALU.subtract).then_inc(S[f"w_lo{i}"], 1)

        graph = ExitStack()

        def gsb(name, shape, dt=F32):
            return graph.enter_context(nc.sbuf_tensor(name, shape, dt))

        idx_i = gsb("idx_i", [P, 2, NCH], I32)
        src_f = gsb("src_f", [P, NCH])
        dst_f = gsb("dst_f", [P, NCH])
        dst_hi = gsb("dst_hi", [P, NCH])
        dst_w = gsb("dst_w", [P, NCH])
        iota_i = gsb("iota_i", [P, T], I32)
        iota = gsb("iota", [P, T], F16)
        hot_s = gsb("hot_s", [P, SLOTS, T + 1], F16)
        hot_d = gsb("hot_d", [P, SLOTS, HALF], F16)
        ident_h = gsb("ident_h", [P, P], F16)
        no_edge = gsb("no_edge", [P, 1])
        free_w = parts[:, 2:6].rearrange("p s h k n -> p (s h k n)").bitcast(I32)
        copied = free_w[0:P, 0:NT * HALF].rearrange("p (t n) -> p t n", t=NT)
        count = free_w[0:P, 2 * K * D:2 * K * D + NT * 2 * HALF].rearrange("p (t n) -> p t n", t=NT)
        digits = gsb("digits", [P, NT, 2, HALF], I32)
        adj = gsb("adj", [P, 2, NT, T], F16)
        xn = xg[:, :, :].rearrange("p t d -> p (t d)").bitcast(F16).rearrange("p (a t d) -> p a t d", a=2, t=NT)


        def evac_T(act, s, u, dst, src, m, where, func, scale=1.0, bias=None, slot_free=None):
            n = where.stop - where.start
            act.wait_ge(S[s + "_mm"], u + 1)
            if slot_free is not None:
                act.wait_ge(*slot_free)
            f = fbuf[:, u % 4, 0:n]
            if bias is None:
                nc.scalar.activation(f, src, func, scale=scale).then_inc(S[s + "_f"], 1)
            else:
                nc.scalar.activation(f, src, func, scale=scale, bias=bias).then_inc(S[s + "_f"], 1)
            act.wait_ge(S[s + "_f"], u + 1)
            nc.scalar.activation(dst[:, 0, m, where], f, ACT.Copy).then_inc(S[s + "_hi"], 1)

        def low_T(dve, s, u, dst, m, where):
            n = where.stop - where.start
            dve.wait_ge(S[s + "_hi"], u + 1)
            nc.vector.tensor_tensor(dst[:, 1, m, where], fbuf[:, u % 4, 0:n], dst[:, 0, m, where],
                                    ALU.subtract).then_inc(S[s + "_lo"], 1)

        def tr_bank(b):
            return ps[:, b, 0:K * P].rearrange("p (k n) -> p k n", k=K)

        def transpose_rows(pe, b, src, sem):
            for k in range(K):
                ins = nc.tensor.transpose(ps[:, b, k * P:(k + 1) * P], src[:, k * 128:(k + 1) * 128],
                                          ident[0:P, 0:P])
            ins.then_inc(sem, 1)

        units8 = [(g, m) for g in range(2) for m in range(K)]
        halves = ((0, 512), (512, T))

        hot_flat = hot_s[:, :, :].rearrange("p s n -> p (s n)").bitcast(F32)

        places = [0]

        def scratch(p, n):
            places.append(places[-1] + n)
            return hot_flat[0:p, places[-2]:places[-1]]

        phase, turns, noise = (scratch(2 * NF, T) for _ in range(3))
        cond_f, e1_f = scratch(81, T), scratch(C, T)
        f_w1f, f_w2f, f_b, freq = scratch(2 * NF, C), scratch(C, 81), scratch(81, 2), scratch(2 * NF, 4)
        emb = scratch(2 * NF, T).bitcast(F16).rearrange("p (a n) -> p a n", a=2)
        e1 = scratch(C, T).bitcast(F16).rearrange("p (a n) -> p a n", a=2)
        f_w1 = scratch(2 * NF, C).bitcast(F16).rearrange("p (a n) -> p a n", a=2)
        f_w2 = scratch(C, 81).bitcast(F16).rearrange("p (a n) -> p a n", a=2)
        freq_i = stats[0:2 * NF, NT - 1, 12:13].bitcast(I32)

        with nc.Block() as block:
            @block.sync
            def _(sp):
                sp.dma_start(idx_i[:, 0, :], A["src"].rearrange("(p c) -> p c", p=P)).then_inc(S["idx_loaded"], 16)
                sp.dma_start(idx_i[:, 1, :], A["dst"].rearrange("(p c) -> p c", p=P)).then_inc(S["idx_loaded"], 16)
                sp.dma_start(x[:, :, :], x_in.rearrange("(t p) d -> p t d", p=P)).then_inc(S["x_loaded"], 16)
                for i, n in enumerate(("L0_gnn_W1", "L0_gnn_W2")):
                    load_w(sp, i, A[n], i)
                sp.dma_start(bias_col[:, 0, :], A["L0_gnn_b1"]).then_inc(S["bias_loaded"], 16)
                sp.dma_start(bias_row[:, 0, :], A["L0_gnn_b2"].partition_broadcast(P)).then_inc(
                    S["bias_loaded"], 16)
                load_w(sp, 2, A["L0_ffn_W1"], 2)
                sp.wait_ge(S["w_lo0"], 1)
                load_w(sp, 3, A["L0_ffn_W2"], 0)
                sp.wait_ge(S["onehot_used"], SLOTS + NCH)
                for dst, src in ((noise, A["noise"].partition_broadcast(2 * NF)), (f_w1f, A["L1_gnn_f_w1"]),
                                 (f_w2f, A["f_w2"]), (f_b, A["f_b"])):
                    sp.dma_start(dst, src).then_inc(S["small_loaded"], 16)
                sp.wait_ge(S["small_loaded"], 64)

            @block.gpsimd
            def _(pool):
                TT = nc.gpsimd.tensor_tensor
                chain = Chain(pool, S["chain_pool"])
                nc.gpsimd.iota(iota_i[:, :], [[1, T]], base=0, channel_multiplier=0).then_inc(S["const_made"], 1)
                nc.gpsimd.memset(no_edge[:, :], NO_EDGE)
                nc.gpsimd.iota(freq_i, [[1, 1]], base=1, channel_multiplier=1)
                chain(nc.gpsimd.memset(ident[:, :], 0.0))
                nc.gpsimd.affine_select(out=ident[:, :], in_=ident[:, :], compare_op=ALU.not_equal, fill=1.0,
                                        base=0, pattern=[[-1, 128]], channel_multiplier=1).then_inc(S["const_made"], 1)
                chain(nc.gpsimd.memset(count[:, :, :], 0))
                pool.sem_inc(S["count_added"], NT)
                for i in range(2):
                    split_lo_scaled(pool, i, i)
                for t in range(NT):
                    pool.wait_ge(S["xn_hi"], t + 1)
                    TT(xn[:, 1, t, :], y[:, t, :], xn[:, 0, t, :], ALU.subtract).then_inc(S["xn_lo"], 1)
                with pool.Fori(0, LOOPS) as g:
                    for t in range(NT):
                        pool.wait_ge(S["count_split"], g * NT + (t + 1))
                        TT(count[:, t, :], count[:, t, :], digits[:, t, :, :].rearrange("p a n -> p (a n)"),
                           ALU.add).then_inc(S["count_added"], 1)
                pool.wait_ge(S["bias_loaded"], 32)
                for t in range(NT):
                    TT(x[:, t, :], x[:, t, :], bias_row[:, 0, :], ALU.add).then_inc(S["resb1"], 1)

            @block.scalar
            def _(act):
                A_ = nc.scalar.activation

                def copy_counts(g, t, chunks):
                    if t < NT - 1:
                        act.wait_ge(S["count_mm"], g * (NT - 1) + (t + 1))
                    else:
                        act.wait_ge(S["onehot_used"], chunks + SLOTS)
                    A_(copied[:, t, :], bank(t, P, HALF), ACT.Copy).then_inc(S["count_copied"], 1)

                for i in range(2):
                    split_hi_scaled(act, i, i)
                for t in range(NT):
                    copy_counts(0, t, GROUP)
                for t in range(NT):
                    act.wait_ge(S["norm1"], t + 1)
                    A_(xn[:, 0, t, :], y[:, t, :], ACT.Copy).then_inc(S["xn_hi"], 1)
                with act.Fori(1, LOOPS) as g:
                    for t in range(NT):
                        act.wait_ge(S["count_split"], (g - 1) * NT + (t + 1))
                        copy_counts(g, t, g * GROUP + GROUP)
                for t in range(NT):
                    act.wait_ge(S["count_split"], (LOOPS - 1) * NT + t + 1)
                    copy_counts(LOOPS, t, NCH)
                for t in range(NT):
                    act.wait_ge(S["count_done"], t + 1)
                    A_(adj[:, 0, t, :], count[:, t, 0:T], ACT.Copy).then_inc(S["adj_hi"], 1)
                act.wait_ge(S["count_done"], NT)
                split_hi(3, 0)
                split_hi(2, 2)
                for u, (g, m) in enumerate(units8):
                    act.wait_ge(S["a_mm"], u + 1)
                    A_(a_T[:, 0, m, cols(g)], bank(u, 128, GROUPS[g][1] * P), ACT.Copy).then_inc(S["a_hi"], 1)
                act.wait_ge(S["e_a"], 1)
                A_(phase, phase, ACT.Sin).then_inc(S["e_b"], 1)
                act.wait_ge(S["bias_loaded"], 32)
                for u, (g, m) in enumerate(units8):
                    evac_T(act, "b", u, b_T, bank(u, 128, GROUPS[g][1] * P), m, cols(g), ACT.Relu,
                           scale=1 / WSCALE, bias=bias_col[:, 0, m:m + 1],
                           slot_free=(S["b_lo"], u - 3) if u >= 4 else None)
                act.wait_ge(S["e_e"], 1)
                A_(e1_f, pair(6, C, T), ACT.Silu, scale=1 / WSCALE, bias=f_b[0:C, 1:2]).then_inc(S["e_d"], 1)
                act.wait_ge(S["e_e"], 2)
                A_(cond_f, pair(6, 81, T), ACT.Identity, scale=1 / WSCALE, bias=f_b[:, 0:1]).then_inc(S["e_d"], 1)
                for t in range(NT):
                    A_(lnc[:, t, :], count[:, t, 0:T], ACT.Ln, scale=2.0, bias=no_edge[:, :]).then_inc(
                        S["ln_f"], 1)

            @block.vector
            def _(dve):
                V = nc.vector
                chain = Chain(dve, S["chain_dve"])
                dve.wait_ge(S["idx_loaded"], 32)
                V.tensor_copy(src_f[:, :], idx_i[:, 0, :])
                chain(V.tensor_copy(dst_f[:, :], idx_i[:, 1, :]))
                chain(V.tensor_scalar(dst_hi[:, :], dst_f[:, :], float(HALF), None, ALU.is_ge))
                chain(V.tensor_scalar(dst_w[:, :], dst_hi[:, :], float(DIGIT - 1), 1.0, ALU.mult, ALU.add))
                chain(V.scalar_tensor_tensor(dst_f[:, :], dst_hi[:, :], -float(HALF), dst_f[:, :],
                                             ALU.mult, ALU.add))
                dve.wait_ge(S["const_made"], 1)
                chain(V.tensor_copy(iota[:, :], iota_i[:, :]))

                def one_hot(c, slot):
                    dve.wait_ge(S["onehot_used"], c + 1)
                    if not isinstance(c, int):
                        c = dve.snap(c)
                    V.tensor_scalar(hot_s[:, slot, 0:T], iota[:, :], src_f[:, bass.ds(c, 1)], None, ALU.is_equal)
                    V.tensor_scalar(hot_d[:, slot, :], iota[:, 0:HALF], dst_f[:, bass.ds(c, 1)],
                                    dst_w[:, bass.ds(c, 1)], ALU.is_equal, ALU.mult).then_inc(S["onehot_ready"], 1)

                def unpack(g, t):
                    dve.wait_ge(S["count_copied"], g * NT + (t + 1))
                    dve.wait_ge(S["count_added"], g * NT + (t + 1))
                    V.tensor_scalar(digits[:, t, 0, :], copied[:, t, :], DIGIT - 1, None, ALU.bitwise_and)
                    return V.tensor_scalar(digits[:, t, 1, :], copied[:, t, :], DIGIT.bit_length() - 1,
                                           None, ALU.logical_shift_right)

                for c in range(GROUP):
                    one_hot(c, c % SLOTS)
                    t = (c - SLOTS + 2) // 2
                    if c == SLOTS - 2:
                        dve.wait_ge(S["x_loaded"], 16)
                    if c >= SLOTS - 2 and c % 2 and t < NT:
                        chain(row_stats(dve, chain, x, t))
                inv_std(dve, chain, 0, NT)
                for t in range(NT):
                    norm(x, t).then_inc(S["norm1"], 1)
                with dve.Fori(1, LOOPS) as g:
                    for j in range(GROUP):
                        one_hot(g * GROUP + j, j % SLOTS)
                        if j % 6 == 5:
                            unpack(g - 1, j // 6).then_inc(S["count_split"], 1)
                for j in range(REST):
                    one_hot(LOOPS * GROUP + j, j % SLOTS)
                    if j % 3 == 2:
                        unpack(LOOPS - 1, j // 3).then_inc(S["count_split"], 1)
                dve.wait_ge(S["const_made"], 2)
                V.tensor_copy(ident_h[:, :], ident[0:P, 0:P]).then_inc(S["const_made"], 1)
                def low_counts(t):
                    dve.wait_ge(S["adj_hi"], t + 1)
                    V.tensor_tensor(adj[:, 1, t, :], count[:, t, 0:T], adj[:, 0, t, :], ALU.subtract).then_inc(
                        S["adj_lo"], 1)

                for t in range(NT):
                    chain(unpack(LOOPS, t))
                    V.tensor_tensor(count[:, t, :], count[:, t, :],
                                    digits[:, t, :, :].rearrange("p a n -> p (a n)"), ALU.add).then_inc(
                        S["count_done"], 1)
                    if t:
                        low_counts(t - 1)
                low_counts(NT - 1)
                split_lo(3, 0)
                split_lo(2, 2)
                k, is_cos, shift, f = (freq[:, i:i + 1] for i in range(4))
                chain(V.tensor_copy(k, freq_i))
                chain(V.tensor_scalar(is_cos, k, float(NF), None, ALU.is_gt))
                chain(V.scalar_tensor_tensor(k, is_cos, -float(NF), k, ALU.mult, ALU.add))
                chain(V.tensor_scalar(shift, is_cos, 1.5707963267948966, None, ALU.mult))
                chain(V.tensor_scalar(f, k, 0.39269908169872414, None, ALU.mult))
                dve.wait_ge(S["small_loaded"], 64)
                chain(V.tensor_scalar(phase, noise, f, None, ALU.mult))
                chain(V.tensor_scalar(turns, phase, INV_TWO_PI, ROUND_MAGIC, ALU.mult, ALU.add))
                chain(V.tensor_scalar(turns, turns, ROUND_MAGIC, None, ALU.subtract))
                for part in TWO_PI_PARTS:
                    chain(V.scalar_tensor_tensor(phase, turns, -part, phase, ALU.mult, ALU.add))
                chain(V.tensor_scalar(phase, phase, shift, None, ALU.add))
                chain(V.tensor_scalar(turns, phase, 3.141592653589793, -6.283185307179586, ALU.is_gt, ALU.mult))
                chain(V.tensor_tensor(phase, phase, turns, ALU.add))
                V.tensor_scalar(phase, phase, PI_SAFE, -PI_SAFE, ALU.min, ALU.max).then_inc(S["e_a"], 1)
                for f_, p_ in ((f_w1f, f_w1), (f_w2f, f_w2)):
                    chain(V.tensor_scalar(f_[:, :], f_[:, :], WSCALE, None, ALU.mult))
                    chain(V.tensor_copy(p_[:, 0, :], f_[:, :]))
                    chain(V.tensor_tensor(p_[:, 1, :], f_[:, :], p_[:, 0, :], ALU.subtract))
                for u, (g, m) in enumerate(units8):
                    dve.wait_ge(S["a_hi"], u + 1)
                    V.tensor_tensor(a_T[:, 1, m, cols(g)], bank(u, 128, GROUPS[g][1] * P), a_T[:, 0, m, cols(g)],
                                    ALU.subtract).then_inc(S["a_lo"], 1)
                for u, (g, m) in enumerate(units8):
                    low_T(dve, "b", u, b_T, m, cols(g))
                    if u == 1:
                        dve.wait_ge(S["e_b"], 1)
                        chain(V.tensor_copy(emb[:, 0, :], phase))
                        V.tensor_tensor(emb[:, 1, :], phase, emb[:, 0, :], ALU.subtract).then_inc(S["e_c"], 1)
                dve.wait_ge(S["e_d"], 1)
                chain(V.tensor_copy(e1[:, 0, :], e1_f))
                V.tensor_tensor(e1[:, 1, :], e1_f, e1[:, 0, :], ALU.subtract).then_inc(S["e_c"], 1)

                for t in range(NT):
                    dve.wait_ge(S["res1_mm"], t + 1)
                    dve.wait_ge(S["resb1"], t + 1)
                    V.scalar_tensor_tensor(x[:, t, :], bank(t % 4, P), 1 / WSCALE, x[:, t, :],
                                           ALU.mult, ALU.add).then_inc(S["res1"], 1)
                    dve.wait_ge(S["res1"], t + 1)
                    chain(row_stats(dve, chain, x, t))
                    if t == 2:
                        dve.wait_ge(S["e_d"], 2)
                        chain(V.tensor_copy(cond[:, :], cond_f))
                        V.tensor_tensor(cond[32:32 + C, :], cond_f[32:32 + C, :], cond[32:32 + C, :], ALU.subtract)

            @block.tensor
            def _(pe):
                pe.sem_inc(S["onehot_used"], SLOTS)

                def add_chunk(c, slot, first, last, g):
                    pe.wait_ge(S["onehot_ready"], c + 1)
                    for t in range(NT):
                        if first and not isinstance(g, int) or first and g:
                            pe.wait_ge(S["count_copied"], (g - 1) * NT + (t + 1))
                        ins = nc.tensor.matmul(bank(t, P, HALF), hot_s[:, slot, span(t)], hot_d[:, slot, :],
                                               start=first, stop=last)
                        if last and t < NT - 1:
                            ins.then_inc(S["count_mm"], 1)
                    ins.then_inc(S["onehot_used"], 1)

                for c in range(GROUP):
                    add_chunk(c, c % SLOTS, c == 0, c == GROUP - 1, 0)
                with pe.Fori(1, LOOPS) as g:
                    for j in range(GROUP):
                        add_chunk(g * GROUP + j, j % SLOTS, j == 0, j == GROUP - 1, g)
                for j in range(REST):
                    add_chunk(LOOPS * GROUP + j, j % SLOTS, j == 0, j == REST - 1, LOOPS)
                pe.wait_ge(S["xn_lo"], NT)
                pe.wait_ge(S["const_made"], 3)
                pe.wait_ge(S["count_copied"], (LOOPS + 1) * NT)
                for t in range(NT):
                    pe.wait_ge(S["adj_lo"], t + 1)
                    for u, (g, m) in enumerate(units8):
                        first, n = GROUPS[g]
                        for i, (ap, wp) in enumerate(PASSES):
                            ins = nc.tensor.matmul(bank(u, 128, n * P), xn[:, ap, t, m * 128:(m + 1) * 128],
                                                   adj[:, wp, t, cols(g)], start=t == 0 and i == 0,
                                                   stop=t == NT - 1 and i == len(PASSES) - 1, skip_group_check=True)
                            if i == 0 and first <= t < first + n:
                                for own in range(2):
                                    nc.tensor.matmul(ps[:, u, (t - first) * P:(t - first + 1) * P],
                                                     xn[:, own, t, m * 128:(m + 1) * 128], ident_h[:, :],
                                                     start=False, stop=False, skip_group_check=True)
                        if t == NT - 1:
                            ins.then_inc(S["a_mm"], 1)
                pe.wait_ge(S["w_lo0"], 1)
                for u, (g, m) in enumerate(units8):
                    pe.wait_ge(S["a_lo"], 4 * (g + 1))
                    mat_to_T(bank(u, 128, GROUPS[g][1] * P), w[0], a_T, m, g).then_inc(S["b_mm"], 1)
                pe.wait_ge(S["w_lo1"], 1)

                def condition_layer(weights, values, width):
                    for a, b in halves:
                        for i, (wp, ep) in enumerate(PASSES):
                            ins = nc.tensor.matmul(pair(6, width, T)[:, a:b], weights[:, wp, :], values[:, ep, a:b],
                                                   start=i == 0, stop=i == len(PASSES) - 1)
                    ins.then_inc(S["e_e"], 1)

                pe.wait_ge(S["e_c"], 1)
                pe.wait_ge(S["b_f"], 8)
                condition_layer(f_w1, emb, C)
                for t in range(NT):
                    pe.wait_ge(S["b_lo"], 4 if t < 3 else 8)
                    if t == 2:
                        pe.wait_ge(S["e_c"], 2)
                        condition_layer(f_w2, e1, 81)
                    if t >= 4:
                        pe.wait_ge(S["res1"], t - 3)
                    mat_to_rows(bank(t % 4, P), w[1], b_T, t).then_inc(S["res1_mm"], 1)
        clear_all()

        graph.close()

        def experts(Wr, br, W1, b1, W2, b2, top, cap, i1, i2, last):
            moe = ExitStack()

            def msb(name, shape, dt=F32):
                return moe.enter_context(nc.sbuf_tensor(name + ("a" if cap else "b"), shape, dt))

            wr_f = msb("wr_f", [128, K, E])
            wr = msb("wr", [128, K, 2, E], F16)
            br_row = msb("br_row", [P, E])
            b2_f = msb("b2_f", [E, D])
            b2_p = msb("b2_p", [E, 2, D], F16)
            prob = msb("prob", [P, NT, E])
            hot = msb("hot", [P, 3, NT, E])
            top_v = msb("top_v", [P, NT, 8])
            top_i = msb("top_i", [P, NT, 8], U32)
            top_f = msb("top_f", [P, NT, 8])
            one = msb("one", [P, 8, NT])
            sent = msb("sent", [P, NT, E], F16)
            before = msb("before", [P, 2, P], F16)
            iota_e = msb("iota_e", [P, E], I32)
            iota_f = msb("iota_f", [P, E])
            wt = msb("wt", [E, 2, T], F16)
            hid = msb("hid", [P, 2, D])

            GM_BANK = (6, 7, 2, 3, 6)

            def each(v):
                return v.unsqueeze(2).to_broadcast([P, NT, E])

            with nc.Block() as block:
                @block.sync
                def _(sp):
                    sp.dma_start(wr_f[:, :, :], Wr).then_inc(S["small_loaded"], 16)
                    sp.dma_start(br_row[:, :], br.partition_broadcast(P)).then_inc(S["small_loaded"], 16)
                    sp.dma_start(b2_f[:, :], b2).then_inc(S["small_loaded"], 16)
                    sp.dma_start(bias_row[:, 1, :], b1.partition_broadcast(P)).then_inc(
                        S["small_loaded"], 16)
                    if last:
                        load_w(sp, i1, W1, 0)
                        load_w(sp, i2, W2, 1)
                    else:
                        for i, n in enumerate(("wq", "wk", "wv")):
                            load_w(sp, i, A["L1_gnn_" + n][0], i)
                    if last:
                        for t in range(NT):
                            sp.wait_ge(S["res1"], t + 1)
                            sp.dma_start(out[span(t), :], x[:, t, :]).then_inc(S["stored"], 16)
                        sp.wait_ge(S["stored"], 16 * NT)

                @block.gpsimd
                def _(pool):
                    chain = Chain(pool, S["chain_pool"])
                    nc.gpsimd.iota(iota_e[:, :], [[1, E]], base=0, channel_multiplier=0).then_inc(S["const_made"], 1)
                    chain(nc.gpsimd.memset(before[:, :, :], 1.0))
                    nc.gpsimd.affine_select(out=before[:, 0, :], in_=before[:, 0, :], compare_op=ALU.is_gt,
                                            fill=0.0, base=0, pattern=[[1, P]], channel_multiplier=-1).then_inc(
                        S["const_made"], 1)
                    if last:
                        for t in range(3, NT):
                            nc.gpsimd.tensor_tensor(x[:, t, :], x[:, t, :], xg[:, t, :], ALU.add).then_inc(
                                S["x_summed"], 1)
                        for i, stg in ((i1, 0), (i2, 1)):
                            split_lo_scaled(pool, i, stg)
                    else:
                        for i in range(3):
                            split_lo_scaled(pool, i, i)

                @block.vector
                def _(dve):
                    V = nc.vector
                    chain = Chain(dve, S["chain_dve"])
                    if last:
                        for t in range(NT):
                            if t < 3:
                                chain(V.tensor_tensor(x[:, t, :], x[:, t, :], xg[:, t, :], ALU.add))
                            else:
                                dve.wait_ge(S["x_summed"], t - 2)
                            chain(row_stats(dve, chain, x, t))
                    inv_std(dve, chain, 0, NT)
                    norm(x, 0).then_inc(S["norm1"], 1)
                    norm(x, 1).then_inc(S["norm1"], 1)
                    dve.wait_ge(S["small_hi"], 2)
                    V.scalar_tensor_tensor(wr[:, :, 1, :], wr_f[:, :, :], WSCALE, wr[:, :, 0, :], ALU.mult, ALU.subtract)
                    V.scalar_tensor_tensor(b2_p[:, 1, :], b2_f[:, :], WSCALE, b2_p[:, 0, :], ALU.mult,
                                           ALU.subtract).then_inc(S["small_lo"], 1)
                    for t in range(NT):
                        dve.wait_ge(S["yt_hi1"], t + 1)
                        V.tensor_tensor(a_T[:, 1, :, span(t)], tr_bank(t % 2), a_T[:, 0, :, span(t)],
                                        ALU.subtract).then_inc(S["yt_lo1"], 1)
                        if t + 2 < NT:
                            norm(x, t + 2).then_inc(S["norm1"], 1)
                    if not last:
                        for t in range(NT):
                            V.scalar_tensor_tensor(lnc[:, t, :], lnc[:, t, :], MASK_UNIT, lnc[:, t, :],
                                                   ALU.mult, ALU.min)

                    def hidden_rows(t):
                        dve.wait_ge(S["gm"], t + 1)
                        if t >= 2:
                            dve.wait_ge(S["hm_done"], t - 1)
                        V.scalar_tensor_tensor(hid[:, t % 2, :], bank(GM_BANK[t], P), 1 / WSCALE, bias_row[:, 1, :],
                                               ALU.mult, ALU.add).then_inc(S["mod1"], 1)

                    dve.wait_ge(S["r_mm"], NT)
                    lg = ps[0:P, 4, 0:NT * 2 * E].rearrange("p (t a e) -> p a t e", a=2, e=E)
                    chain(V.scalar_tensor_tensor(prob[:, :, :], lg[:, 0], 1 / WSCALE,
                                                 br_row[:, :].unsqueeze(1).to_broadcast([P, NT, E]),
                                                 ALU.mult, ALU.add))
                    chain(V.scalar_tensor_tensor(prob[:, :, :], lg[:, 1], 1 / WSCALE, prob[:, :, :],
                                                 ALU.mult, ALU.add))
                    chain(V.reduce_max(one[:, 0, :], prob[:, :, :], AX_X))
                    V.tensor_tensor(prob[:, :, :], prob[:, :, :], each(one[:, 0, :]), ALU.subtract).then_inc(
                        S["r_lg"], 1)
                    dve.wait_ge(S["r_exp"], 1)
                    chain(V.reduce_sum(one[:, 1, :], prob[:, :, :], AX_X))
                    chain(V.reciprocal(one[:, 2, :], one[:, 1, :]))
                    chain(V.tensor_tensor(prob[:, :, :], prob[:, :, :], each(one[:, 2, :]), ALU.mult))
                    for t in range(NT):
                        chain(V.max(top_v[:, t, :], prob[:, t, :]))
                        chain(V.max_index(top_i[:, t, :], top_v[:, t, :], prob[:, t, :]))
                    chain(V.tensor_copy(top_f[:, :, :], top_i[:, :, :]))
                    dve.wait_ge(S["const_made"], 2)
                    chain(V.tensor_copy(iota_f[:, :], iota_e[:, :]))
                    for j in range(top):
                        chain(V.tensor_tensor(hot[:, j], iota_f[:, :].unsqueeze(1).to_broadcast([P, NT, E]),
                                              each(top_f[:, :, j]), ALU.is_equal))
                    gate = hot[:, 0]
                    if top == 1:
                        chain(V.tensor_tensor(gate, gate, each(top_v[:, :, 0]), ALU.mult))
                    else:
                        chain(V.tensor_tensor(hot[:, 2], hot[:, 0], hot[:, 1], ALU.add))
                        V.tensor_copy(sent[:, :, :], hot[:, 2]).then_inc(S["r_w"], 1)
                        chain(V.tensor_tensor(one[:, 3, :], top_v[:, :, 0], top_v[:, :, 1], ALU.add))
                        chain(V.tensor_scalar(one[:, 3, :], one[:, 3, :], 1e-9, None, ALU.add))
                        chain(V.reciprocal(one[:, 4, :], one[:, 3, :]))
                        for j in range(top):
                            chain(V.tensor_tensor(one[:, 5 + j, :], top_v[:, :, j], one[:, 4, :], ALU.mult))
                            chain(V.tensor_tensor(hot[:, j], hot[:, j], each(one[:, 5 + j, :]), ALU.mult))
                        chain(V.tensor_tensor(gate, hot[:, 0], hot[:, 1], ALU.add))
                        hidden_rows(0)
                        dve.wait_ge(S["pos_mm"], NT)
                        pos = ps[0:P, 5, 0:NT * E].rearrange("p (t e) -> p t e", e=E)
                        chain(V.tensor_scalar(hot[:, 2], pos, float(cap), None, ALU.is_lt))
                        chain(V.tensor_tensor(gate, gate, hot[:, 2], ALU.mult))
                        chain(V.reduce_sum(one[:, 1, :], gate, AX_X))
                        chain(V.tensor_scalar(one[:, 1, :], one[:, 1, :], 1e-9, None, ALU.add))
                        chain(V.reciprocal(one[:, 2, :], one[:, 1, :]))
                        chain(V.tensor_tensor(gate, gate, each(one[:, 2, :]), ALU.mult))
                    V.nop().then_inc(S["pos_done"], 1)
                    def gated(t):
                        dve.wait_ge(S["gelu_done"], t + 1)
                        V.tensor_tensor(y[:, t, :].rearrange("p (e f) -> p e f", e=E),
                                        hid[:, t % 2, :].rearrange("p (e f) -> p e f", e=E),
                                        gate[:, t, :].unsqueeze(2).to_broadcast([P, E, DFF]),
                                        ALU.mult).then_inc(S["hm_done"], 1)

                    if top == 1:
                        hidden_rows(0)
                    for t in range(NT - 2):
                        hidden_rows(t + 1)
                        gated(t)
                    dve.wait_ge(S["wt_mm"], 1)
                    wtp = blocks(4, E)
                    wt3 = wt[:, :, :].rearrange("e a (t n) -> e a t n", n=P)
                    chain(V.tensor_copy(wt3[:, 0], wtp))
                    V.tensor_tensor(wt3[:, 1], wtp, wt3[:, 0], ALU.subtract).then_inc(S["wt_parts"], 1)
                    gated(NT - 2)
                    hidden_rows(NT - 1)
                    gated(NT - 1)

                    def low_hidden(t):
                        dve.wait_ge(S["yt_hi2"], t + 1)
                        V.tensor_tensor(b_T[:, 1, :, span(t)], tr_bank(t % 2), b_T[:, 0, :, span(t)],
                                        ALU.subtract).then_inc(S["yt_lo2"], 1)

                    for t in range(3):
                        low_hidden(t)
                    for t in range(NT):
                        dve.wait_ge(S["res1_mm"], t + 1)
                        V.scalar_tensor_tensor(x[:, t, :], bank(2 + t % 2, P), 1 / WSCALE, x[:, t, :],
                                               ALU.mult, ALU.add).then_inc(S["res1"], 1)
                        if t + 3 < NT:
                            low_hidden(t + 3)
                        if not last:
                            dve.wait_ge(S["res1"], t + 1)
                            chain(row_stats(dve, chain, x, t))

                @block.scalar
                def _(act):
                    act.wait_ge(S["small_loaded"], 64)
                    nc.scalar.activation(wr[:, :, 0, :], wr_f[:, :, :], ACT.Copy, scale=WSCALE).then_inc(S["small_hi"], 1)
                    nc.scalar.activation(b2_p[:, 0, :], b2_f[:, :], ACT.Copy, scale=WSCALE).then_inc(S["small_hi"], 1)
                    if last:
                        split_hi_scaled(act, i1, 0)
                    for t in range(NT):
                        act.wait_ge(S["yt_mm1"], t + 1)
                        nc.scalar.activation(a_T[:, 0, :, span(t)], tr_bank(t % 2), ACT.Copy).then_inc(S["yt_hi1"], 1)
                    if last:
                        split_hi_scaled(act, i2, 1)
                    else:
                        split_hi_scaled(act, 0, 0)
                    act.wait_ge(S["r_lg"], 1)
                    nc.scalar.activation(prob[:, :, :], prob[:, :, :], ACT.Exp).then_inc(S["r_exp"], 1)
                    for t in range(NT):
                        act.wait_ge(S["mod1"], t + 1)
                        nc.scalar.activation(hid[:, t % 2, :], hid[:, t % 2, :], ACT.Gelu).then_inc(S["gelu_done"], 1)
                    for t in range(NT):
                        act.wait_ge(S["yt_mm2"], t + 1)
                        nc.scalar.activation(b_T[:, 0, :, span(t)], tr_bank(t % 2), ACT.Copy).then_inc(S["yt_hi2"], 1)
                        if not last and 2 <= t < NT - 1:
                            split_hi_scaled(act, t - 1, t - 1)

                @block.tensor
                def _(pe):
                    def rows_T(t):
                        pe.wait_ge(S["norm1"], t + 1)
                        if t >= 2:
                            pe.wait_ge(S["yt_lo1"], t - 1)
                        transpose_rows(pe, t % 2, y[:, t, :], S["yt_mm1"])

                    def router(t):
                        pe.wait_ge(S["yt_lo1"], t + 1)
                        at = t * 2 * E
                        for k in range(K):
                            nc.tensor.matmul(ps[0:P, 4, at:at + 2 * E], a_T[:, 0, k, span(t)],
                                             wr[:, k, :, :].rearrange("p a e -> p (a e)"), start=k == 0,
                                             stop=False, skip_group_check=True)
                        for k in range(K):
                            ins = nc.tensor.matmul(ps[0:P, 4, at:at + E], a_T[:, 1, k, span(t)], wr[:, k, 0, :],
                                                   start=False, stop=k == K - 1, skip_group_check=True)
                        ins.then_inc(S["r_mm"], 1)

                    rows_T(0)
                    rows_T(1)
                    pe.wait_ge(S["small_lo"], 1)
                    for t in range(NT):
                        router(t)
                        if t + 2 < NT:
                            rows_T(t + 2)
                    if last:
                        pe.wait_ge(S[f"w_lo{i1}"], 1)
                    for t in range(2):
                        mat_to_rows(bank(GM_BANK[t], P), w[i1], a_T, t).then_inc(S["gm"], 1)
                    if cap:
                        pe.wait_ge(S["const_made"], 2)
                        pe.wait_ge(S["r_w"], 1)
                        for t in range(NT):
                            for s in range(t + 1):
                                ins = nc.tensor.matmul(ps[0:P, 5, t * E:(t + 1) * E],
                                                       before[:, 0 if s == t else 1, :], sent[:, s, :],
                                                       start=s == 0, stop=s == t)
                            ins.then_inc(S["pos_mm"], 1)
                    for t in range(2, NT):
                        if t == 4:
                            pe.wait_ge(S["pos_done"], 1)
                            for s in range(NT):
                                ins = nc.tensor.transpose(blocks(4, E)[:, s, :], hot[:, 0, s, :], ident[0:P, 0:P])
                            ins.then_inc(S["wt_mm"], 1)
                            pe.wait_ge(S["mod1"], 1)
                        mat_to_rows(bank(GM_BANK[t], P), w[i1], a_T, t).then_inc(S["gm"], 1)

                    def hidden_T(t):
                        pe.wait_ge(S["hm_done"], t + 1)
                        if t >= 2:
                            pe.wait_ge(S["yt_lo2"], t - 1)
                        transpose_rows(pe, t % 2, y[:, t, :], S["yt_mm2"])

                    for t in range(3):
                        hidden_T(t)
                    pe.wait_ge(S["wt_parts"], 1)
                    if last:
                        pe.wait_ge(S[f"w_lo{i2}"], 1)
                    for t in range(NT):
                        pe.wait_ge(S["yt_lo2"], t + 1)
                        if t >= 2:
                            pe.wait_ge(S["res1"], t - 1)
                        mat_to_rows(bank(2 + t % 2, P), w[i2], b_T, t, last=False)
                        for i, (ap, wp) in enumerate(PASSES):
                            ins = nc.tensor.matmul(bank(2 + t % 2, P), wt[:, ap, span(t)], b2_p[:, wp, :],
                                                   start=False, stop=i == len(PASSES) - 1)
                        ins.then_inc(S["res1_mm"], 1)
                        if t + 3 < NT:
                            hidden_T(t + 3)
            moe.close()
            clear_all()

        experts(A["L0_ffn_Wr"], A["L0_ffn_br"], A["L0_ffn_W1"], A["L0_ffn_b1"], A["L0_ffn_W2"], A["L0_ffn_b2"],
                top=2, cap=CAP, i1=2, i2=3, last=False)

        net = ExitStack()

        def nsb(name, shape, dt=F32):
            return net.enter_context(nc.sbuf_tensor(name, shape, dt))

        mod_f = nsb("mod_f", [81, 4, D])
        mod_p = nsb("mod_p", [81, 4, D], F16)
        q_T = nsb("q_T", [128, 2, K, T], F16)
        k_T = b_T
        v_p = nsb("v_p", [P, 2, NT, D], F16)
        GMAX = max(n for _, n in GROUPS) * P + 1
        p_T = nsb("p_T", [P, 2, 2, NT, GMAX], F16)
        rows_s = nsb("rows_s", [P, 3, T])
        soft = nsb("soft", [P, 3, 4])

        def mod_hi(act, half):
            own = slice(2 * half, 2 * half + 2)
            nc.scalar.activation(mod_p[:, own, :], mod_f[:, own, :], ACT.Copy, scale=WSCALE).then_inc(
                S[f"mod_hi{half}"], 1)

        def mod_lo(dve, half):
            own = slice(2 * half, 2 * half + 2)
            dve.wait_ge(S[f"mod_hi{half}"], 1)
            nc.vector.scalar_tensor_tensor(mod_p[64:81, own], mod_f[64:81, own], WSCALE, mod_p[64:81, own],
                                           ALU.mult, ALU.subtract).then_inc(S[f"mod_lo{half}"], 1)

        def mod_rows(t, j, b):
            nc.tensor.matmul(bank(b, P), cond[:, span(t)], mod_p[:, 2 * (j - 1), :],
                             start=True, stop=True).then_inc(S[f"mod_mm{j}"], 1)

        def transposed(pe, t, i, j, b):
            pe.wait_ge(S[f"mod{j}"], i + 1)
            for k in range(K):
                nc.tensor.matmul(ps[:, b, k * P:(k + 1) * P], y[:, t, k * 128:(k + 1) * 128],
                                 ident[0:P, 0:P], is_transpose=True, start=k == 0, stop=False,
                                 skip_group_check=True)
            for k in range(K):
                ins = nc.tensor.matmul(ps[:, b, k * P:(k + 1) * P],
                                       mod_p[:, 2 * j - 1, k * 128:(k + 1) * 128], cond[:, span(t)],
                                       start=False, stop=k == K - 1, skip_group_check=True)
            ins.then_inc(S[f"yt_mm{j}"], 1)

        def high_rows(act, t, i, j, b, dst):
            act.wait_ge(S[f"yt_mm{j}"], i + 1)
            nc.scalar.activation(dst[:, 0, :, span(t)], tr_bank(b), ACT.Copy, scale=1 / WSCALE).then_inc(
                S[f"yt_hi{j}"], 1)

        def low_rows(dve, t, i, j, b, dst):
            dve.wait_ge(S[f"yt_hi{j}"], i + 1)
            nc.vector.scalar_tensor_tensor(dst[:, 1, :, span(t)], tr_bank(b), 1 / WSCALE,
                                           dst[:, 0, :, span(t)], ALU.mult, ALU.subtract).then_inc(
                S[f"yt_lo{j}"], 1)

        def scale_rows(dve, t, i, j, b):
            norm(xg, t).then_inc(S[f"norm{j}"], 1)
            dve.wait_ge(S[f"norm{j}"], i + 1)
            dve.wait_ge(S[f"mod_mm{j}"], i + 1)
            nc.vector.scalar_tensor_tensor(y[:, t, :], bank(b, P), WSCALE, y[:, t, :],
                                           ALU.add, ALU.mult).then_inc(S[f"mod{j}"], 1)

        G0, G1 = (range(first, first + n) for first, n in GROUPS)
        MOD_BANK = {0: 0, 1: 1, 2: 5, 3: 4, 4: 5}
        TR_BANK = {0: 6, 1: 7, 2: 2, 3: 2, 4: 3}
        MOD2_BANK = {0: 3, 1: 4, 2: 5, 3: 3, 4: 4}
        TR2_BANK = {0: 6, 1: 7, 2: 2, 3: 6, 4: 7}
        WO_BANK = (0, 1, 2, 0, 1)

        def load_biases(sp, layer):
            sp.dma_start(bias_col[:, :, :], A["L1_gnn_cols"][bass.ds(layer, 1)][0]).then_inc(S["bias_loaded"], 16)
            for i, n in enumerate(("bv", "bo", "m_b2")):
                sp.dma_start(bias_row[:, i, :], A["L1_gnn_" + n][bass.ds(layer, 1)][0].partition_broadcast(P)).then_inc(
                    S["bias_loaded"], 16)

        with nc.Block() as block:
            @block.sync
            def _(sp):
                sp.dma_start(mod_f[:, :, :], A["mod"][0]).then_inc(S["small_loaded"], 16)
                for i, n in enumerate(("wo", "m_w1", "m_w2")):
                    load_w(sp, 3 + i, A["L1_gnn_" + n][0], i)
                load_biases(sp, 0)
                for i in range(3):
                    sp.wait_ge(S[f"w_loaded{3 + i}"], 16)
                sp.wait_ge(S["bias_loaded"], 64)

            @block.vector
            def _(dve):
                chain = Chain(dve, S["chain_dve"])
                inv_std(dve, chain, 0, NT)
                for t in G0:
                    chain(norm(x, t, dst=xg))
                    chain(row_stats(dve, chain, xg, t))
                inv_std(dve, chain, G0.start, G0.stop)
                mod_lo(dve, 0)
                for t in G0:
                    scale_rows(dve, t, t, 1, MOD_BANK[t])
                    if t:
                        low_rows(dve, t - 1, t - 1, 1, TR_BANK[t - 1], a_T)
                for t in G1:
                    norm(x, t, dst=xg).then_inc(S["resb1"], 1)
                low_rows(dve, G0.stop - 1, G0.stop - 1, 1, TR_BANK[G0.stop - 1], a_T)

            @block.scalar
            def _(act):
                act.wait_ge(S["small_loaded"], 16)
                mod_hi(act, 0)
                for t in G0:
                    high_rows(act, t, t, 1, TR_BANK[t], a_T)

            @block.tensor
            def _(pe):
                pe.wait_ge(S["mod_lo0"], 1)
                for t in G0:
                    mod_rows(t, 1, MOD_BANK[t])
                for t in G0:
                    transposed(pe, t, t, 1, TR_BANK[t])
        clear_all()

        qk_units = [(g, which, m) for g in range(2) for which in range(2) for m in range(K)]
        QK_BANK = (6, 7, 0, 1)
        C_BANK = (5, 2, 0, 1, 5, 2, 0, 1)
        C_FREE = (None, None, ("res1", 4), ("res1", 5), ("c_f", 1), ("c_f", 2), ("c_f", 3), ("c_f", 4))
        heads = [(g, h) for g in range(2) for h in range(H)]
        s_units = [(g, h, i) for g, h in heads for i in range(GROUPS[g][1])]
        NS = len(s_units)
        last_of = {}
        for n, (g, h, i) in enumerate(s_units):
            last_of[g * H + h] = n
        v_parts, o_after = {}, {}
        for gh in range(2 * H):
            c = GROUPS[gh // H][1]
            for part in range(c):
                v_parts.setdefault(min(last_of[gh] + 2 + part, NS), []).append((gh, part, c))
            o_after.setdefault(min(last_of[gh] + 2 + c, NS), []).append(gh)

        def probs_T(n):
            return blocks(2 + 2 * (n % 2), P)

        with nc.Fori(0, NL) as layer:
            with nc.Block() as block:
                @block.sync
                def _(sp):
                    nxt = sp.snap((layer + 1) % NL)

                    def of(name, which):
                        return A[name][bass.ds(which, 1)]

                    sp.wait_ge(S["w_lo3"], 1)
                    load_w(sp, 0, of("L1_gnn_wq", nxt)[0], 0)
                    sp.wait_ge(S["w_lo4"], 1)
                    load_w(sp, 1, of("L1_gnn_wk", nxt)[0], 1)
                    sp.wait_ge(S["mod_lo1"], 1)
                    sp.dma_start(mod_f[:, :, :], of("mod", nxt)[0]).then_inc(S["small_loaded"], 16)
                    sp.wait_ge(S["w_lo5"], 1)
                    load_w(sp, 2, of("L1_gnn_wv", nxt)[0], 2)
                    sp.wait_ge(S["w_lo0"], 1)
                    load_w(sp, 3, of("L1_gnn_wo", nxt)[0], 0)
                    sp.wait_ge(S["w_lo1"], 1)
                    load_w(sp, 4, of("L1_gnn_m_w1", nxt)[0], 1)
                    sp.wait_ge(S["resb2"], NT)
                    sp.wait_ge(S["c_f"], len(units8))
                    load_biases(sp, nxt)
                    sp.wait_ge(S["w_lo2"], 1)
                    load_w(sp, 5, of("L1_gnn_m_w2", nxt)[0], 2)
                    for i in (3, 4, 5):
                        sp.wait_ge(S[f"w_loaded{i}"], 16)
                    sp.wait_ge(S["bias_loaded"], 64)

                @block.gpsimd
                def _(pool):
                    for t in range(NT):
                        if t in G1:
                            pool.wait_ge(S["norm1"], t - G1.start + 1)
                        nc.gpsimd.tensor_tensor(xg[:, t, :], xg[:, t, :], bias_row[:, 1, :], ALU.add).then_inc(
                            S["resb1"], 1)
                    for t in range(NT):
                        pool.wait_ge(S["v_f"], t + 1)
                        pool.wait_ge(S["v_hi"], t + 1)
                        nc.gpsimd.tensor_tensor(v_p[:, 1, t, :], y[:, t, :], v_p[:, 0, t, :],
                                                ALU.subtract).then_inc(S["v_lo"], 1)
                    for i in range(2):
                        split_lo_scaled(pool, i, i)
                    for t in range(NT):
                        pool.wait_ge(S["norm2"], t + 1)
                        nc.gpsimd.tensor_tensor(xg[:, t, :], xg[:, t, :], bias_row[:, 2, :], ALU.add).then_inc(
                            S["resb2"], 1)
                    pool.wait_ge(S["resb2"], NT)
                    pool.wait_ge(S["mod_hi0"], 1)
                    nc.gpsimd.tensor_tensor(mod_p[64:81, 0:2], mod_f[64:81, 0:2], mod_p[64:81, 0:2],
                                            ALU.subtract).then_inc(S["mod_lo0"], 1)

                @block.tensor
                def _(pe):
                    def score(n):
                        g, h, i = s_units[n]
                        t = GROUPS[g][0] + i
                        if n:
                            pe.wait_ge(S["s_max"], n)
                        for a, b in halves:
                            for j, (qp, kp) in enumerate(PASSES):
                                ins = nc.tensor.matmul(pair(0, P, T)[:, a:b], q_T[:, qp, h, span(t)],
                                                       k_T[:, kp, h, a:b], start=j == 0, stop=j == len(PASSES) - 1)
                        ins.then_inc(S["s_mm"], 1)

                    def prob_T(n):
                        pe.wait_ge(S[f"s_prob{n % 2}"], n // 2 + 1)
                        if n >= 2:
                            pe.wait_ge(S["pt_lo"], n - 1)
                        for j in range(NT):
                            ins = nc.tensor.transpose(probs_T(n)[:, j, :], rows_s[:, n % 3, span(j)],
                                                      ident[0:P, 0:P])
                        ins.then_inc(S["pt_mm"], 1)

                    def times_v(gh, part, parts):
                        g, h = heads[gh]
                        cells = GROUPS[g][1] * P
                        if part == 0:
                            pe.wait_ge(S["pt_lo"], last_of[gh] + 1)
                            if gh >= 2:
                                pe.wait_ge(S["o_lo"], gh - 1)
                        c = len(PASSES) * NT
                        for i in range(c * part // parts, c * (part + 1) // parts):
                            (vp, pp), j = PASSES[i // NT], i % NT
                            ins = nc.tensor.matmul(bank(6 + gh % 2, 128, cells),
                                                   v_p[:, vp, j, h * DH:(h + 1) * DH],
                                                   p_T[:, gh % 2, pp, j, 0:cells], start=i == 0, stop=i == c - 1)
                        if part == parts - 1:
                            ins.then_inc(S["o_mm"], 1)

                    def times_wo(t):
                        pe.wait_ge(S["o_lo"], H if t in G0 else 2 * H)
                        if t in G1:
                            pe.wait_ge(S["res1"], t - 2)
                        mat_to_rows(bank(WO_BANK[t], P), w[3], a_T, t).then_inc(S["res1_mm"], 1)

                    for t in G1:
                        mod_rows(t, 1, MOD_BANK[t])
                    for u, (g, which, m) in enumerate(qk_units):
                        if u >= 4:
                            pe.wait_ge(S["a_f"], u - 3)
                        if u == 2 * K:
                            pe.wait_ge(S["yt_lo1"], len(G1))
                        mat_to_T(bank(QK_BANK[u % 4], 128, GROUPS[g][1] * P), w[which], a_T, m, g).then_inc(
                            S["a_mm"], 1)
                        if u == 5:
                            for i, t in enumerate(G1):
                                transposed(pe, t, i, 1, TR_BANK[t])
                    for t in range(NT):
                        if t >= 2:
                            pe.wait_ge(S["v_f"], t - 1)
                        mat_to_rows(bank(2 + t % 2, P), w[2], a_T, t).then_inc(S["v_mm"], 1)
                        if t == 1:
                            pe.wait_ge(S["a_lo"], len(qk_units))
                            score(0)
                        if t == 2:
                            score(1)
                    pe.wait_ge(S["v_f"], NT)
                    for n in range(NS):
                        if n + 2 < NS:
                            score(n + 2)
                        if n == min(v_parts):
                            pe.wait_ge(S["v_lo"], NT)
                        for v in v_parts.get(n, ()):
                            times_v(*v)
                        if n == NS - 2:
                            pe.wait_ge(S["s_max"], NS)
                            pe.wait_ge(S["w_lo3"], 1)
                            times_wo(0)
                        prob_T(n)
                    times_v(*v_parts[NS][0])
                    times_wo(1)
                    for v in v_parts[NS][1:]:
                        times_v(*v)
                    times_wo(2)
                    pe.wait_ge(S["mod_lo1"], 1)
                    for t in G0:
                        mod_rows(t, 2, MOD2_BANK[t])
                    for t in G1:
                        times_wo(t)
                    pe.wait_ge(S["w_lo4"], 1)
                    for g, (first, n) in enumerate(GROUPS):
                        for t in range(first, first + n):
                            transposed(pe, t, t, 2, TR2_BANK[t])
                        if g == 0:
                            for t in G1:
                                mod_rows(t, 2, MOD2_BANK[t])
                        pe.wait_ge(S["yt_lo2"], first + n)
                        for m in range(K):
                            u = g * K + m
                            if C_FREE[u]:
                                pe.wait_ge(S[C_FREE[u][0]], C_FREE[u][1])
                            mat_to_T(bank(C_BANK[u], 128, n * P), w[4], b_T, m, g).then_inc(S["c_mm"], 1)
                    pe.wait_ge(S["w_lo5"], 1)
                    for t in range(NT):
                        pe.wait_ge(S["c_lo"], 4 if t in G0 else 8)
                        if t >= 2:
                            pe.wait_ge(S["res2"], t - 1)
                        mat_to_rows(bank(3 + t % 2, P), w[5], q_T, t).then_inc(S["res2_mm"], 1)
                        if t == 3:
                            pe.wait_ge(S["mod_lo0"], 1)
                            for k in G0:
                                mod_rows(k, 1, MOD_BANK[k])
                    for t in G0:
                        transposed(pe, t, len(G1) + t, 1, TR_BANK[t])

                @block.scalar
                def _(act):
                    A_ = nc.scalar.activation
                    act.wait_ge(S["small_lo"], 1)
                    for u, (g, which, m) in enumerate(qk_units):
                        evac_T(act, "a", u, (q_T, k_T)[which], bank(QK_BANK[u % 4], 128, GROUPS[g][1] * P), m, cols(g),
                               ACT.Identity, scale=(SCORE if which == 0 else 1.0) / WSCALE,
                               bias=bias_col[:, which, m:m + 1],
                               slot_free=(S["a_lo"], u - 3) if u >= 4 else None)
                        if u == 5:
                            for i, t in enumerate(G1):
                                high_rows(act, t, i, 1, TR_BANK[t], a_T)
                        if u in (3, 7, 11):
                            split_hi_now(3 + u // 4, u // 4)
                        if u == 9:
                            mod_hi(act, 1)
                    def hidden(u):
                        g, m = units8[u]
                        evac_T(act, "c", u, q_T, bank(C_BANK[u], 128, GROUPS[g][1] * P), m, cols(g), ACT.Relu,
                               scale=1 / WSCALE, bias=bias_col[:, 2, m:m + 1],
                               slot_free=(S["c_lo"], u - 3) if u >= 4 else (S["o_lo"], 2 * H))

                    def prob_hi(n):
                        g, h, i = s_units[n]
                        act.wait_ge(S["pt_mm"], n + 1)
                        gh = g * H + h
                        if gh >= 2 and i == 0:
                            act.wait_ge(S["o_mm"], gh - 1)
                        A_(p_T[:, gh % 2, 0, :, span(i)], probs_T(n), ACT.Copy).then_inc(S["pt_hi"], 1)

                    def out_hi(gh):
                        g, h = heads[gh]
                        act.wait_ge(S["o_mm"], gh + 1)
                        A_(a_T[:, 0, h, cols(g)], bank(6 + gh % 2, 128, GROUPS[g][1] * P), ACT.Copy,
                           scale=1 / PSCALE).then_inc(S["o_hi"], 1)

                    def exps(n):
                        act.wait_ge(S["s_max"], n + 1)
                        A_(rows_s[:, n % 3, :], rows_s[:, n % 3, :], ACT.Exp, scale=-1.0, bias=soft[:, n % 3, 1:2],
                           accum_out=soft[:, n % 3, 2:3]).then_inc(S["s_exp"], 1)

                    def normalise(n):
                        act.wait_ge(S["s_inv"], n + 1)
                        A_(rows_s[:, n % 3, :], rows_s[:, n % 3, :], ACT.Copy, scale=soft[:, n % 3, 3:4]).then_inc(
                            S["s_prob0"], 1)

                    for t in range(NT):
                        act.wait_ge(S["v_f"], t + 1)
                        A_(v_p[:, 0, t, :], y[:, t, :], ACT.Copy).then_inc(S["v_hi"], 1)
                        if t in (0, 1):
                            split_hi_scaled(act, t, t)
                        if t == 2:
                            exps(0)

                    for n in range(NS):
                        if n:
                            prob_hi(n - 1)
                        if n % 2 == 0:
                            normalise(n)
                        if n + 1 < NS:
                            exps(n + 1)
                        for gh in o_after.get(n, ()):
                            out_hi(gh)
                    prob_hi(NS - 1)
                    for gh in o_after[NS]:
                        out_hi(gh)
                    for t in G0:
                        high_rows(act, t, t, 2, TR2_BANK[t], b_T)
                    for u in range(K):
                        hidden(u)
                    for t in G1:
                        high_rows(act, t, t, 2, TR2_BANK[t], b_T)
                    act.wait_ge(S["small_loaded"], 16)
                    A_(mod_f[:, 0:2, :], mod_f[:, 0:2, :], ACT.Copy, scale=WSCALE).then_inc(S["mod_scaled"], 1)
                    act.wait_ge(S["mod_scaled"], 1)
                    A_(mod_p[:, 0:2, :], mod_f[:, 0:2, :], ACT.Copy).then_inc(S["mod_hi0"], 1)
                    for u in range(K, 2 * K):
                        hidden(u)
                    split_hi(2, 2)
                    for t in G0:
                        high_rows(act, t, len(G1) + t, 1, TR_BANK[t], a_T)

                @block.vector
                def _(dve):
                    V = nc.vector
                    chain = Chain(dve, S["chain_dve"])

                    V.tensor_scalar(bias_col[:, 0, :], bias_col[:, 0, :], SCORE, None, ALU.mult).then_inc(
                        S["small_lo"], 1)
                    for t in G1:
                        chain(row_stats(dve, chain, xg, t))
                    inv_std(dve, chain, G1.start, G1.stop)
                    for i, t in enumerate(G1):
                        scale_rows(dve, t, i, 1, MOD_BANK[t])
                    for u, (g, which, m) in enumerate(qk_units):
                        low_T(dve, "a", u, (q_T, k_T)[which], m, cols(g))
                        if u == 5:
                            for i, t in enumerate(G1):
                                low_rows(dve, t, i, 1, TR_BANK[t], a_T)
                        if u in (3, 7, 11):
                            split_lo(3 + u // 4, u // 4)
                        if u == 9:
                            mod_lo(dve, 1)
                    def row_max(n):
                        g, h, i = s_units[n]
                        t = GROUPS[g][0] + i
                        dve.wait_ge(S["s_mm"], n + 1)
                        if n >= 3:
                            dve.wait_ge(S["pt_mm"], n - 2)
                        V.tensor_tensor_reduce(out=rows_s[:, n % 3, :], in0=pair(0, P, T), in1=lnc[:, t, :], scale=-1.0, scalar=-FLOOR, op0=ALU.add,
                                               op1=ALU.min, accum_out=soft[:, n % 3, 1:2]).then_inc(S["s_max"], 1)

                    def inverse(n):
                        dve.wait_ge(S["s_exp"], n + 1)
                        chain(V.tensor_scalar(soft[:, n % 3, 2:3], soft[:, n % 3, 2:3], 1 / PSCALE, 1e-30, ALU.mult,
                                              ALU.max))
                        V.reciprocal(soft[:, n % 3, 3:4], soft[:, n % 3, 2:3]).then_inc(S["s_inv"], 1)

                    def normalise(n):
                        dve.wait_ge(S["s_inv"], n + 1)
                        V.tensor_scalar(rows_s[:, n % 3, :], rows_s[:, n % 3, :], soft[:, n % 3, 3:4], None,
                                        ALU.mult).then_inc(S["s_prob1"], 1)

                    def prob_lo(n):
                        g, h, i = s_units[n]
                        gh = g * H + h
                        dve.wait_ge(S["pt_hi"], n + 1)
                        V.tensor_tensor(p_T[:, gh % 2, 1, :, span(i)], probs_T(n), p_T[:, gh % 2, 0, :, span(i)],
                                        ALU.subtract).then_inc(S["pt_lo"], 1)

                    def out_lo(gh):
                        g, h = heads[gh]
                        dve.wait_ge(S["o_hi"], gh + 1)
                        V.scalar_tensor_tensor(a_T[:, 1, h, cols(g)], bank(6 + gh % 2, 128, GROUPS[g][1] * P),
                                               1 / PSCALE, a_T[:, 0, h, cols(g)], ALU.mult, ALU.subtract).then_inc(
                            S["o_lo"], 1)

                    for t in range(NT):
                        if 2 <= t < 4:
                            row_max(t - 2)
                        dve.wait_ge(S["v_mm"], t + 1)
                        V.scalar_tensor_tensor(y[:, t, :], bank(2 + t % 2, P), 1 / WSCALE, bias_row[:, 0, :],
                                               ALU.mult, ALU.add).then_inc(S["v_f"], 1)
                    for n in range(NS):
                        inverse(n)
                        if n % 2:
                            normalise(n)
                        if n + 2 < NS:
                            row_max(n + 2)
                        if n:
                            prob_lo(n - 1)
                        for gh in o_after.get(n, ()):
                            out_lo(gh)
                    prob_lo(NS - 1)
                    for gh in o_after[NS]:
                        out_lo(gh)

                    def residual(t, j, b):
                        dve.wait_ge(S[f"res{j}_mm"], t + 1)
                        dve.wait_ge(S[f"resb{j}"], t + 1)
                        V.scalar_tensor_tensor(xg[:, t, :], bank(b, P), 1 / WSCALE, xg[:, t, :],
                                               ALU.mult, ALU.add).then_inc(S[f"res{j}"], 1)

                    for g, (first, n) in enumerate(GROUPS):
                        for t in range(first, first + n):
                            residual(t, 1, WO_BANK[t])
                            dve.wait_ge(S["res1"], t + 1)
                            chain(row_stats(dve, chain, xg, t))
                        inv_std(dve, chain, first, first + n)
                        for t in range(first, first + n):
                            scale_rows(dve, t, t, 2, MOD2_BANK[t])
                        for t in range(first, first + n):
                            low_rows(dve, t, t, 2, TR2_BANK[t], b_T)
                        if g == 1:
                            for u in range(2 * K):
                                low_T(dve, "c", u, q_T, units8[u][1], cols(units8[u][0]))
                    split_lo(2, 2)
                    for t in G0:
                        residual(t, 2, 3 + t % 2)
                        dve.wait_ge(S["res2"], t + 1)
                        chain(row_stats(dve, chain, xg, t))
                    inv_std(dve, chain, G0.start, G0.stop)
                    i = len(G1)
                    scale_rows(dve, 0, i, 1, MOD_BANK[0])
                    residual(3, 2, 4)
                    scale_rows(dve, 1, i + 1, 1, MOD_BANK[1])
                    scale_rows(dve, 2, i + 2, 1, MOD_BANK[2])
                    residual(4, 2, 3)
                    low_rows(dve, 0, i, 1, TR_BANK[0], a_T)
                    low_rows(dve, 1, i + 1, 1, TR_BANK[1], a_T)
                    low_rows(dve, 2, i + 2, 1, TR_BANK[2], a_T)
            clear_all()
        net.close()

        experts(A["L1_ffn_Ws"], A["L1_ffn_bs"], A["L1_ffn_W1"], A["L1_ffn_b1"], A["L1_ffn_W2"], A["L1_ffn_b2"],
                top=1, cap=0, i1=0, i2=1, last=True)


def layout(inputs):
    import numpy as np

    a = {k: np.asarray(v) for k, v in inputs.items()}

    def tiles(m):
        *lead, rows, n = m.shape
        return np.ascontiguousarray(np.moveaxis(m.reshape(*lead, rows // 128, 128, n), -2, -3))

    def columns(v):
        return np.ascontiguousarray(np.swapaxes(v.reshape(*v.shape[:-1], -1, 128), -1, -2))

    out = {k: a[k] for k in ("x", "src", "dst", "L0_gnn_b2", "L0_ffn_br", "L0_ffn_b2", "L1_ffn_bs", "L1_ffn_b2",
                             "L1_gnn_bv", "L1_gnn_bo", "L1_gnn_m_b2", "L1_gnn_f_w1")}
    out["noise"] = a["node_vec1"].reshape(-1)
    for k in ("L0_gnn_W1", "L0_gnn_W2", "L0_ffn_Wr", "L1_ffn_Ws", "L1_gnn_wq", "L1_gnn_wk", "L1_gnn_wv",
              "L1_gnn_wo", "L1_gnn_m_w1", "L1_gnn_m_w2"):
        out[k] = tiles(a[k])
    out["L0_gnn_b1"] = columns(a["L0_gnn_b1"])
    out["L1_gnn_cols"] = np.ascontiguousarray(
        np.stack([columns(a["L1_gnn_" + k]) for k in ("bq", "bk", "m_b1")], axis=2))
    for k in ("L0_ffn_", "L1_ffn_"):
        w1, w2 = a[k + "W1"], a[k + "W2"]
        out[k + "W1"] = tiles(np.moveaxis(w1, 0, 1).reshape(w1.shape[1], -1))
        out[k + "b1"] = a[k + "b1"].reshape(-1)
        out[k + "W2"] = tiles(w2.reshape(-1, w2.shape[-1]))
    nl, c, d = a["L1_gnn_s1_w"].shape
    mod = np.zeros((nl, 81, 4, d), np.float32)
    for j, k in enumerate(("s1", "b1", "s2", "b2")):
        for at in (0, 32, 64):
            mod[:, at:at + c, j] = a[f"L1_gnn_{k}_w"]
            if at != 32:
                mod[:, at + c, j] = a[f"L1_gnn_{k}_b"]
    out["mod"] = mod
    f_w2 = np.zeros((c, 81), np.float32)
    f_b = np.zeros((81, 2), np.float32)
    for at in (0, 32, 64):
        f_w2[:, at:at + c] = a["L1_gnn_f_w2"]
        f_b[at:at + c, 0] = a["L1_gnn_f_b2"]
        if at != 32:
            f_b[at + c, 0] = 1.0
    f_b[0:c, 1] = a["L1_gnn_f_b1"]
    out["f_w2"], out["f_b"] = f_w2, f_b
    return out


def kernel(**inputs):
    import numpy as np
    import concourse.bacc as bacc
    from concourse.bass_utils import run_bass_kernel_spmd

    nc = bacc.Bacc("TRN2", target_bir_lowering=False, num_devices=1)
    arrays, args = {}, {}
    for name, a in layout(inputs).items():
        a = np.ascontiguousarray(a)
        arrays[f"in_{name}_dram"] = a
        args[name] = nc.dram_tensor(f"in_{name}_dram", a.shape, mybir.dt.from_np(a.dtype),
                                    kind="ExternalInput").ap()
    shape = inputs["x"].shape
    out = nc.dram_tensor("out_0_dram", tuple(shape), F32, kind="ExternalOutput").ap()
    build(nc, args, out)
    r = run_bass_kernel_spmd(nc, [arrays], core_ids=[0])
    return r.results[0]["out_0_dram"]
```

```python
from contextlib import ExitStack

import concourse.bass as bass
from concourse import mybir

F32 = mybir.dt.float32
F16 = mybir.dt.float16
I32 = mybir.dt.int32
U32 = mybir.dt.uint32
ALU = mybir.AluOpType
ACT = mybir.ActivationFunctionType
AX_X = mybir.AxisListType.X

WSCALE = 64.0
PSCALE = 1024.0
PASSES = ((0, 0), (1, 0), (0, 1))
DIGIT = 4096
MASK_UNIT = 1.0e28
NO_EDGE = 1.0e-10
FLOOR = -1.0e20
RSQRT_MAGIC = 0x5F3759DF
EPS = 1e-5
TWO_PI_PARTS = (6.28125, 0.0019350051879882812, 3.019916050561733e-07)
INV_TWO_PI = 0.15915494309189535
ROUND_MAGIC = 12582912.0
PI_SAFE = 3.1415925


class Chain:

    def __init__(self, engine, sem):
        self.engine, self.sem, self.n = engine, sem, 0

    def __call__(self, ins):
        self.n += 1
        ins.then_inc(self.sem, 1)
        self.engine.wait_ge(self.sem, self.n)


def build(nc, A, out):
    x_in = A["x"]
    T, D = x_in.shape
    P = 125
    NT = T // P
    K = D // 128
    E = A["L0_ffn_Wr"].shape[2]
    DFF = D // E
    NL = A["mod"].shape[0]
    C = A["f_w2"].shape[0]
    H = 4
    DH = D // H
    SCORE = float(DH) ** -0.5
    NE = A["src"].shape[0]
    NCH = NE // P
    assert T == NT * P and D == K * 128 and NE == NCH * P and E * DFF == D and DH == 128
    CAP = -(-5 * T * 2 // (4 * E))
    NF = A["L1_gnn_f_w1"].shape[0] // 2
    HALF = -(-T // 4) * 2
    GROUPS = [(0, 3), (3, 2)]
    SLOTS = 15
    GROUP = 2 * SLOTS
    LOOPS = NCH // GROUP
    REST = NCH - LOOPS * GROUP
    assert 0 < REST <= GROUP and REST % SLOTS == 0 and GROUP * P < DIGIT and GROUP * P * DIGIT < 2 ** 24

    SEMS = ("x_loaded idx_loaded const_made chain_dve chain_pool onehot_ready onehot_used "
            "count_mm count_copied count_split count_added count_done adj_hi adj_lo xn_hi xn_lo "
            "x_summed mod_loaded rows_normed hid_ready xt_mm xt_hi xt_lo "
            "mod_scaled w_scaled0 w_scaled1 w_scaled2 w_scaled3 ln_f "
            "w_loaded0 w_loaded1 w_loaded2 w_loaded3 w_loaded4 w_loaded5 "
            "w_hi0 w_hi1 w_hi2 w_hi3 w_hi4 w_hi5 w_lo0 w_lo1 w_lo2 w_lo3 w_lo4 w_lo5 "
            "small_loaded small_hi small_lo mod_hi0 mod_hi1 mod_lo0 mod_lo1 bias_loaded "
            "norm1 norm2 mod_mm1 mod_mm2 mod1 mod2 yt_mm1 yt_mm2 yt_hi1 yt_hi2 yt_lo1 yt_lo2 "
            "a_mm a_f a_hi a_lo b_mm b_f b_hi b_lo c_mm c_f c_hi c_lo "
            "v_mm v_f v_hi v_lo o_mm o_hi o_lo res1_mm res2_mm res1 res2 resb1 resb2 "
            "s_mm s_max s_exp s_inv s_prob0 s_prob1 pt_mm pt_hi pt_lo "
            "r_mm r_lg r_exp r_w wt_mm wt_parts pos_mm pos_done gm gelu_done hm_done "
            "phase_made sines_made cond_parts cond_layer cond_mm stored").split()
    ctx = ExitStack()
    with ctx:
        S = {n: ctx.enter_context(nc.semaphore(n)) for n in SEMS}
        nums = [s.num for s in S.values()]
        assert nums == list(range(nums[0], nums[0] + len(nums)))

        def clear_all():
            nc.all_engine_barrier(sems_to_clear=range(nums[0], nums[0] + len(nums)))

        def sb(name, shape, dt=F32):
            return ctx.enter_context(nc.sbuf_tensor(name, shape, dt))

        ps = ctx.enter_context(nc.psum_tensor("ps", [128, 8, 512], F32))

        def bank(b, p=128, n=512):
            return ps[0:p, b, 0:n]

        def pair(b, p, n):
            return ps[0:p, b:b + 2, :].rearrange("p b n -> p (b n)")[:, 0:n]

        def blocks(b, p):
            return pair(b, p, NT * 128).rearrange("p (t n) -> p t n", n=128)[:, :, 0:P]

        x = sb("x", [P, NT, D])
        xg = sb("xg", [P, NT, D])
        y = sb("y", [P, NT, D])
        stats = sb("stats", [P, NT, 16])
        ident = sb("ident", [128, 128])
        lnc = sb("lnc", [P, NT, T])
        stage = [sb(f"stage{i}", [128, K, D])[:, :, :] for i in range(3)]
        parts = sb("parts", [128, 6, 2, K, D], F16)
        w = [parts[:, i] for i in range(6)]
        bias_col = sb("bias_col", [128, 3, K])
        bias_row = sb("bias_row", [P, 3, D])
        a_T = sb("a_T", [128, 2, K, T], F16)
        b_T = sb("b_T", [128, 2, K, T], F16)
        fbuf = sb("fbuf", [128, 4, 375])
        cond = sb("cond", [81, T], F16)

        def row_stats(dve, chain, src, t):
            chain(nc.vector.bn_stats(stats[:, t, 2:8], src[:, t, :]))
            return nc.vector.bn_aggr(stats[:, t, 0:2], stats[:, t, 2:8])

        def inv_std(dve, chain, t0, t1):
            V = nc.vector
            ve, r, q, h = (stats[:, t0:t1, i] for i in range(8, 12))
            chain(V.tensor_scalar(ve, stats[:, t0:t1, 1], EPS, (256.0 / 3) ** 2, ALU.add, ALU.mult))
            chain(V.tensor_scalar(r.bitcast(I32), ve.bitcast(I32), -0.5, float(RSQRT_MAGIC - 2 ** 31),
                                  ALU.mult, ALU.add))
            chain(V.tensor_tensor(q, r, r, ALU.mult))
            chain(V.tensor_tensor(q, q, ve, ALU.mult))
            chain(V.scalar_tensor_tensor(r, q, 3.0, r, ALU.subtract, ALU.mult))
            chain(V.tensor_tensor(q, r, r, ALU.mult))
            chain(V.tensor_tensor(q, q, ve, ALU.mult))
            chain(V.scalar_tensor_tensor(h, q, 4 * 10 / 3, q, ALU.subtract, ALU.mult))
            chain(V.scalar_tensor_tensor(r, h, 16 * 5.0, r, ALU.add, ALU.mult))

        def norm(src, t, dst=None):
            return nc.vector.tensor_scalar((y if dst is None else dst)[:, t, :], src[:, t, :], stats[:, t, 0:1],
                                           stats[:, t, 9:10], ALU.subtract, ALU.mult)

        def cols(g):
            return slice(GROUPS[g][0] * P, (GROUPS[g][0] + GROUPS[g][1]) * P)

        def span(t):
            return slice(t * P, (t + 1) * P)

        def mat_to_T(dst, weights, act, m, g, low=None):
            n = len(PASSES) * K
            for i in range(n):
                (wp, ap), k = PASSES[i // K], i % K
                if low and i == 2 * K:
                    nc.tensor.wait_ge(*low)
                ins = nc.tensor.matmul(dst, weights[:, wp, k, m * 128:(m + 1) * 128], act[:, ap, k, cols(g)],
                                       start=i == 0, stop=i == n - 1)
            return ins

        def mat_to_rows(dst, weights, act, t, last=True, low=None):
            n = len(PASSES) * K
            for i in range(n):
                (wp, ap), k = PASSES[i // K], i % K
                if low and i == 2 * K:
                    nc.tensor.wait_ge(*low)
                ins = nc.tensor.matmul(dst, act[:, ap, k, span(t)], weights[:, wp, k, :],
                                       start=i == 0, stop=last and i == n - 1)
            return ins

        def load_w(eng, i, src, stg):
            eng.dma_start(stage[stg], src).then_inc(S[f"w_loaded{i}"], 16)

        def split_hi(i, stg):
            nc.scalar.wait_ge(S[f"w_loaded{i}"], 16)
            split_hi_now(i, stg)

        def split_hi_now(i, stg):
            nc.scalar.activation(w[i][:, 0], stage[stg], ACT.Copy, scale=WSCALE).then_inc(S[f"w_hi{i}"], 1)

        def split_hi_scaled(act, i, stg):
            act.wait_ge(S[f"w_loaded{i}"], 16)
            nc.scalar.activation(stage[stg], stage[stg], ACT.Copy, scale=WSCALE).then_inc(S[f"w_scaled{i}"], 1)
            act.wait_ge(S[f"w_scaled{i}"], 1)
            nc.scalar.activation(w[i][:, 0], stage[stg], ACT.Copy).then_inc(S[f"w_hi{i}"], 1)

        def split_lo_scaled(pool, i, stg):
            pool.wait_ge(S[f"w_hi{i}"], 1)
            nc.gpsimd.tensor_tensor(w[i][:, 1], stage[stg], w[i][:, 0], ALU.subtract).then_inc(S[f"w_lo{i}"], 1)

        def split_lo(i, stg):
            nc.vector.wait_ge(S[f"w_hi{i}"], 1)
            nc.vector.scalar_tensor_tensor(w[i][:, 1], stage[stg], WSCALE, w[i][:, 0],
                                           ALU.mult, ALU.subtract).then_inc(S[f"w_lo{i}"], 1)

        graph = ExitStack()

        def gsb(name, shape, dt=F32):
            return graph.enter_context(nc.sbuf_tensor(name, shape, dt))

        idx_i = gsb("idx_i", [P, 2, NCH], I32)
        src_f = gsb("src_f", [P, NCH])
        dst_f = gsb("dst_f", [P, NCH])
        dst_hi = gsb("dst_hi", [P, NCH])
        dst_w = gsb("dst_w", [P, NCH])
        iota_i = gsb("iota_i", [P, T], I32)
        iota = gsb("iota", [P, T], F16)
        hot_s = gsb("hot_s", [P, SLOTS, T + 1], F16)
        hot_d = gsb("hot_d", [P, SLOTS, HALF], F16)
        ident_h = gsb("ident_h", [P, P], F16)
        no_edge = gsb("no_edge", [P, 1])
        free_w = parts[:, 2:6].rearrange("p s h k n -> p (s h k n)").bitcast(I32)
        copied = free_w[0:P, 0:NT * HALF].rearrange("p (t n) -> p t n", t=NT)
        count = free_w[0:P, 2 * K * D:2 * K * D + NT * 2 * HALF].rearrange("p (t n) -> p t n", t=NT)
        digits = gsb("digits", [P, NT, 2, HALF], I32)
        adj = gsb("adj", [P, 2, NT, T], F16)
        xn = xg[:, :, :].rearrange("p t d -> p (t d)").bitcast(F16).rearrange("p (a t d) -> p a t d", a=2, t=NT)


        def evac_T(act, s, u, dst, src, m, where, func, scale=1.0, bias=None, slot_free=None):
            n = where.stop - where.start
            act.wait_ge(S[s + "_mm"], u + 1)
            if slot_free is not None:
                act.wait_ge(*slot_free)
            f = fbuf[:, u % 4, 0:n]
            if bias is None:
                nc.scalar.activation(f, src, func, scale=scale).then_inc(S[s + "_f"], 1)
            else:
                nc.scalar.activation(f, src, func, scale=scale, bias=bias).then_inc(S[s + "_f"], 1)
            act.wait_ge(S[s + "_f"], u + 1)
            nc.scalar.activation(dst[:, 0, m, where], f, ACT.Copy).then_inc(S[s + "_hi"], 1)

        def low_T(dve, s, u, dst, m, where):
            n = where.stop - where.start
            dve.wait_ge(S[s + "_hi"], u + 1)
            nc.vector.tensor_tensor(dst[:, 1, m, where], fbuf[:, u % 4, 0:n], dst[:, 0, m, where],
                                    ALU.subtract).then_inc(S[s + "_lo"], 1)

        def tr_bank(b):
            return ps[:, b, 0:K * P].rearrange("p (k n) -> p k n", k=K)

        def transpose_rows(pe, b, src, sem):
            for k in range(K):
                ins = nc.tensor.transpose(ps[:, b, k * P:(k + 1) * P], src[:, k * 128:(k + 1) * 128],
                                          ident[0:P, 0:P])
            ins.then_inc(sem, 1)

        units8 = [(g, m) for g in range(2) for m in range(K)]
        halves = ((0, 512), (512, T))

        hot_flat = hot_s[:, :, :].rearrange("p s n -> p (s n)").bitcast(F32)

        places = [0]

        def scratch(p, n):
            places.append(places[-1] + n)
            return hot_flat[0:p, places[-2]:places[-1]]

        phase, turns, noise = (scratch(2 * NF, T) for _ in range(3))
        cond_f, e1_f = scratch(81, T), scratch(C, T)
        f_w1f, f_w2f, f_b, freq = scratch(2 * NF, C), scratch(C, 81), scratch(81, 2), scratch(2 * NF, 4)
        emb = scratch(2 * NF, T).bitcast(F16).rearrange("p (a n) -> p a n", a=2)
        e1 = scratch(C, T).bitcast(F16).rearrange("p (a n) -> p a n", a=2)
        f_w1 = scratch(2 * NF, C).bitcast(F16).rearrange("p (a n) -> p a n", a=2)
        f_w2 = scratch(C, 81).bitcast(F16).rearrange("p (a n) -> p a n", a=2)
        freq_i = stats[0:2 * NF, NT - 1, 12:13].bitcast(I32)

        with nc.Block() as block:
            @block.sync
            def _(sp):
                sp.dma_start(idx_i[:, 0, :], A["src"].rearrange("(p c) -> p c", p=P)).then_inc(S["idx_loaded"], 16)
                sp.dma_start(idx_i[:, 1, :], A["dst"].rearrange("(p c) -> p c", p=P)).then_inc(S["idx_loaded"], 16)
                sp.dma_start(x[:, :, :], x_in.rearrange("(t p) d -> p t d", p=P)).then_inc(S["x_loaded"], 16)
                for i, n in enumerate(("L0_gnn_W1", "L0_gnn_W2")):
                    load_w(sp, i, A[n], i)
                sp.dma_start(bias_col[:, 0, :], A["L0_gnn_b1"]).then_inc(S["bias_loaded"], 16)
                sp.dma_start(bias_row[:, 0, :], A["L0_gnn_b2"].partition_broadcast(P)).then_inc(
                    S["bias_loaded"], 16)
                load_w(sp, 2, A["L0_ffn_W1"], 2)
                sp.wait_ge(S["w_lo0"], 1)
                load_w(sp, 3, A["L0_ffn_W2"], 0)
                sp.wait_ge(S["onehot_used"], SLOTS + NCH)
                for dst, src in ((noise, A["noise"].partition_broadcast(2 * NF)), (f_w1f, A["L1_gnn_f_w1"]),
                                 (f_w2f, A["f_w2"]), (f_b, A["f_b"])):
                    sp.dma_start(dst, src).then_inc(S["small_loaded"], 16)
                sp.wait_ge(S["small_loaded"], 64)

            @block.gpsimd
            def _(pool):
                TT = nc.gpsimd.tensor_tensor
                chain = Chain(pool, S["chain_pool"])
                nc.gpsimd.iota(iota_i[:, :], [[1, T]], base=0, channel_multiplier=0).then_inc(S["const_made"], 1)
                nc.gpsimd.memset(no_edge[:, :], NO_EDGE)
                nc.gpsimd.iota(freq_i, [[1, 1]], base=1, channel_multiplier=1)
                chain(nc.gpsimd.memset(ident[:, :], 0.0))
                nc.gpsimd.affine_select(out=ident[:, :], in_=ident[:, :], compare_op=ALU.not_equal, fill=1.0,
                                        base=0, pattern=[[-1, 128]], channel_multiplier=1).then_inc(S["const_made"], 1)
                chain(nc.gpsimd.memset(count[:, :, :], 0))
                pool.sem_inc(S["count_added"], NT)
                for i in range(2):
                    split_lo_scaled(pool, i, i)
                for t in range(NT):
                    pool.wait_ge(S["xn_hi"], t + 1)
                    TT(xn[:, 1, t, :], y[:, t, :], xn[:, 0, t, :], ALU.subtract).then_inc(S["xn_lo"], 1)
                with pool.Fori(0, LOOPS) as g:
                    for t in range(NT):
                        pool.wait_ge(S["count_split"], g * NT + (t + 1))
                        TT(count[:, t, :], count[:, t, :], digits[:, t, :, :].rearrange("p a n -> p (a n)"),
                           ALU.add).then_inc(S["count_added"], 1)
                pool.wait_ge(S["bias_loaded"], 32)
                for t in range(NT):
                    TT(x[:, t, :], x[:, t, :], bias_row[:, 0, :], ALU.add).then_inc(S["resb1"], 1)

            @block.scalar
            def _(act):
                A_ = nc.scalar.activation

                def copy_counts(g, t, chunks):
                    if t < NT - 1:
                        act.wait_ge(S["count_mm"], g * (NT - 1) + (t + 1))
                    else:
                        act.wait_ge(S["onehot_used"], chunks + SLOTS)
                    A_(copied[:, t, :], bank(t, P, HALF), ACT.Copy).then_inc(S["count_copied"], 1)

                for i in range(2):
                    split_hi_scaled(act, i, i)
                for t in range(NT):
                    copy_counts(0, t, GROUP)
                for t in range(NT):
                    act.wait_ge(S["norm1"], t + 1)
                    A_(xn[:, 0, t, :], y[:, t, :], ACT.Copy).then_inc(S["xn_hi"], 1)
                with act.Fori(1, LOOPS) as g:
                    for t in range(NT):
                        act.wait_ge(S["count_split"], (g - 1) * NT + (t + 1))
                        copy_counts(g, t, g * GROUP + GROUP)
                for t in range(NT):
                    act.wait_ge(S["count_split"], (LOOPS - 1) * NT + t + 1)
                    copy_counts(LOOPS, t, NCH)
                for t in range(NT):
                    act.wait_ge(S["count_done"], t + 1)
                    A_(adj[:, 0, t, :], count[:, t, 0:T], ACT.Copy).then_inc(S["adj_hi"], 1)
                act.wait_ge(S["count_done"], NT)
                split_hi(3, 0)
                split_hi(2, 2)
                for u, (g, m) in enumerate(units8):
                    act.wait_ge(S["a_mm"], u + 1)
                    A_(a_T[:, 0, m, cols(g)], bank(u, 128, GROUPS[g][1] * P), ACT.Copy).then_inc(S["a_hi"], 1)
                act.wait_ge(S["phase_made"], 1)
                A_(phase, phase, ACT.Sin).then_inc(S["sines_made"], 1)
                act.wait_ge(S["bias_loaded"], 32)
                for u, (g, m) in enumerate(units8):
                    evac_T(act, "b", u, b_T, bank(u, 128, GROUPS[g][1] * P), m, cols(g), ACT.Relu,
                           scale=1 / WSCALE, bias=bias_col[:, 0, m:m + 1],
                           slot_free=(S["b_lo"], u - 3) if u >= 4 else None)
                act.wait_ge(S["cond_mm"], 1)
                A_(e1_f, pair(6, C, T), ACT.Silu, scale=1 / WSCALE, bias=f_b[0:C, 1:2]).then_inc(S["cond_layer"], 1)
                act.wait_ge(S["cond_mm"], 2)
                A_(cond_f, pair(6, 81, T), ACT.Identity, scale=1 / WSCALE, bias=f_b[:, 0:1]).then_inc(S["cond_layer"], 1)
                for t in range(NT):
                    A_(lnc[:, t, :], count[:, t, 0:T], ACT.Ln, scale=2.0, bias=no_edge[:, :]).then_inc(
                        S["ln_f"], 1)

            @block.vector
            def _(dve):
                V = nc.vector
                chain = Chain(dve, S["chain_dve"])
                dve.wait_ge(S["const_made"], 1)
                V.tensor_copy(iota[:, :], iota_i[:, :])
                dve.wait_ge(S["idx_loaded"], 32)
                chain(V.tensor_scalar(dst_hi[:, :], idx_i[:, 1, :], float(HALF), None, ALU.is_ge))
                V.tensor_scalar(dst_w[:, :], dst_hi[:, :], float(DIGIT - 1), 1.0, ALU.mult, ALU.add)
                V.tensor_copy(src_f[:, :], idx_i[:, 0, :])
                chain(V.scalar_tensor_tensor(dst_f[:, :], dst_hi[:, :], -float(HALF), idx_i[:, 1, :],
                                             ALU.mult, ALU.add))

                def one_hot(c, slot):
                    dve.wait_ge(S["onehot_used"], c + 1)
                    if not isinstance(c, int):
                        c = dve.snap(c)
                    V.tensor_scalar(hot_s[:, slot, 0:T], iota[:, :], src_f[:, bass.ds(c, 1)], None, ALU.is_equal)
                    V.tensor_scalar(hot_d[:, slot, :], iota[:, 0:HALF], dst_f[:, bass.ds(c, 1)],
                                    dst_w[:, bass.ds(c, 1)], ALU.is_equal, ALU.mult).then_inc(S["onehot_ready"], 1)

                def unpack(g, t):
                    dve.wait_ge(S["count_copied"], g * NT + (t + 1))
                    dve.wait_ge(S["count_added"], g * NT + (t + 1))
                    V.tensor_scalar(digits[:, t, 0, :], copied[:, t, :], DIGIT - 1, None, ALU.bitwise_and)
                    return V.tensor_scalar(digits[:, t, 1, :], copied[:, t, :], DIGIT.bit_length() - 1,
                                           None, ALU.logical_shift_right)

                for c in range(GROUP):
                    one_hot(c, c % SLOTS)
                    t = (c - SLOTS + 2) // 2
                    if c == SLOTS - 2:
                        dve.wait_ge(S["x_loaded"], 16)
                    if c >= SLOTS - 2 and c % 2 and t < NT:
                        chain(row_stats(dve, chain, x, t))
                inv_std(dve, chain, 0, NT)
                for t in range(NT):
                    norm(x, t).then_inc(S["norm1"], 1)
                with dve.Fori(1, LOOPS) as g:
                    for j in range(GROUP):
                        one_hot(g * GROUP + j, j % SLOTS)
                        if j % 6 == 5:
                            unpack(g - 1, j // 6).then_inc(S["count_split"], 1)
                for j in range(REST):
                    one_hot(LOOPS * GROUP + j, j % SLOTS)
                    if j % 3 == 2:
                        unpack(LOOPS - 1, j // 3).then_inc(S["count_split"], 1)
                dve.wait_ge(S["const_made"], 2)
                V.tensor_copy(ident_h[:, :], ident[0:P, 0:P]).then_inc(S["const_made"], 1)
                def low_counts(t):
                    dve.wait_ge(S["adj_hi"], t + 1)
                    V.tensor_tensor(adj[:, 1, t, :], count[:, t, 0:T], adj[:, 0, t, :], ALU.subtract).then_inc(
                        S["adj_lo"], 1)

                for t in range(NT):
                    chain(unpack(LOOPS, t))
                    V.tensor_tensor(count[:, t, :], count[:, t, :],
                                    digits[:, t, :, :].rearrange("p a n -> p (a n)"), ALU.add).then_inc(
                        S["count_done"], 1)
                    if t:
                        low_counts(t - 1)
                low_counts(NT - 1)
                split_lo(3, 0)

                def low_sums(u):
                    g, m = units8[u]
                    dve.wait_ge(S["a_hi"], u + 1)
                    V.tensor_tensor(a_T[:, 1, m, cols(g)], bank(u, 128, GROUPS[g][1] * P), a_T[:, 0, m, cols(g)],
                                    ALU.subtract).then_inc(S["a_lo"], 1)

                for u in range(K):
                    low_sums(u)
                k, is_cos, shift, f = (freq[:, i:i + 1] for i in range(4))
                chain(V.tensor_copy(k, freq_i))
                chain(V.tensor_scalar(is_cos, k, float(NF), None, ALU.is_gt))
                chain(V.scalar_tensor_tensor(k, is_cos, -float(NF), k, ALU.mult, ALU.add))
                chain(V.tensor_scalar(shift, is_cos, 1.5707963267948966, None, ALU.mult))
                chain(V.tensor_scalar(f, k, 0.39269908169872414, None, ALU.mult))
                dve.wait_ge(S["small_loaded"], 64)
                chain(V.tensor_scalar(phase, noise, f, None, ALU.mult))
                chain(V.tensor_scalar(turns, phase, INV_TWO_PI, ROUND_MAGIC, ALU.mult, ALU.add))
                chain(V.tensor_scalar(turns, turns, ROUND_MAGIC, None, ALU.subtract))
                for part in TWO_PI_PARTS:
                    chain(V.scalar_tensor_tensor(phase, turns, -part, phase, ALU.mult, ALU.add))
                chain(V.tensor_scalar(phase, phase, shift, None, ALU.add))
                chain(V.tensor_scalar(turns, phase, 3.141592653589793, -6.283185307179586, ALU.is_gt, ALU.mult))
                chain(V.tensor_tensor(phase, phase, turns, ALU.add))
                V.tensor_scalar(phase, phase, PI_SAFE, -PI_SAFE, ALU.min, ALU.max).then_inc(S["phase_made"], 1)
                for f_, p_ in ((f_w1f, f_w1), (f_w2f, f_w2)):
                    chain(V.tensor_scalar(f_[:, :], f_[:, :], WSCALE, None, ALU.mult))
                    chain(V.tensor_copy(p_[:, 0, :], f_[:, :]))
                    chain(V.tensor_tensor(p_[:, 1, :], f_[:, :], p_[:, 0, :], ALU.subtract))
                for u in range(K, 2 * K):
                    low_sums(u)
                split_lo(2, 2)
                for u, (g, m) in enumerate(units8):
                    low_T(dve, "b", u, b_T, m, cols(g))
                    if u == 1:
                        dve.wait_ge(S["sines_made"], 1)
                        chain(V.tensor_copy(emb[:, 0, :], phase))
                        V.tensor_tensor(emb[:, 1, :], phase, emb[:, 0, :], ALU.subtract).then_inc(S["cond_parts"], 1)
                dve.wait_ge(S["cond_layer"], 1)
                chain(V.tensor_copy(e1[:, 0, :], e1_f))
                V.tensor_tensor(e1[:, 1, :], e1_f, e1[:, 0, :], ALU.subtract).then_inc(S["cond_parts"], 1)

                for t in range(NT):
                    dve.wait_ge(S["res1_mm"], t + 1)
                    dve.wait_ge(S["resb1"], t + 1)
                    V.scalar_tensor_tensor(x[:, t, :], bank(t % 4, P), 1 / WSCALE, x[:, t, :],
                                           ALU.mult, ALU.add).then_inc(S["res1"], 1)
                    dve.wait_ge(S["res1"], t + 1)
                    chain(row_stats(dve, chain, x, t))
                    if t == 2:
                        dve.wait_ge(S["cond_layer"], 2)
                        chain(V.tensor_copy(cond[:, :], cond_f))
                        V.tensor_tensor(cond[32:32 + C, :], cond_f[32:32 + C, :], cond[32:32 + C, :], ALU.subtract)

            @block.tensor
            def _(pe):
                pe.sem_inc(S["onehot_used"], SLOTS)

                def add_chunk(c, slot, first, last, g):
                    pe.wait_ge(S["onehot_ready"], c + 1)
                    for t in range(NT):
                        if first and not isinstance(g, int) or first and g:
                            pe.wait_ge(S["count_copied"], (g - 1) * NT + (t + 1))
                        ins = nc.tensor.matmul(bank(t, P, HALF), hot_s[:, slot, span(t)], hot_d[:, slot, :],
                                               start=first, stop=last)
                        if last and t < NT - 1:
                            ins.then_inc(S["count_mm"], 1)
                    ins.then_inc(S["onehot_used"], 1)

                for c in range(GROUP):
                    add_chunk(c, c % SLOTS, c == 0, c == GROUP - 1, 0)
                with pe.Fori(1, LOOPS) as g:
                    for j in range(GROUP):
                        add_chunk(g * GROUP + j, j % SLOTS, j == 0, j == GROUP - 1, g)
                for j in range(REST):
                    add_chunk(LOOPS * GROUP + j, j % SLOTS, j == 0, j == REST - 1, LOOPS)
                pe.wait_ge(S["xn_lo"], NT)
                pe.wait_ge(S["const_made"], 3)
                pe.wait_ge(S["count_copied"], (LOOPS + 1) * NT)
                for g, (first, n) in enumerate(GROUPS):
                    for t in range(NT):
                        pe.wait_ge(S["adj_lo"], t + 1)
                        for m in range(K):
                            u = g * K + m
                            for i, (ap, wp) in enumerate(PASSES):
                                ins = nc.tensor.matmul(bank(u, 128, n * P), xn[:, ap, t, m * 128:(m + 1) * 128],
                                                       adj[:, wp, t, cols(g)], start=t == 0 and i == 0,
                                                       stop=t == NT - 1 and i == len(PASSES) - 1,
                                                       skip_group_check=True)
                                if i == 0 and first <= t < first + n:
                                    for own in range(2):
                                        nc.tensor.matmul(ps[:, u, (t - first) * P:(t - first + 1) * P],
                                                         xn[:, own, t, m * 128:(m + 1) * 128], ident_h[:, :],
                                                         start=False, stop=False, skip_group_check=True)
                            if t == NT - 1:
                                ins.then_inc(S["a_mm"], 1)
                pe.wait_ge(S["w_lo0"], 1)
                for u, (g, m) in enumerate(units8):
                    pe.wait_ge(S["a_lo"], 4 * (g + 1))
                    mat_to_T(bank(u, 128, GROUPS[g][1] * P), w[0], a_T, m, g).then_inc(S["b_mm"], 1)
                pe.wait_ge(S["w_lo1"], 1)

                def condition_layer(weights, values, width):
                    for a, b in halves:
                        for i, (wp, ep) in enumerate(PASSES):
                            ins = nc.tensor.matmul(pair(6, width, T)[:, a:b], weights[:, wp, :], values[:, ep, a:b],
                                                   start=i == 0, stop=i == len(PASSES) - 1)
                    ins.then_inc(S["cond_mm"], 1)

                pe.wait_ge(S["cond_parts"], 1)
                pe.wait_ge(S["b_f"], 8)
                condition_layer(f_w1, emb, C)
                for t in range(NT):
                    pe.wait_ge(S["b_lo"], 4 if t < 3 else 8)
                    if t == 2:
                        pe.wait_ge(S["cond_parts"], 2)
                        condition_layer(f_w2, e1, 81)
                    if t >= 4:
                        pe.wait_ge(S["res1"], t - 3)
                    mat_to_rows(bank(t % 4, P), w[1], b_T, t).then_inc(S["res1_mm"], 1)
        clear_all()

        graph.close()

        def experts(Wr, br, W1, b1, W2, b2, top, cap, i1, i2, last, then=None):
            moe = ExitStack()

            def msb(name, shape, dt=F32):
                return moe.enter_context(nc.sbuf_tensor(name + ("a" if cap else "b"), shape, dt))

            wr_f = msb("wr_f", [128, K, E])
            wr = msb("wr", [128, K, 2, E], F16)
            br_row = msb("br_row", [P, E])
            b2_f = bias_row[0:E, 0, :]
            b2_p = msb("b2_p", [E, 2, D], F16)
            prob = msb("prob", [P, NT, E])
            hot = msb("hot", [P, 3, NT, E])
            top_v = msb("top_v", [P, NT, 8])
            top_i = msb("top_i", [P, NT, 8], U32)
            top_f = msb("top_f", [P, NT, 8])
            one = msb("one", [P, 8, NT])
            sent = msb("sent", [P, NT, E], F16)
            iota_e = msb("iota_e", [P, E], I32)
            iota_f = msb("iota_f", [P, E])
            wt = msb("wt", [E, 2, T], F16)
            flat_f = fbuf[0:P, :, :].rearrange("p a n -> p (a n)")
            hid = flat_f[:, 0:2 * D].rearrange("p (a n) -> p a n", a=2)
            before = flat_f[:, 2 * D:2 * D + P].bitcast(F16).rearrange("p (a n) -> p a n", a=2)

            GM_BANK = (6, 7, 2, 3, 6)

            def each(v):
                return v.unsqueeze(2).to_broadcast([P, NT, E])

            with nc.Block() as block:
                @block.sync
                def _(sp):
                    sp.dma_start(wr_f[:, :, :], Wr).then_inc(S["small_loaded"], 16)
                    sp.dma_start(b2_f[:, :], b2).then_inc(S["small_loaded"], 16)
                    sp.dma_start(br_row[:, :], br.partition_broadcast(P)).then_inc(S["bias_loaded"], 16)
                    sp.dma_start(bias_row[:, 1, :], b1.partition_broadcast(P)).then_inc(S["bias_loaded"], 16)
                    if last:
                        load_w(sp, i1, W1, 0)
                        load_w(sp, i2, W2, 1)
                    else:
                        for i, n in enumerate(("wq", "wk", "wv")):
                            load_w(sp, i, A["L1_gnn_" + n][0], i)
                        then["sync"](sp)
                    if last:
                        for t in range(NT):
                            sp.wait_ge(S["res1"], t + 1)
                            sp.dma_start(out[span(t), :], x[:, t, :]).then_inc(S["stored"], 16)
                        sp.wait_ge(S["stored"], 16 * NT)

                @block.gpsimd
                def _(pool):
                    chain = Chain(pool, S["chain_pool"])
                    nc.gpsimd.iota(iota_e[:, :], [[1, E]], base=0, channel_multiplier=0).then_inc(S["const_made"], 1)
                    chain(nc.gpsimd.memset(before, 1.0))
                    nc.gpsimd.affine_select(out=before[:, 0, :], in_=before[:, 0, :], compare_op=ALU.is_gt,
                                            fill=0.0, base=0, pattern=[[1, P]], channel_multiplier=-1).then_inc(
                        S["const_made"], 1)
                    if last:
                        for t in range(3, NT):
                            nc.gpsimd.tensor_tensor(x[:, t, :], x[:, t, :], xg[:, t, :], ALU.add).then_inc(
                                S["x_summed"], 1)
                        for i, stg in ((i1, 0), (i2, 1)):
                            split_lo_scaled(pool, i, stg)
                    else:
                        for i in range(3):
                            split_lo_scaled(pool, i, i)

                @block.vector
                def _(dve):
                    V = nc.vector
                    chain = Chain(dve, S["chain_dve"])
                    if last:
                        for t in range(NT):
                            if t < 3:
                                chain(V.tensor_tensor(x[:, t, :], x[:, t, :], xg[:, t, :], ALU.add))
                            else:
                                dve.wait_ge(S["x_summed"], t - 2)
                            chain(row_stats(dve, chain, x, t))
                    inv_std(dve, chain, 0, NT)
                    norm(x, 0).then_inc(S["rows_normed"], 1)
                    norm(x, 1).then_inc(S["rows_normed"], 1)
                    norm(x, 2).then_inc(S["rows_normed"], 1)
                    dve.wait_ge(S["small_hi"], 1)
                    V.scalar_tensor_tensor(wr[:, :, 1, :], wr_f[:, :, :], WSCALE, wr[:, :, 0, :], ALU.mult,
                                           ALU.subtract).then_inc(S["small_lo"], 1)
                    for t in range(NT):
                        dve.wait_ge(S["xt_hi"], t + 1)
                        V.tensor_tensor(a_T[:, 1, :, span(t)], tr_bank(t % 2), a_T[:, 0, :, span(t)],
                                        ALU.subtract).then_inc(S["xt_lo"], 1)
                        if t + 3 < NT:
                            norm(x, t + 3).then_inc(S["rows_normed"], 1)
                    dve.wait_ge(S["small_hi"], 2)
                    V.scalar_tensor_tensor(b2_p[:, 1, :], b2_f[:, :], WSCALE, b2_p[:, 0, :], ALU.mult,
                                           ALU.subtract).then_inc(S["small_lo"], 1)
                    if not last:
                        for t in range(NT):
                            V.scalar_tensor_tensor(lnc[:, t, :], lnc[:, t, :], MASK_UNIT, lnc[:, t, :],
                                                   ALU.mult, ALU.min)

                    def hidden_rows(t):
                        dve.wait_ge(S["gm"], t + 1)
                        if t >= 2:
                            dve.wait_ge(S["hm_done"], t - 1)
                        V.scalar_tensor_tensor(hid[:, t % 2, :], bank(GM_BANK[t], P), 1 / WSCALE, bias_row[:, 1, :],
                                               ALU.mult, ALU.add).then_inc(S["hid_ready"], 1)

                    dve.wait_ge(S["const_made"], 2)
                    chain(V.tensor_copy(iota_f[:, :], iota_e[:, :]))
                    dve.wait_ge(S["bias_loaded"], 32)
                    dve.wait_ge(S["r_mm"], NT)
                    lg = ps[0:P, 4, 0:NT * 2 * E].rearrange("p (t a e) -> p a t e", a=2, e=E)
                    chain(V.scalar_tensor_tensor(prob[:, :, :], lg[:, 0], 1 / WSCALE,
                                                 br_row[:, :].unsqueeze(1).to_broadcast([P, NT, E]),
                                                 ALU.mult, ALU.add))
                    chain(V.scalar_tensor_tensor(prob[:, :, :], lg[:, 1], 1 / WSCALE, prob[:, :, :],
                                                 ALU.mult, ALU.add))
                    chain(V.reduce_max(one[:, 0, :], prob[:, :, :], AX_X))
                    V.tensor_tensor(prob[:, :, :], prob[:, :, :], each(one[:, 0, :]), ALU.subtract).then_inc(
                        S["r_lg"], 1)
                    dve.wait_ge(S["r_exp"], 1)
                    chain(V.reduce_sum(one[:, 1, :], prob[:, :, :], AX_X))
                    chain(V.reciprocal(one[:, 2, :], one[:, 1, :]))
                    chain(V.tensor_tensor(prob[:, :, :], prob[:, :, :], each(one[:, 2, :]), ALU.mult))
                    for t in range(NT):
                        ins = V.max(top_v[:, t, :], prob[:, t, :])
                    chain(ins)
                    for t in range(NT):
                        ins = V.max_index(top_i[:, t, :], top_v[:, t, :], prob[:, t, :])
                    chain(ins)
                    chain(V.tensor_copy(top_f[:, :, :], top_i[:, :, :]))
                    for j in range(top):
                        ins = V.tensor_tensor(hot[:, j], iota_f[:, :].unsqueeze(1).to_broadcast([P, NT, E]),
                                              each(top_f[:, :, j]), ALU.is_equal)
                    chain(ins)
                    gate = hot[:, 0]
                    if top == 1:
                        chain(V.tensor_tensor(gate, gate, each(top_v[:, :, 0]), ALU.mult))
                    else:
                        chain(V.tensor_tensor(hot[:, 2], hot[:, 0], hot[:, 1], ALU.add))
                        V.tensor_copy(sent[:, :, :], hot[:, 2]).then_inc(S["r_w"], 1)
                        chain(V.tensor_tensor(one[:, 3, :], top_v[:, :, 0], top_v[:, :, 1], ALU.add))
                        chain(V.tensor_scalar(one[:, 3, :], one[:, 3, :], 1e-9, None, ALU.add))
                        chain(V.reciprocal(one[:, 4, :], one[:, 3, :]))
                        for j in range(top):
                            ins = V.tensor_tensor(one[:, 5 + j, :], top_v[:, :, j], one[:, 4, :], ALU.mult)
                        chain(ins)
                        for j in range(top):
                            ins = V.tensor_tensor(hot[:, j], hot[:, j], each(one[:, 5 + j, :]), ALU.mult)
                        chain(ins)
                        chain(V.tensor_tensor(gate, hot[:, 0], hot[:, 1], ALU.add))
                        hidden_rows(0)
                        dve.wait_ge(S["pos_mm"], NT)
                        pos = ps[0:P, 5, 0:NT * E].rearrange("p (t e) -> p t e", e=E)
                        chain(V.tensor_scalar(hot[:, 2], pos, float(cap), None, ALU.is_lt))
                        chain(V.tensor_tensor(gate, gate, hot[:, 2], ALU.mult))
                        chain(V.reduce_sum(one[:, 1, :], gate, AX_X))
                        chain(V.tensor_scalar(one[:, 1, :], one[:, 1, :], 1e-9, None, ALU.add))
                        chain(V.reciprocal(one[:, 2, :], one[:, 1, :]))
                        chain(V.tensor_tensor(gate, gate, each(one[:, 2, :]), ALU.mult))
                    V.nop().then_inc(S["pos_done"], 1)
                    def gated(t):
                        dve.wait_ge(S["gelu_done"], t + 1)
                        V.tensor_tensor(y[:, t, :].rearrange("p (e f) -> p e f", e=E),
                                        hid[:, t % 2, :].rearrange("p (e f) -> p e f", e=E),
                                        gate[:, t, :].unsqueeze(2).to_broadcast([P, E, DFF]),
                                        ALU.mult).then_inc(S["hm_done"], 1)

                    def low_hidden(t):
                        dve.wait_ge(S["yt_hi2"], t + 1)
                        V.tensor_tensor(b_T[:, 1, :, span(t)], tr_bank(t % 2), b_T[:, 0, :, span(t)],
                                        ALU.subtract).then_inc(S["yt_lo2"], 1)

                    if top == 1:
                        hidden_rows(0)
                    hidden_rows(1)
                    for t in range(NT - 2):
                        gated(t)
                        if t == 0:
                            hidden_rows(2)
                        if t == 1:
                            hidden_rows(3)
                    dve.wait_ge(S["wt_mm"], 1)
                    wtp = blocks(4, E)
                    wt3 = wt[:, :, :].rearrange("e a (t n) -> e a t n", n=P)
                    chain(V.tensor_copy(wt3[:, 0], wtp))
                    V.tensor_tensor(wt3[:, 1], wtp, wt3[:, 0], ALU.subtract).then_inc(S["wt_parts"], 1)
                    gated(NT - 2)
                    low_hidden(0)
                    low_hidden(1)
                    hidden_rows(NT - 1)
                    gated(NT - 1)
                    low_hidden(2)

                    def residual(t):
                        dve.wait_ge(S["res1_mm"], t + 1)
                        V.scalar_tensor_tensor(x[:, t, :], bank(2 + t % 2, P), 1 / WSCALE, x[:, t, :],
                                               ALU.mult, ALU.add).then_inc(S["res1"], 1)

                    def residual_stats(t):
                        residual(t)
                        dve.wait_ge(S["res1"], t + 1)
                        chain(row_stats(dve, chain, x, t))

                    for t in range(NT):
                        if t < 2:
                            (residual if last else residual_stats)(t)
                            low_hidden(t + 3)
                        elif last:
                            residual(t)
                    if not last:
                        then["vector"](dve, chain, residual_stats)

                @block.scalar
                def _(act):
                    def gelu(t):
                        act.wait_ge(S["hid_ready"], t + 1)
                        nc.scalar.activation(hid[:, t % 2, :], hid[:, t % 2, :], ACT.Gelu).then_inc(S["gelu_done"], 1)

                    act.wait_ge(S["small_loaded"], 32)
                    nc.scalar.activation(wr[:, :, 0, :], wr_f[:, :, :], ACT.Copy, scale=WSCALE).then_inc(S["small_hi"], 1)
                    if last:
                        split_hi_scaled(act, i1, 0)
                    for t in range(NT):
                        act.wait_ge(S["xt_mm"], t + 1)
                        nc.scalar.activation(a_T[:, 0, :, span(t)], tr_bank(t % 2), ACT.Copy).then_inc(S["xt_hi"], 1)
                    nc.scalar.activation(b2_p[:, 0, :], b2_f[:, :], ACT.Copy, scale=WSCALE).then_inc(S["small_hi"], 1)
                    if last:
                        split_hi_scaled(act, i2, 1)
                    else:
                        split_hi_scaled(act, 0, 0)
                    act.wait_ge(S["r_lg"], 1)
                    nc.scalar.activation(prob[:, :, :], prob[:, :, :], ACT.Exp).then_inc(S["r_exp"], 1)
                    for t in range(NT - 1):
                        gelu(t)
                    for t in range(NT):
                        if t == 2:
                            gelu(NT - 1)
                        act.wait_ge(S["yt_mm2"], t + 1)
                        nc.scalar.activation(b_T[:, 0, :, span(t)], tr_bank(t % 2), ACT.Copy).then_inc(S["yt_hi2"], 1)
                        if not last and 2 <= t < NT - 1:
                            split_hi_scaled(act, t - 1, t - 1)
                    if not last:
                        then["scalar"](act)

                @block.tensor
                def _(pe):
                    def rows_T(t):
                        pe.wait_ge(S["rows_normed"], t + 1)
                        if t >= 2:
                            pe.wait_ge(S["xt_lo"], t - 1)
                        transpose_rows(pe, t % 2, y[:, t, :], S["xt_mm"])

                    def router(t):
                        pe.wait_ge(S["xt_lo"], t + 1)
                        at = t * 2 * E
                        for k in range(K):
                            nc.tensor.matmul(ps[0:P, 4, at:at + 2 * E], a_T[:, 0, k, span(t)],
                                             wr[:, k, :, :].rearrange("p a e -> p (a e)"), start=k == 0,
                                             stop=False, skip_group_check=True)
                        for k in range(K):
                            ins = nc.tensor.matmul(ps[0:P, 4, at:at + E], a_T[:, 1, k, span(t)], wr[:, k, 0, :],
                                                   start=False, stop=k == K - 1, skip_group_check=True)
                        ins.then_inc(S["r_mm"], 1)

                    rows_T(0)
                    rows_T(1)
                    pe.wait_ge(S["small_lo"], 1)
                    for t in range(NT):
                        router(t)
                        if t + 2 < NT:
                            rows_T(t + 2)
                    if last:
                        pe.wait_ge(S[f"w_lo{i1}"], 1)
                    for t in range(2):
                        mat_to_rows(bank(GM_BANK[t], P), w[i1], a_T, t).then_inc(S["gm"], 1)
                    if cap:
                        pe.wait_ge(S["const_made"], 2)
                        pe.wait_ge(S["r_w"], 1)
                        for t in range(NT):
                            for s in range(t + 1):
                                ins = nc.tensor.matmul(ps[0:P, 5, t * E:(t + 1) * E],
                                                       before[:, 0 if s == t else 1, :], sent[:, s, :],
                                                       start=s == 0, stop=s == t)
                            ins.then_inc(S["pos_mm"], 1)
                    def hidden_T(t):
                        pe.wait_ge(S["hm_done"], t + 1)
                        if t >= 2:
                            pe.wait_ge(S["yt_lo2"], t - 1)
                        transpose_rows(pe, t % 2, y[:, t, :], S["yt_mm2"])

                    for t in range(2, NT):
                        if t == 4:
                            pe.wait_ge(S["pos_done"], 1)
                            for s in range(NT):
                                ins = nc.tensor.transpose(blocks(4, E)[:, s, :], hot[:, 0, s, :], ident[0:P, 0:P])
                            ins.then_inc(S["wt_mm"], 1)
                            hidden_T(0)
                            hidden_T(1)
                            pe.wait_ge(S["hid_ready"], 1)
                        mat_to_rows(bank(GM_BANK[t], P), w[i1], a_T, t).then_inc(S["gm"], 1)
                    hidden_T(2)
                    pe.wait_ge(S["wt_parts"], 1)
                    pe.wait_ge(S["small_lo"], 2)
                    if last:
                        pe.wait_ge(S[f"w_lo{i2}"], 1)
                    for t in range(NT):
                        pe.wait_ge(S["yt_lo2"], t + 1)
                        if t >= 2:
                            pe.wait_ge(S["res1"], t - 1)
                        mat_to_rows(bank(2 + t % 2, P), w[i2], b_T, t, last=False)
                        for i, (ap, wp) in enumerate(PASSES):
                            ins = nc.tensor.matmul(bank(2 + t % 2, P), wt[:, ap, span(t)], b2_p[:, wp, :],
                                                   start=False, stop=i == len(PASSES) - 1)
                        ins.then_inc(S["res1_mm"], 1)
                        if t + 3 < NT:
                            hidden_T(t + 3)
                    if not last:
                        then["tensor"](pe)
            moe.close()
            clear_all()

        net = ExitStack()

        def nsb(name, shape, dt=F32):
            return net.enter_context(nc.sbuf_tensor(name, shape, dt))

        mod_f = nsb("mod_f", [81, 4, D])
        mod_p = nsb("mod_p", [81, 4, D], F16)
        q_T = nsb("q_T", [128, 2, K, T], F16)
        k_T = b_T
        v_p = nsb("v_p", [P, 2, NT, D], F16)
        GMAX = max(n for _, n in GROUPS) * P + 1
        p_T = nsb("p_T", [P, 2, 2, NT, GMAX], F16)
        rows_s = nsb("rows_s", [P, 3, T])
        soft = nsb("soft", [P, 3, 4])

        def mod_hi(act, half):
            own = slice(2 * half, 2 * half + 2)
            nc.scalar.activation(mod_p[:, own, :], mod_f[:, own, :], ACT.Copy, scale=WSCALE).then_inc(
                S[f"mod_hi{half}"], 1)

        def mod_lo(dve, half):
            own = slice(2 * half, 2 * half + 2)
            dve.wait_ge(S[f"mod_hi{half}"], 1)
            nc.vector.scalar_tensor_tensor(mod_p[64:81, own], mod_f[64:81, own], WSCALE, mod_p[64:81, own],
                                           ALU.mult, ALU.subtract).then_inc(S[f"mod_lo{half}"], 1)

        def mod_rows(t, j, b):
            nc.tensor.matmul(bank(b, P), cond[:, span(t)], mod_p[:, 2 * (j - 1), :],
                             start=True, stop=True).then_inc(S[f"mod_mm{j}"], 1)

        def transposed(pe, t, i, j, b):
            pe.wait_ge(S[f"mod{j}"], i + 1)
            for k in range(K):
                nc.tensor.matmul(ps[:, b, k * P:(k + 1) * P], y[:, t, k * 128:(k + 1) * 128],
                                 ident[0:P, 0:P], is_transpose=True, start=k == 0, stop=False,
                                 skip_group_check=True)
            for k in range(K):
                ins = nc.tensor.matmul(ps[:, b, k * P:(k + 1) * P],
                                       mod_p[:, 2 * j - 1, k * 128:(k + 1) * 128], cond[:, span(t)],
                                       start=False, stop=k == K - 1, skip_group_check=True)
            ins.then_inc(S[f"yt_mm{j}"], 1)

        def high_rows(act, t, i, j, b, dst):
            act.wait_ge(S[f"yt_mm{j}"], i + 1)
            nc.scalar.activation(dst[:, 0, :, span(t)], tr_bank(b), ACT.Copy, scale=1 / WSCALE).then_inc(
                S[f"yt_hi{j}"], 1)

        def low_rows(dve, t, i, j, b, dst):
            dve.wait_ge(S[f"yt_hi{j}"], i + 1)
            nc.vector.scalar_tensor_tensor(dst[:, 1, :, span(t)], tr_bank(b), 1 / WSCALE,
                                           dst[:, 0, :, span(t)], ALU.mult, ALU.subtract).then_inc(
                S[f"yt_lo{j}"], 1)

        def scale_rows(dve, t, i, j, b):
            norm(xg, t).then_inc(S[f"norm{j}"], 1)
            dve.wait_ge(S[f"norm{j}"], i + 1)
            dve.wait_ge(S[f"mod_mm{j}"], i + 1)
            nc.vector.scalar_tensor_tensor(y[:, t, :], bank(b, P), WSCALE, y[:, t, :],
                                           ALU.add, ALU.mult).then_inc(S[f"mod{j}"], 1)

        G0, G1 = (range(first, first + n) for first, n in GROUPS)
        MOD_BANK = {0: 0, 1: 1, 2: 5, 3: 4, 4: 5}
        TR_BANK = {0: 6, 1: 7, 2: 2, 3: 2, 4: 3}
        MOD2_BANK = {0: 3, 1: 4, 2: 2, 3: 3, 4: 4}
        TR2_BANK = {0: 6, 1: 7, 2: 5, 3: 6, 4: 7}
        WO_BANK = (0, 1, 5, 0, 1)

        def load_biases(sp, layer):
            sp.dma_start(bias_col[:, :, :], A["L1_gnn_cols"][bass.ds(layer, 1)][0]).then_inc(S["bias_loaded"], 16)
            for i, n in enumerate(("bv", "bo", "m_b2")):
                sp.dma_start(bias_row[:, i, :], A["L1_gnn_" + n][bass.ds(layer, 1)][0].partition_broadcast(P)).then_inc(
                    S["bias_loaded"], 16)

        def before_blocks_sync(sp):
            sp.dma_start(mod_f[:, :, :], A["mod"][0]).then_inc(S["mod_loaded"], 16)
            for i, n in enumerate(("wo", "m_w1", "m_w2")):
                sp.wait_ge(S[f"w_lo{i}"], 1)
                load_w(sp, 3 + i, A["L1_gnn_" + n][0], i)
            sp.wait_ge(S["hid_ready"], NT)
            load_biases(sp, 0)
            for i in range(3):
                sp.wait_ge(S[f"w_loaded{3 + i}"], 16)
            sp.wait_ge(S["bias_loaded"], 32 + 64)

        def before_blocks_vector(dve, chain, residual_stats):
            residual_stats(2)
            inv_std(dve, chain, G0.start, G0.stop)
            for t in G0:
                chain(norm(x, t, dst=xg))
                chain(row_stats(dve, chain, xg, t))
            for t in G1:
                residual_stats(t)
            inv_std(dve, chain, 0, NT)
            mod_lo(dve, 0)
            for t in G0:
                scale_rows(dve, t, t, 1, MOD_BANK[t])
            for t in G1:
                norm(x, t, dst=xg).then_inc(S["resb1"], 1)
            for t in G0:
                low_rows(dve, t, t, 1, TR_BANK[t], a_T)

        def before_blocks_scalar(act):
            act.wait_ge(S["mod_loaded"], 16)
            mod_hi(act, 0)
            for t in G0:
                high_rows(act, t, t, 1, TR_BANK[t], a_T)

        def before_blocks_tensor(pe):
            pe.wait_ge(S["mod_lo0"], 1)
            for t in G0:
                mod_rows(t, 1, MOD_BANK[t])
            for t in G0:
                transposed(pe, t, t, 1, TR_BANK[t])

        experts(A["L0_ffn_Wr"], A["L0_ffn_br"], A["L0_ffn_W1"], A["L0_ffn_b1"], A["L0_ffn_W2"], A["L0_ffn_b2"],
                top=2, cap=CAP, i1=2, i2=3, last=False,
                then={"sync": before_blocks_sync, "vector": before_blocks_vector, "scalar": before_blocks_scalar,
                      "tensor": before_blocks_tensor})

        qk_units = [(g, which, m) for g in range(2) for which in range(2) for m in range(K)]
        QK_BANK = (6, 7, 0, 1)
        C_BANK = (2, 5, 0, 1, 2, 5, 0, 1)
        C_FREE = (None, None, ("res1", 4), ("res1", 5), ("c_f", 1), ("c_f", 2), ("c_f", 3), ("c_f", 4))
        heads = [(g, h) for g in range(2) for h in range(H)]
        s_units = [(g, h, i) for g, h in heads for i in range(GROUPS[g][1])]
        NS = len(s_units)
        last_of = {}
        for n, (g, h, i) in enumerate(s_units):
            last_of[g * H + h] = n
        v_parts, o_after = {}, {}
        for gh in range(2 * H):
            c = GROUPS[gh // H][1]
            for part in range(c):
                v_parts.setdefault(min(last_of[gh] + 2 + part, NS), []).append((gh, part, c))
            o_after.setdefault(min(last_of[gh] + 2 + c, NS), []).append(gh)

        def probs_T(n):
            return blocks(4 - 2 * (n % 2), P)

        with nc.Fori(0, NL) as layer:
            with nc.Block() as block:
                @block.sync
                def _(sp):
                    nxt = sp.snap((layer + 1) % NL)

                    def of(name, which):
                        return A[name][bass.ds(which, 1)]

                    sp.wait_ge(S["w_lo3"], 1)
                    load_w(sp, 0, of("L1_gnn_wq", nxt)[0], 0)
                    sp.wait_ge(S["w_lo4"], 1)
                    load_w(sp, 1, of("L1_gnn_wk", nxt)[0], 1)
                    sp.wait_ge(S["mod_lo1"], 1)
                    sp.dma_start(mod_f[:, :, :], of("mod", nxt)[0]).then_inc(S["mod_loaded"], 16)
                    sp.wait_ge(S["w_lo5"], 1)
                    load_w(sp, 2, of("L1_gnn_wv", nxt)[0], 2)
                    sp.wait_ge(S["w_lo0"], 1)
                    load_w(sp, 3, of("L1_gnn_wo", nxt)[0], 0)
                    sp.wait_ge(S["w_lo1"], 1)
                    load_w(sp, 4, of("L1_gnn_m_w1", nxt)[0], 1)
                    sp.wait_ge(S["resb2"], NT)
                    sp.wait_ge(S["c_f"], len(units8))
                    load_biases(sp, nxt)
                    sp.wait_ge(S["w_lo2"], 1)
                    load_w(sp, 5, of("L1_gnn_m_w2", nxt)[0], 2)
                    for i in (3, 4, 5):
                        sp.wait_ge(S[f"w_loaded{i}"], 16)
                    sp.wait_ge(S["bias_loaded"], 64)

                @block.gpsimd
                def _(pool):
                    for t in range(NT):
                        if t in G1:
                            pool.wait_ge(S["norm1"], t - G1.start + 1)
                        nc.gpsimd.tensor_tensor(xg[:, t, :], xg[:, t, :], bias_row[:, 1, :], ALU.add).then_inc(
                            S["resb1"], 1)
                    for t in range(NT):
                        pool.wait_ge(S["v_f"], t + 1)
                        pool.wait_ge(S["v_hi"], t + 1)
                        nc.gpsimd.tensor_tensor(v_p[:, 1, t, :], y[:, t, :], v_p[:, 0, t, :],
                                                ALU.subtract).then_inc(S["v_lo"], 1)
                    for i in range(2):
                        split_lo_scaled(pool, i, i)
                    for t in range(NT):
                        pool.wait_ge(S["norm2"], t + 1)
                        nc.gpsimd.tensor_tensor(xg[:, t, :], xg[:, t, :], bias_row[:, 2, :], ALU.add).then_inc(
                            S["resb2"], 1)
                    pool.wait_ge(S["resb2"], NT)
                    pool.wait_ge(S["mod_hi0"], 1)
                    nc.gpsimd.tensor_tensor(mod_p[64:81, 0:2], mod_f[64:81, 0:2], mod_p[64:81, 0:2],
                                            ALU.subtract).then_inc(S["mod_lo0"], 1)

                @block.tensor
                def _(pe):
                    def score(n):
                        g, h, i = s_units[n]
                        t = GROUPS[g][0] + i
                        if n:
                            pe.wait_ge(S["s_max"], n)
                        for a, b in halves:
                            for j, (qp, kp) in enumerate(PASSES):
                                ins = nc.tensor.matmul(pair(0, P, T)[:, a:b], q_T[:, qp, h, span(t)],
                                                       k_T[:, kp, h, a:b], start=j == 0, stop=j == len(PASSES) - 1)
                        ins.then_inc(S["s_mm"], 1)

                    def prob_T(n):
                        pe.wait_ge(S[f"s_prob{n % 2}"], n // 2 + 1)
                        if n >= 2:
                            pe.wait_ge(S["pt_lo"], n - 1)
                        for j in range(NT):
                            ins = nc.tensor.transpose(probs_T(n)[:, j, :], rows_s[:, n % 3, span(j)],
                                                      ident[0:P, 0:P])
                        ins.then_inc(S["pt_mm"], 1)

                    def times_v(gh, part, parts):
                        g, h = heads[gh]
                        cells = GROUPS[g][1] * P
                        if part == 0:
                            pe.wait_ge(S["pt_hi"], last_of[gh] + 1)
                            if gh >= 2:
                                pe.wait_ge(S["o_lo"], gh - 1)
                        c = len(PASSES) * NT
                        for i in range(c * part // parts, c * (part + 1) // parts):
                            (vp, pp), j = PASSES[i // NT], i % NT
                            if i == 2 * NT:
                                pe.wait_ge(S["pt_lo"], last_of[gh] + 1)
                            ins = nc.tensor.matmul(bank(6 + gh % 2, 128, cells),
                                                   v_p[:, vp, j, h * DH:(h + 1) * DH],
                                                   p_T[:, gh % 2, pp, j, 0:cells], start=i == 0, stop=i == c - 1)
                        if part == parts - 1:
                            ins.then_inc(S["o_mm"], 1)

                    def times_wo(t):
                        heads_done = H if t in G0 else 2 * H
                        pe.wait_ge(S["o_hi"], heads_done)
                        if t in G1:
                            pe.wait_ge(S["res1"], t - 2)
                        mat_to_rows(bank(WO_BANK[t], P), w[3], a_T, t, low=(S["o_lo"], heads_done)).then_inc(
                            S["res1_mm"], 1)

                    for t in G1:
                        mod_rows(t, 1, MOD_BANK[t])
                    for u, (g, which, m) in enumerate(qk_units):
                        if u >= 4:
                            pe.wait_ge(S["a_f"], u - 3)
                        if u == 2 * K:
                            pe.wait_ge(S["yt_lo1"], len(G1))
                        mat_to_T(bank(QK_BANK[u % 4], 128, GROUPS[g][1] * P), w[which], a_T, m, g).then_inc(
                            S["a_mm"], 1)
                        if u == 5:
                            for i, t in enumerate(G1):
                                transposed(pe, t, i, 1, TR_BANK[t])
                    for t in range(NT):
                        if t >= 2:
                            pe.wait_ge(S["v_f"], t - 1)
                        mat_to_rows(bank(2 + t % 2, P), w[2], a_T, t).then_inc(S["v_mm"], 1)
                        if t == 1:
                            pe.wait_ge(S["a_lo"], len(qk_units))
                            score(0)
                        if t in (2, 3):
                            score(t - 1)
                    for n in range(NS):
                        if 0 < n < NS - 2:
                            score(n + 2)
                        if n == 1:
                            pe.wait_ge(S["v_f"], NT)
                        if n == min(v_parts):
                            pe.wait_ge(S["v_lo"], NT)
                        for v in v_parts.get(n, ()):
                            times_v(*v)
                        if n == NS - 2:
                            pe.wait_ge(S["s_max"], NS)
                            pe.wait_ge(S["w_lo3"], 1)
                            times_wo(0)
                        prob_T(n)
                    times_wo(1)
                    for v in v_parts[NS][:1]:
                        times_v(*v)
                    pe.wait_ge(S["pt_lo"], NS - 1)
                    times_wo(2)
                    for v in v_parts[NS][1:]:
                        times_v(*v)
                    pe.wait_ge(S["mod_lo1"], 1)
                    for t in G0:
                        mod_rows(t, 2, MOD2_BANK[t])
                    for t in G1:
                        times_wo(t)
                    def times_w2(t):
                        hidden_done = K if t in G0 else 2 * K
                        pe.wait_ge(S["c_hi"], hidden_done)
                        if t >= 2:
                            pe.wait_ge(S["res2"], t - 1)
                        mat_to_rows(bank(3 + t % 2, P), w[5], q_T, t, low=(S["c_lo"], hidden_done)).then_inc(
                            S["res2_mm"], 1)

                    pe.wait_ge(S["w_lo4"], 1)
                    pe.wait_ge(S["w_lo5"], 1)
                    for g, (first, n) in enumerate(GROUPS):
                        for t in range(first, first + n):
                            transposed(pe, t, t, 2, TR2_BANK[t])
                        if g == 0:
                            for t in G1:
                                mod_rows(t, 2, MOD2_BANK[t])
                        else:
                            times_w2(0)
                        pe.wait_ge(S["yt_hi2"], first + n)
                        for m in range(K):
                            u = g * K + m
                            if C_FREE[u]:
                                pe.wait_ge(S[C_FREE[u][0]], C_FREE[u][1])
                            mat_to_T(bank(C_BANK[u], 128, n * P), w[4], b_T, m, g,
                                     low=(S["yt_lo2"], first + n)).then_inc(S["c_mm"], 1)
                    for t in range(1, NT):
                        times_w2(t)
                        if t == 3:
                            pe.wait_ge(S["mod_lo0"], 1)
                            for k in G0:
                                mod_rows(k, 1, MOD_BANK[k])
                    for t in G0:
                        transposed(pe, t, len(G1) + t, 1, TR_BANK[t])

                @block.scalar
                def _(act):
                    A_ = nc.scalar.activation
                    act.wait_ge(S["small_lo"], 1)
                    for u, (g, which, m) in enumerate(qk_units):
                        evac_T(act, "a", u, (q_T, k_T)[which], bank(QK_BANK[u % 4], 128, GROUPS[g][1] * P), m, cols(g),
                               ACT.Identity, scale=(SCORE if which == 0 else 1.0) / WSCALE,
                               bias=bias_col[:, which, m:m + 1],
                               slot_free=(S["a_lo"], u - 3) if u >= 4 else None)
                        if u == 5:
                            for i, t in enumerate(G1):
                                high_rows(act, t, i, 1, TR_BANK[t], a_T)
                        if u in (3, 7, 11):
                            split_hi_now(3 + u // 4, u // 4)
                        if u == 9:
                            mod_hi(act, 1)
                    def hidden(u):
                        g, m = units8[u]
                        evac_T(act, "c", u, q_T, bank(C_BANK[u], 128, GROUPS[g][1] * P), m, cols(g), ACT.Relu,
                               scale=1 / WSCALE, bias=bias_col[:, 2, m:m + 1],
                               slot_free=(S["c_lo"], u - 3) if u >= 4 else (S["o_lo"], 2 * H))

                    def prob_hi(n):
                        g, h, i = s_units[n]
                        act.wait_ge(S["pt_mm"], n + 1)
                        gh = g * H + h
                        if gh >= 2 and i == 0:
                            act.wait_ge(S["o_mm"], gh - 1)
                        A_(p_T[:, gh % 2, 0, :, span(i)], probs_T(n), ACT.Copy).then_inc(S["pt_hi"], 1)

                    def out_hi(gh):
                        g, h = heads[gh]
                        act.wait_ge(S["o_mm"], gh + 1)
                        A_(a_T[:, 0, h, cols(g)], bank(6 + gh % 2, 128, GROUPS[g][1] * P), ACT.Copy,
                           scale=1 / PSCALE).then_inc(S["o_hi"], 1)

                    def exps(n):
                        act.wait_ge(S["s_max"], n + 1)
                        A_(rows_s[:, n % 3, :], rows_s[:, n % 3, :], ACT.Exp, scale=-1.0, bias=soft[:, n % 3, 1:2],
                           accum_out=soft[:, n % 3, 2:3]).then_inc(S["s_exp"], 1)

                    def normalise(n):
                        act.wait_ge(S["s_inv"], n + 1)
                        A_(rows_s[:, n % 3, :], rows_s[:, n % 3, :], ACT.Copy, scale=soft[:, n % 3, 3:4]).then_inc(
                            S["s_prob0"], 1)

                    for t in range(NT):
                        act.wait_ge(S["v_f"], t + 1)
                        A_(v_p[:, 0, t, :], y[:, t, :], ACT.Copy).then_inc(S["v_hi"], 1)
                        if t in (0, 1):
                            split_hi_scaled(act, t, t)
                        if t == 2:
                            exps(0)
                        if t == 3:
                            normalise(0)
                            exps(1)

                    for n in range(NS):
                        if n:
                            prob_hi(n - 1)
                        if n and n % 2 == 0:
                            normalise(n)
                        if n and n + 1 < NS:
                            exps(n + 1)
                        for gh in o_after.get(n, ()):
                            out_hi(gh)
                    prob_hi(NS - 1)
                    for gh in o_after[NS]:
                        out_hi(gh)
                    split_hi(2, 2)
                    for t in G0:
                        high_rows(act, t, t, 2, TR2_BANK[t], b_T)
                    for u in range(K):
                        hidden(u)
                    for t in G1:
                        high_rows(act, t, t, 2, TR2_BANK[t], b_T)
                    act.wait_ge(S["mod_loaded"], 16)
                    A_(mod_f[:, 0:2, :], mod_f[:, 0:2, :], ACT.Copy, scale=WSCALE).then_inc(S["mod_scaled"], 1)
                    act.wait_ge(S["mod_scaled"], 1)
                    A_(mod_p[:, 0:2, :], mod_f[:, 0:2, :], ACT.Copy).then_inc(S["mod_hi0"], 1)
                    for u in range(K, 2 * K):
                        hidden(u)
                    for t in G0:
                        high_rows(act, t, len(G1) + t, 1, TR_BANK[t], a_T)

                @block.vector
                def _(dve):
                    V = nc.vector
                    chain = Chain(dve, S["chain_dve"])

                    V.tensor_scalar(bias_col[:, 0, :], bias_col[:, 0, :], SCORE, None, ALU.mult).then_inc(
                        S["small_lo"], 1)
                    for t in G1:
                        chain(row_stats(dve, chain, xg, t))
                    inv_std(dve, chain, G1.start, G1.stop)
                    for i, t in enumerate(G1):
                        scale_rows(dve, t, i, 1, MOD_BANK[t])
                    for u, (g, which, m) in enumerate(qk_units):
                        low_T(dve, "a", u, (q_T, k_T)[which], m, cols(g))
                        if u == 5:
                            for i, t in enumerate(G1):
                                low_rows(dve, t, i, 1, TR_BANK[t], a_T)
                        if u in (3, 7, 11):
                            split_lo(3 + u // 4, u // 4)
                        if u == 9:
                            mod_lo(dve, 1)
                    def row_max(n):
                        g, h, i = s_units[n]
                        t = GROUPS[g][0] + i
                        dve.wait_ge(S["s_mm"], n + 1)
                        if n >= 3:
                            dve.wait_ge(S["pt_mm"], n - 2)
                        V.tensor_tensor_reduce(out=rows_s[:, n % 3, :], in0=pair(0, P, T), in1=lnc[:, t, :], scale=-1.0, scalar=-FLOOR, op0=ALU.add,
                                               op1=ALU.min, accum_out=soft[:, n % 3, 1:2]).then_inc(S["s_max"], 1)

                    def inverse(n):
                        dve.wait_ge(S["s_exp"], n + 1)
                        chain(V.tensor_scalar(soft[:, n % 3, 2:3], soft[:, n % 3, 2:3], 1 / PSCALE, 1e-30, ALU.mult,
                                              ALU.max))
                        V.reciprocal(soft[:, n % 3, 3:4], soft[:, n % 3, 2:3]).then_inc(S["s_inv"], 1)

                    def normalise(n):
                        dve.wait_ge(S["s_inv"], n + 1)
                        V.tensor_scalar(rows_s[:, n % 3, :], rows_s[:, n % 3, :], soft[:, n % 3, 3:4], None,
                                        ALU.mult).then_inc(S["s_prob1"], 1)

                    def prob_lo(n):
                        g, h, i = s_units[n]
                        gh = g * H + h
                        dve.wait_ge(S["pt_hi"], n + 1)
                        V.tensor_tensor(p_T[:, gh % 2, 1, :, span(i)], probs_T(n), p_T[:, gh % 2, 0, :, span(i)],
                                        ALU.subtract).then_inc(S["pt_lo"], 1)

                    def out_lo(gh):
                        g, h = heads[gh]
                        dve.wait_ge(S["o_hi"], gh + 1)
                        V.scalar_tensor_tensor(a_T[:, 1, h, cols(g)], bank(6 + gh % 2, 128, GROUPS[g][1] * P),
                                               1 / PSCALE, a_T[:, 0, h, cols(g)], ALU.mult, ALU.subtract).then_inc(
                            S["o_lo"], 1)

                    for t in range(NT):
                        if t == 4:
                            inverse(0)
                        if t >= 2:
                            row_max(t - 2)
                        dve.wait_ge(S["v_mm"], t + 1)
                        V.scalar_tensor_tensor(y[:, t, :], bank(2 + t % 2, P), 1 / WSCALE, bias_row[:, 0, :],
                                               ALU.mult, ALU.add).then_inc(S["v_f"], 1)
                    for n in range(NS):
                        if n:
                            inverse(n)
                        if n % 2:
                            normalise(n)
                        if 0 < n < NS - 2:
                            row_max(n + 2)
                        if n:
                            prob_lo(n - 1)
                        for gh in o_after.get(n, ()):
                            out_lo(gh)
                    prob_lo(NS - 1)
                    ends = list(o_after[NS])

                    def residual(t, j, b):
                        dve.wait_ge(S[f"res{j}_mm"], t + 1)
                        dve.wait_ge(S[f"resb{j}"], t + 1)
                        V.scalar_tensor_tensor(xg[:, t, :], bank(b, P), 1 / WSCALE, xg[:, t, :],
                                               ALU.mult, ALU.add).then_inc(S[f"res{j}"], 1)

                    for g, (first, n) in enumerate(GROUPS):
                        for t in range(first, first + n):
                            residual(t, 1, WO_BANK[t])
                            dve.wait_ge(S["res1"], t + 1)
                            chain(row_stats(dve, chain, xg, t))
                            if t in (1, 2):
                                out_lo(ends.pop(0))
                        inv_std(dve, chain, first, first + n)
                        for t in range(first, first + n):
                            scale_rows(dve, t, t, 2, MOD2_BANK[t])
                        if g == 0:
                            for t in G0:
                                low_rows(dve, t, t, 2, TR2_BANK[t], b_T)
                    def low_hidden(u):
                        low_T(dve, "c", u, q_T, units8[u][1], cols(units8[u][0]))

                    def residual_stats(t):
                        residual(t, 2, 3 + t % 2)
                        dve.wait_ge(S["res2"], t + 1)
                        chain(row_stats(dve, chain, xg, t))

                    for u in range(K):
                        low_hidden(u)
                    for t in G1:
                        low_rows(dve, t, t, 2, TR2_BANK[t], b_T)
                    residual_stats(0)
                    split_lo(2, 2)
                    for u in range(K, 2 * K):
                        low_hidden(u)
                    for t in G0[1:]:
                        residual_stats(t)
                    inv_std(dve, chain, G0.start, G0.stop)
                    i = len(G1)
                    scale_rows(dve, 0, i, 1, MOD_BANK[0])
                    residual(3, 2, 4)
                    scale_rows(dve, 1, i + 1, 1, MOD_BANK[1])
                    scale_rows(dve, 2, i + 2, 1, MOD_BANK[2])
                    residual(4, 2, 3)
                    low_rows(dve, 0, i, 1, TR_BANK[0], a_T)
                    low_rows(dve, 1, i + 1, 1, TR_BANK[1], a_T)
                    low_rows(dve, 2, i + 2, 1, TR_BANK[2], a_T)
            clear_all()
        net.close()

        experts(A["L1_ffn_Ws"], A["L1_ffn_bs"], A["L1_ffn_W1"], A["L1_ffn_b1"], A["L1_ffn_W2"], A["L1_ffn_b2"],
                top=1, cap=0, i1=0, i2=1, last=True)


def layout(inputs):
    import numpy as np

    a = {k: np.asarray(v) for k, v in inputs.items()}

    def tiles(m):
        *lead, rows, n = m.shape
        return np.ascontiguousarray(np.moveaxis(m.reshape(*lead, rows // 128, 128, n), -2, -3))

    def columns(v):
        return np.ascontiguousarray(np.swapaxes(v.reshape(*v.shape[:-1], -1, 128), -1, -2))

    out = {k: a[k] for k in ("x", "src", "dst", "L0_gnn_b2", "L0_ffn_br", "L0_ffn_b2", "L1_ffn_bs", "L1_ffn_b2",
                             "L1_gnn_bv", "L1_gnn_bo", "L1_gnn_m_b2", "L1_gnn_f_w1")}
    out["noise"] = a["node_vec1"].reshape(-1)
    for k in ("L0_gnn_W1", "L0_gnn_W2", "L0_ffn_Wr", "L1_ffn_Ws", "L1_gnn_wq", "L1_gnn_wk", "L1_gnn_wv",
              "L1_gnn_wo", "L1_gnn_m_w1", "L1_gnn_m_w2"):
        out[k] = tiles(a[k])
    out["L0_gnn_b1"] = columns(a["L0_gnn_b1"])
    out["L1_gnn_cols"] = np.ascontiguousarray(
        np.stack([columns(a["L1_gnn_" + k]) for k in ("bq", "bk", "m_b1")], axis=2))
    for k in ("L0_ffn_", "L1_ffn_"):
        w1, w2 = a[k + "W1"], a[k + "W2"]
        out[k + "W1"] = tiles(np.moveaxis(w1, 0, 1).reshape(w1.shape[1], -1))
        out[k + "b1"] = a[k + "b1"].reshape(-1)
        out[k + "W2"] = tiles(w2.reshape(-1, w2.shape[-1]))
    nl, c, d = a["L1_gnn_s1_w"].shape
    mod = np.zeros((nl, 81, 4, d), np.float32)
    for j, k in enumerate(("s1", "b1", "s2", "b2")):
        for at in (0, 32, 64):
            mod[:, at:at + c, j] = a[f"L1_gnn_{k}_w"]
            if at != 32:
                mod[:, at + c, j] = a[f"L1_gnn_{k}_b"]
    out["mod"] = mod
    f_w2 = np.zeros((c, 81), np.float32)
    f_b = np.zeros((81, 2), np.float32)
    for at in (0, 32, 64):
        f_w2[:, at:at + c] = a["L1_gnn_f_w2"]
        f_b[at:at + c, 0] = a["L1_gnn_f_b2"]
        if at != 32:
            f_b[at + c, 0] = 1.0
    f_b[0:c, 1] = a["L1_gnn_f_b1"]
    out["f_w2"], out["f_b"] = f_w2, f_b
    return out


def kernel(**inputs):
    import numpy as np
    import concourse.bacc as bacc
    from concourse.bass_utils import run_bass_kernel_spmd

    nc = bacc.Bacc("TRN2", target_bir_lowering=False, num_devices=1)
    arrays, args = {}, {}
    for name, a in layout(inputs).items():
        a = np.ascontiguousarray(a)
        arrays[f"in_{name}_dram"] = a
        args[name] = nc.dram_tensor(f"in_{name}_dram", a.shape, mybir.dt.from_np(a.dtype),
                                    kind="ExternalInput").ap()
    shape = inputs["x"].shape
    out = nc.dram_tensor("out_0_dram", tuple(shape), F32, kind="ExternalOutput").ap()
    build(nc, args, out)
    r = run_bass_kernel_spmd(nc, [arrays], core_ids=[0])
    return r.results[0]["out_0_dram"]
```
